# Optimizing a Trainium2 kernel written in Bass

```python
import numpy as np
import jax
import jax.numpy as jnp

def _softmax(x, axis=-1):
    return jax.nn.softmax(x, axis=axis)

def _gelu(x):
    return jax.nn.gelu(x, approximate=True)

def _silu(x):
    return jax.nn.silu(x)

def _sigmoid(x):
    return jax.nn.sigmoid(x)

def _layernorm(x, axis=-1, eps=1e-05):
    m = jnp.mean(x, axis=axis, keepdims=True)
    v = jnp.var(x, axis=axis, keepdims=True)
    return (x - m) / jnp.sqrt(v + eps)

def _scatter_add(tgt, idx, src, axis=0):
    return tgt.at[idx].add(src)

def _segment_sum(src, seg, n):
    return jax.ops.segment_sum(src, seg, n)
kernel_name = 'mk_decoder_postln_d1_seqx_r8_1d82a8'

def setup_inputs(seed: int=0):
    np.random.seed(seed)
    _w = jnp.asarray

    def _rec_inputs():
        import jax
        import jax.numpy as jnp
        _rk = jax.random.key(seed)
        x = -0.000125 + 0.9999 * jax.random.normal(jax.random.fold_in(_rk, 1), (4, 256, 256), jnp.float32)
        _lenS = 256 - jax.random.randint(jax.random.fold_in(_rk, 7), (4,), 0, max(1, 256 // 4) + 1, jnp.int32)
        _lenS2 = 256 - jax.random.randint(jax.random.fold_in(_rk, 8), (4,), 0, max(1, 256 // 4) + 1, jnp.int32)
        itok_BxS_13_99985 = jax.random.randint(jax.random.fold_in(_rk, 11), (4, 256), 13, 99986, jnp.int32)
        _ctx_2048P = jax.random.normal(jax.random.fold_in(_rk, 12), (4, 16, 256), jnp.float32)
        _ctx_2048c = jax.random.dirichlet(jax.random.fold_in(_rk, 512), 0.3 * jnp.ones((16,), jnp.float32), (4, 256))
        _ctx_2048t = jnp.einsum('bsk,bkd->bsd', _ctx_2048c, _ctx_2048P)
        _ctx_2048t = _ctx_2048t * jax.lax.rsqrt(jnp.mean(jnp.square(_ctx_2048t)) + 1e-12) * 0.953939
        ctx_2048 = 6.82029e-06 + 0.0200006 * (_ctx_2048t + 0.3 * jax.random.normal(jax.random.fold_in(_rk, 612), (4, 256, 256), jnp.float32))
        return (x, itok_BxS_13_99985, ctx_2048)
    x, itok_BxS_13_99985, ctx_2048 = _rec_inputs()

    def _L0_attn_setup():
        import jax, jax.numpy as jnp
        import numpy as np
        DIM, HK, HV, DK, DV, KC = (256, 16, 32, 128, 128, 4)
        B, L = (1, 1024)
        EPS = 1e-06

        def _causal_conv_silu(qkv, conv_w, seq_idx):
            Bb, Ll, C = qkv.shape
            xp = jnp.pad(qkv, ((0, 0), (KC - 1, 0), (0, 0)))
            sp = jnp.pad(seq_idx, ((0, 0), (KC - 1, 0)), constant_values=-1)
            out = jnp.zeros_like(qkv)
            for i in range(KC):
                m = (sp[:, i:i + Ll] == seq_idx)[..., None]
                out = out + conv_w[:, i] * jnp.where(m, xp[:, i:i + Ll], 0.0)
            return jax.nn.silu(out)

        def _l2norm(x):
            return x * jax.lax.rsqrt(jnp.sum(x * x, axis=-1, keepdims=True) + EPS)
        key = jax.random.key(seed)
        ks = jax.random.split(key, 12)
        conv_dim = 2 * HK * DK + HV * DV
        inp = {'x': jax.random.normal(ks[0], (B, L, DIM), jnp.float32), 'cu_seqlens': jnp.array([0, 256, 512, 768, 1024], jnp.int64), 'Wqkv': jax.random.normal(ks[1], (DIM, conv_dim), jnp.float32) * 0.02, 'Wz': jax.random.normal(ks[2], (DIM, HV * DV), jnp.float32) * 0.02, 'Wa': jax.random.normal(ks[3], (DIM, HV), jnp.float32) * 0.02, 'Wb': jax.random.normal(ks[4], (DIM, HV), jnp.float32) * 0.02, 'conv_w': jax.random.normal(ks[5], (conv_dim, KC), jnp.float32) * 0.2, 'A_log': jnp.zeros((HV,), jnp.float32), 'dt_bias': jnp.ones((HV,), jnp.float32), 'norm_w': jnp.ones((DV,), jnp.float32), 'Wout': jax.random.normal(ks[6], (HV * DV, DIM), jnp.float32) * 0.02}
        return inp
    _L0_attn_all = _L0_attn_setup()
    _L0_attn_in = {k: v for k, v in _L0_attn_all.items() if k in ('cu_seqlens', 'Wqkv', 'Wz', 'Wa', 'Wb', 'conv_w', 'A_log', 'dt_bias', 'norm_w', 'Wout')}
    del _L0_attn_all

    def _L0_xattn_setup():
        import jax, jax.numpy as jnp
        import numpy as np
        B, S, D = (4, 512, 256)
        E = 4
        F = 1024 // E
        VOCAB = 12500
        key = jax.random.key(seed)
        k1, k2, k3, k4, k5 = jax.random.split(key, 5)
        hidden_states = jax.random.normal(k1, (B, S, D), dtype=jnp.float32)
        token_ids = jax.random.randint(k2, (B, S), 0, VOCAB, dtype=jnp.int64)
        Wg = jax.random.normal(k3, (E, F, D), dtype=jnp.float32) * 0.02
        Wu = jax.random.normal(k4, (E, F, D), dtype=jnp.float32) * 0.02
        Wd = jax.random.normal(k5, (E, D, F), dtype=jnp.float32) * 0.02
        return {'hidden_states': hidden_states, 'token_ids': token_ids, 'Wg': Wg, 'Wu': Wu, 'Wd': Wd}
    _L0_xattn_all = _L0_xattn_setup()
    _L0_xattn_in = {k: v for k, v in _L0_xattn_all.items() if k in ()}
    del _L0_xattn_all

    def _L0_ffn_setup():
        import jax, jax.numpy as jnp
        import numpy as np
        B, T, D = (4, 256, 256)
        E = 8
        K = 2
        F = 1024 // (E // 2)
        key = jax.random.key(seed)
        ks = jax.random.split(key, 5)
        s_in = 1.0 / np.sqrt(D)
        s_mid = 1.0 / np.sqrt(F)
        x = jax.random.normal(ks[0], (B, T, D), dtype=jnp.float32)
        Wr = jax.random.normal(ks[1], (D, E), dtype=jnp.float32) * s_in
        Wg = jax.random.normal(ks[2], (E, D, F), dtype=jnp.float32) * s_in
        Wu = jax.random.normal(ks[3], (E, D, F), dtype=jnp.float32) * s_in
        Wd = jax.random.normal(ks[4], (E, F, D), dtype=jnp.float32) * s_mid
        return {'x': x, 'Wr': Wr, 'Wg': Wg, 'Wu': Wu, 'Wd': Wd}
    _L0_ffn_all = _L0_ffn_setup()
    _L0_ffn_in = {k: v for k, v in _L0_ffn_all.items() if k in ('Wr', 'Wg', 'Wu', 'Wd')}
    del _L0_ffn_all
    return {'x': x, 'itok_BxS_13_99985': itok_BxS_13_99985, 'ctx_2048': ctx_2048, 'L0_attn_cu_seqlens': _L0_attn_in['cu_seqlens'], 'L0_attn_Wqkv': _L0_attn_in['Wqkv'], 'L0_attn_Wz': _L0_attn_in['Wz'], 'L0_attn_Wa': _L0_attn_in['Wa'], 'L0_attn_Wb': _L0_attn_in['Wb'], 'L0_attn_conv_w': _L0_attn_in['conv_w'], 'L0_attn_A_log': _L0_attn_in['A_log'], 'L0_attn_dt_bias': _L0_attn_in['dt_bias'], 'L0_attn_norm_w': _L0_attn_in['norm_w'], 'L0_attn_Wout': _L0_attn_in['Wout'], 'L0_ffn_Wr': _L0_ffn_in['Wr'], 'L0_ffn_Wg': _L0_ffn_in['Wg'], 'L0_ffn_Wu': _L0_ffn_in['Wu'], 'L0_ffn_Wd': _L0_ffn_in['Wd']}

def reference(x, itok_BxS_13_99985, ctx_2048, L0_attn_cu_seqlens, L0_attn_Wqkv, L0_attn_Wz, L0_attn_Wa, L0_attn_Wb, L0_attn_conv_w, L0_attn_A_log, L0_attn_dt_bias, L0_attn_norm_w, L0_attn_Wout, L0_ffn_Wr, L0_ffn_Wg, L0_ffn_Wu, L0_ffn_Wd):
    import jax
    import jax.numpy as jnp

    def _L0_attn_ref(x, cu_seqlens, Wqkv, Wz, Wa, Wb, conv_w, A_log, dt_bias, norm_w, Wout):
        import jax, jax.numpy as jnp
        import numpy as np
        DIM, HK, HV, DK, DV, KC = (256, 16, 32, 128, 128, 4)
        B, L = (1, 1024)
        EPS = 1e-06

        def _causal_conv_silu(qkv, conv_w, seq_idx):
            Bb, Ll, C = qkv.shape
            xp = jnp.pad(qkv, ((0, 0), (KC - 1, 0), (0, 0)))
            sp = jnp.pad(seq_idx, ((0, 0), (KC - 1, 0)), constant_values=-1)
            out = jnp.zeros_like(qkv)
            for i in range(KC):
                m = (sp[:, i:i + Ll] == seq_idx)[..., None]
                out = out + conv_w[:, i] * jnp.where(m, xp[:, i:i + Ll], 0.0)
            return jax.nn.silu(out)

        def _l2norm(x):
            return x * jax.lax.rsqrt(jnp.sum(x * x, axis=-1, keepdims=True) + EPS)
        Bb, Ll, _ = x.shape
        qkv = x @ Wqkv
        z = x @ Wz
        a = x @ Wa
        b = x @ Wb
        pos = jnp.arange(Ll)
        seq_idx = jnp.searchsorted(cu_seqlens[1:-1], pos, side='right').astype(jnp.int32)
        seq_idx = jnp.broadcast_to(seq_idx[None, :], (Bb, Ll))
        mixed = _causal_conv_silu(qkv, conv_w, seq_idx)
        key_dim, value_dim = (HK * DK, HV * DV)
        q, k, v = jnp.split(mixed, [key_dim, 2 * key_dim], axis=-1)
        q = q.reshape(Bb, Ll, HK, DK)
        k = k.reshape(Bb, Ll, HK, DK)
        v = v.reshape(Bb, Ll, HV, DV)
        rep = HV // HK
        q = jnp.repeat(q, rep, axis=2)
        k = jnp.repeat(k, rep, axis=2)
        g = -jnp.exp(A_log) * jax.nn.softplus(a + dt_bias)
        beta = jax.nn.sigmoid(b)
        q = _l2norm(q) * DK ** (-0.5)
        k = _l2norm(k)
        starts = jnp.zeros((Ll,), bool).at[cu_seqlens[:-1]].set(True)

        def step(S, inp):
            q_t, k_t, v_t, g_t, b_t, s_t = inp
            S = jnp.where(s_t, 0.0, S)
            S = S * jnp.exp(g_t)[..., None, None]
            kv = jnp.einsum('bhk,bhkv->bhv', k_t, S)
            delta = (v_t - kv) * b_t[..., None]
            S = S + k_t[..., :, None] * delta[..., None, :]
            o = jnp.einsum('bhk,bhkv->bhv', q_t, S)
            return (S, o)
        S0 = jnp.zeros((Bb, HV, DK, DV), q.dtype)
        xs = (jnp.moveaxis(q, 1, 0), jnp.moveaxis(k, 1, 0), jnp.moveaxis(v, 1, 0), jnp.moveaxis(g, 1, 0), jnp.moveaxis(beta, 1, 0), starts)
        _, o = jax.lax.scan(step, S0, xs)
        o = jnp.moveaxis(o, 0, 1)
        zh = z.reshape(Bb, Ll, HV, DV)
        y = o * jax.nn.silu(zh)
        y = y * jax.lax.rsqrt(jnp.mean(y * y, axis=-1, keepdims=True) + EPS) * norm_w
        return y.reshape(Bb, Ll, HV * DV) @ Wout

    def _L0_xattn_ref(hidden_states, token_ids, Wg, Wu, Wd):
        import jax, jax.numpy as jnp
        import numpy as np
        B, S, D = (4, 512, 256)
        E = 4
        F = 1024 // E
        VOCAB = 12500
        tokens_per_expert = VOCAB // E
        tid = jnp.clip(token_ids, 0, VOCAB - 1)
        expert_ids = jnp.minimum(tid // tokens_per_expert, E - 1)
        out = jnp.zeros_like(hidden_states)
        for e in range(E):
            g = jax.nn.silu(jnp.einsum('bsd,fd->bsf', hidden_states, Wg[e]))
            u = jnp.einsum('bsd,fd->bsf', hidden_states, Wu[e])
            y = jnp.einsum('bsf,df->bsd', g * u, Wd[e])
            out = jnp.where((expert_ids == e)[..., None], y, out)
        return out

    def _L0_ffn_ref(x, Wr, Wg, Wu, Wd):
        import jax, jax.numpy as jnp
        import numpy as np
        B, T, D = (4, 256, 256)
        E = 8
        K = 2
        F = 1024 // (E // 2)
        probs = jax.nn.softmax(x @ Wr, axis=-1)
        topk_w, topk_idx = jax.lax.top_k(probs, K)
        topk_w = topk_w / jnp.sum(topk_w, axis=-1, keepdims=True)
        output = jnp.zeros_like(x)
        for i in range(E):
            sel = topk_idx == i
            w_i = jnp.sum(topk_w * sel.astype(x.dtype), axis=-1, keepdims=True)
            h = jax.nn.silu(x @ Wg[i]) * (x @ Wu[i])
            e_out = h @ Wd[i]
            output = output + w_i * e_out
        return output
    x = _layernorm(x + _L0_attn_ref(x, L0_attn_cu_seqlens, L0_attn_Wqkv, L0_attn_Wz, L0_attn_Wa, L0_attn_Wb, L0_attn_conv_w, L0_attn_A_log, L0_attn_dt_bias, L0_attn_norm_w, L0_attn_Wout), axis=-1)
    x = _layernorm(x + _L0_xattn_ref(x, itok_BxS_13_99985, ctx_2048, ctx_2048, ctx_2048), axis=-1)
    x = _layernorm(x + _L0_ffn_ref(x, L0_ffn_Wr, L0_ffn_Wg, L0_ffn_Wu, L0_ffn_Wd), axis=-1)
    return x

_drawn_inputs = setup_inputs


def setup_inputs(seed=0):
    import zlib

    import numpy as np

    out = dict(_drawn_inputs(seed))
    spreads = {'L0_attn_A_log': (0.0, 0.376), 'L0_attn_dt_bias': (1.0, 0.6), 'L0_attn_norm_w': (1.0, 0.2)}
    factors = {'L0_attn_Wa': 4.998}
    for name, (base, spread) in spreads.items():
        noise = np.random.default_rng([zlib.crc32(name.encode()), seed]).standard_normal(out[name].shape)
        drawn = base * np.exp(spread * noise) if base else spread * noise
        out[name] = jnp.asarray(drawn.astype(out[name].dtype))
    for name, factor in factors.items():
        out[name] = (out[name] * factor).astype(out[name].dtype)
    return out
```

```python
import math
from contextlib import ExitStack

import concourse.bass as bass
import numpy as np
from concourse import mybir

P = 128
B, S, D = 4, 256, 256
T = B * S
NT = T // P
KT = D // P
HK, HV = 16, 32
TAPS = 4
E1, E2 = 4, 8
F = 256
HALF = T // 2
LEVELS = 7
NEG = -30000.0
QEPS, NEPS, LEPS = 1e-6, 1e-6, 1e-5
NC = 5

C_M0, C_M1, C_SUF, C_PRE, C_ROW, C_COL, C_ID, C_ONE, C_E8, C_END = np.cumsum(
    [0, 256, 128, 128, 128, 256, 2, 128, 128, 64]).tolist()


def constants():
    p = np.arange(P)[:, None]
    i = np.arange(S)[None, :]
    f = i[:, :P]
    c = np.zeros((P, C_END), np.float32)
    c[:, C_M0:C_M1] = np.where(p <= i, 0.0, NEG)
    c[:, C_M1:C_SUF] = np.where(p <= f, 0.0, NEG)
    c[:, C_SUF:C_PRE] = np.where(p > f, -1.0, 0.0)
    c[:, C_PRE:C_ROW] = np.where(p <= f, 1.0, 0.0)
    c[:, C_ROW:C_COL] = i
    c[:, C_COL:C_ID] = p + P * np.arange(2)[None, :]
    c[:, C_ID:C_ONE] = p == f
    c[:, C_ONE:C_E8] = 1.0
    c[:, C_E8:C_END] = np.tile(np.arange(E2), NT)[None, :]
    same = [(p >> n) == (f >> n) for n in range(LEVELS + 1)]
    h = np.zeros((P, LEVELS + 2, P), np.float16)
    for n in range(LEVELS):
        h[:, n] = same[0].astype(int) + same[n].astype(int) - same[n + 1].astype(int)
    h[:, LEVELS] = same[0]
    h[:, LEVELS + 1] = h[:, 0].T
    return c, h


def build(nc, x, ids, ctx_in, cu, Wqkv, Wz, Wa, Wb, conv_w, A_log, dt_bias, norm_w, Wout,
          Wr, Wg, Wu, Wd, consts, levels, g_rows, out):
    f32, f16, i32 = mybir.dt.float32, mybir.dt.float16, mybir.dt.int32
    ALU, ACT, AX = mybir.AluOpType, mybir.ActivationFunctionType, mybir.AxisListType
    ds = bass.ds
    stack = ExitStack()
    with stack:
        def sb(name, shape, dt=f32):
            return stack.enter_context(nc.sbuf_tensor(name, shape, dt))

        attention = stack.enter_context(ExitStack())

        def own(name, shape, dt=f32):
            return attention.enter_context(nc.sbuf_tensor(name, shape, dt))

        def sem(name):
            return stack.enter_context(nc.semaphore(name))

        waits_passed = sem("waits_passed")

        def apart(engine):
            engine.sem_inc(waits_passed, 1)

        def two(name):
            return [sem(f"{name}{r}") for r in range(2)]

        cst = sb("cst", [P, C_END])
        acc = sb("acc", [P, NT, D])
        xT = sb("xT", [P, KT, T])
        eps_l = sb("eps_l", [P, 1])
        lev = own("lev", [P, LEVELS + 2, P], f16)
        ident, ones = cst[:, C_ID:C_ONE], cst[:, C_ONE:C_E8]
        wA = own("wA", [P, KT, 4, P])
        wZ = own("wZ", [P, KT, 2 * P])
        wO = own("wO", [P, 2, D])
        cw = own("cw", [P, 4, TAPS])
        Gb = own("Gb", [P, 2, T])
        nw = own("nw", [P, 1])
        wab = own("wab", [P, KT, 2 * HV])
        hb = own("hb", [P, 2, HV])
        cu_i = own("cu_i", [P, NC], i32)
        cu_f = own("cu_f", [P, NC])
        cnt = own("cnt", [P, 2, S])
        cntc = own("cntc", [P, 2])
        M0 = own("M0", [P, S])
        M1 = own("M1", [P, P])
        tmpm = own("tmpm", [P, S])
        cmask = own("cmask", [P, TAPS - 1, S])
        bad = own("bad", [P, 1])
        flag = own("flag", [P, 1], i32)
        u_ab = own("u_ab", [P, NT, 2 * HV])
        v_ab = own("v_ab", [P, NT, 2 * HV])
        w_ab = own("w_ab", [P, NT, 2 * HV])
        ea = own("ea", [P, HV])
        g_tok = own("g_tok", [P, 2, B, HV])
        G_tok = own("G_tok", [P, NT, HV])
        bias = own("bias", [P, NT, HV])
        bcur = own("bcur", [P, NT, 2])
        Grow = own("Grow", [HV, T])
        cv = [own(f"cv{r}", [P, 2, S]) for r in range(2)]
        ct_ = [own(f"ct{r}", [P, 2, S]) for r in range(2)]
        KQ = own("KQ", [P, 2, T])
        VV = own("VV", [P, 2, T])
        sq = [own(f"sq{r}", [P, HALF]) for r in range(2)]
        ln = [own(f"ln{r}", [P, HALF]) for r in range(2)]
        sz = own("sz", [P, NT, 2 * P])
        gm = [own(f"gm{r}", [P, 2, 3 * P]) for r in range(2)]
        Ex = [own(f"Ex{r}", [P, 2, 3 * P]) for r in range(2)]
        AP0 = [own(f"AP0_{b}", [P, 2, 2, S]) for b in range(B)]
        AP1 = [own(f"AP1_{b}", [P, 2, 2, P]) for b in range(B)]
        Ah = [own(f"Ah{b}", [P, 2, 2, P], f16) for b in range(B)]
        R = [own(f"R{b}", [P, 2, 2, P]) for b in range(B)]
        Rh = [own(f"Rh{b}", [P, 2, 2, P], f16) for b in range(B)]
        Tn = [own(f"Tn{r}", [P, 4, P], f16) for r in range(2)]
        Tt = [own(f"Tt{r}", [P, 4, P], f16) for r in range(2)]
        Zn = [own(f"Zn{r}", [P, 4, P], f16) for r in range(2)]
        W = [own(f"W{r}", [P, 2, 2, P]) for r in range(2)]
        rr = [own(f"rr{r}", [P, 2, 2, P], f16) for r in range(2)]
        y = [own(f"y{r}", [P, 2, 2, P]) for r in range(2)]
        y2 = [own(f"y2{r}", [P, 2, 2, P]) for r in range(2)]
        ss = [own(f"ss{r}", [P, 4]) for r in range(2)]
        sl = [own(f"sl{r}", [P, 4]) for r in range(2)]
        rs = [own(f"rs{r}", [P, 4]) for r in range(2)]
        yT = own("yT", [P, 2, T])
        eps_q = own("eps_q", [P, 1])
        eps_s = own("eps_s", [P, 1])
        eps_n = own("eps_n", [P, 1])

        PJ = [stack.enter_context(nc.psum_tensor(f"PJ{r}", [P, 512], f32)) for r in range(2)]
        PA, PB, PC = ([stack.enter_context(nc.psum_tensor(f"{n}{r}", [P, 512], f32))
                       for r in range(2)] for n in ("PA", "PB", "PC"))

        in_x, in_c, in_l, in_s, in_e = sem("in_x"), sem("in_c"), sem("in_l"), sem("in_s"), sem("in_e")
        mask_chain, masks_done = sem("mask_chain"), sem("masks_done")
        eps_done = sem("eps_done")
        xt_mm, xt_done = two("xt_mm"), two("xt_done")
        ab_mm, ab_act, ab_chain, g_done = sem("ab_mm"), sem("ab_act"), sem("ab_chain"), sem("g_done")
        G_mm, G_done, Gt_mm, Gt_done, G_out = sem("G_mm"), sem("G_done"), sem("Gt_mm"), sem("Gt_done"), sem("G_out")
        wA_in, wZ_in, wO_in, cw_in, Gb_in = sem("wA_in"), sem("wZ_in"), sem("wO_in"), sem("cw_in"), sem("Gb_in")
        nw_in = in_e
        pj_full, pj_free = two("pj_full"), two("pj_free")
        tap_done, mix_done = two("tap_done"), two("mix_done")
        conv_chain = sem("conv_chain")
        sq_done, ln_done, rn_done, norm_done = two("sq_done"), two("ln_done"), two("rn_done"), two("norm_done")
        bcur_done = sem("bcur_done")
        kq_mm, vt_mm = two("kq_mm"), two("vt_mm")
        gm_done, e_done, r_done, ap_done = two("gm_done"), two("e_done"), two("r_done"), two("ap_done")
        diag_done, ah_done, tt0_done = two("diag_done"), two("ah_done"), two("tt0_done")
        at_mm, z_done, tt_mm, t_done = two("at_mm"), two("z_done"), two("tt_mm"), two("t_done")
        w0_mm, w0_done, aw_mm, rr_done = two("w0_mm"), two("w0_done"), two("aw_mm"), two("rr_done")
        cor_mm, w_done, x_mm, r2_done = two("cor_mm"), two("w_done"), two("x_mm"), two("r2_done")
        o_mm, y_done, ysq_done, ss_done = two("o_mm"), two("y_done"), two("ysq_done"), two("ss_done")
        sl_done, rs_done, yn_done, yt_mm, yt_done = (two("sl_done"), two("rs_done"), two("yn_done"),
                                                     two("yt_mm"), two("yt_done"))

        with nc.Block() as block:
            @block.sync
            def _(sp):
                xf = x.rearrange("b s d -> (b s) d").rearrange("(n p) d -> p n d", p=P)
                sp.dma_start(acc[:, :, :], xf).then_inc(in_x, 16)
                sp.dma_start(cst[:, :], consts).then_inc(in_c, 16)
                sp.dma_start(lev[:, :, :], levels).then_inc(in_l, 16)
                sp.dma_start(cu_i[:, :], cu.rearrange("(o n) -> o n", o=1).to_broadcast((P, NC))).then_inc(in_s, 16)
                sp.wait_ge(Gt_done, NT)
                sp.dma_start(g_rows, Grow[:, :]).then_inc(G_out, 16)
                sp.wait_ge(G_out, 16)

            @block.scalar
            def _(act):
                act.dma_start(wab[:, :, 0:HV], Wa.rearrange("(k p) n -> p k n", p=P)).then_inc(in_e, 16)
                act.dma_start(wab[:, :, HV:], Wb.rearrange("(k p) n -> p k n", p=P)).then_inc(in_e, 16)
                act.dma_start(hb[:, 0, :], A_log.rearrange("(o n) -> o n", o=1).to_broadcast((P, HV))).then_inc(in_e, 16)
                act.dma_start(hb[:, 1, :], dt_bias.rearrange("(o n) -> o n", o=1).to_broadcast((P, HV))).then_inc(in_e, 16)
                act.dma_start(nw[:, :], norm_w.rearrange("(p o) -> p o", o=1)).then_inc(in_e, 16)
                act.wait_ge(in_e, 80)
                nc.scalar.activation(ea[:, :], hb[:, 0, :], ACT.Exp).then_inc(ab_act, 1)
                act.wait_ge(ab_chain, 4)
                nc.scalar.activation(w_ab[:, :, :], v_ab[:, :, :], ACT.Exp).then_inc(ab_act, 1)
                act.wait_ge(ab_act, 2)
                act.wait_ge(eps_done, 1)
                nc.scalar.activation(v_ab[:, :, :], w_ab[:, :, :], ACT.Ln, bias=ones[:, 0:1]).then_inc(ab_act, 1)

            @block.gpsimd
            def _(pool):
                nc.gpsimd.memset(eps_q[:, :], QEPS)
                nc.gpsimd.memset(eps_s[:, :], -0.5 * math.log(P))
                nc.gpsimd.memset(eps_l[:, :], LEPS)
                nc.gpsimd.memset(eps_n[:, :], NEPS).then_inc(eps_done, 1)

            @block.vector
            def _(dve):
                n = [0]

                def link(ins):
                    n[0] += 1
                    ins.then_inc(mask_chain, 1)
                    dve.wait_ge(mask_chain, n[0])

                dve.wait_ge(in_c, 16)
                dve.wait_ge(in_s, 16)
                link(nc.vector.tensor_copy(cu_f[:, :], cu_i[:, :]))
                row = cst[:, C_ROW:C_COL]
                link(nc.vector.tensor_scalar(cnt[:, 1, :], row, cu_f[:, 1:2], None, ALU.is_ge))
                for m in (2, 3):
                    link(nc.vector.scalar_tensor_tensor(cnt[:, 1, :], row, cu_f[:, m:m + 1], cnt[:, 1, :],
                                                        ALU.is_ge, ALU.add))
                link(nc.vector.scalar_tensor_tensor(cnt[:, 0, :], row, cu_f[:, 0:1], cnt[:, 1, :],
                                                    ALU.is_ge, ALU.add))
                col = cst[:, C_COL:C_ID]
                link(nc.vector.tensor_scalar(cntc[:, :], col, cu_f[:, 0:1], None, ALU.is_ge))
                for m in (1, 2, 3):
                    link(nc.vector.scalar_tensor_tensor(cntc[:, :], col, cu_f[:, m:m + 1], cntc[:, :],
                                                        ALU.is_ge, ALU.add))
                link(nc.vector.tensor_scalar(tmpm[:, :], cnt[:, 0, :], cntc[:, 0:1], NEG, ALU.not_equal, ALU.mult))
                link(nc.vector.tensor_tensor(M0[:, :], tmpm[:, :], cst[:, C_M0:C_M1], ALU.add))
                link(nc.vector.tensor_scalar(tmpm[:, 0:P], cnt[:, 0, P:S], cntc[:, 1:2], NEG, ALU.not_equal, ALU.mult))
                link(nc.vector.tensor_tensor(M1[:, :], tmpm[:, 0:P], cst[:, C_M1:C_SUF], ALU.add))
                link(nc.vector.memset(cmask[:, :, :], 1.0))
                for s in range(1, TAPS):
                    link(nc.vector.tensor_tensor(cmask[:, s - 1, s:S], cnt[:, 1, s:S], cnt[:, 1, 0:S - s],
                                                 ALU.is_equal))
                link(nc.vector.tensor_reduce(bad[:, :], cmask[:, :, :], AX.XY, ALU.min))
                link(nc.vector.tensor_copy(flag[:, :], bad[:, :]))

                for q in range(KT * 2):
                    dve.wait_ge(xt_mm[q % 2], q // 2 + 1)
                    k, hf = q // 2, q % 2
                    nc.vector.tensor_copy(xT[:, k, hf * HALF:(hf + 1) * HALF], PJ[q % 2][:, :]).then_inc(xt_done[q % 2], 1)

                dve.wait_ge(in_e, 80)
                dve.wait_ge(ab_mm, 1)
                ab = PA[0][:, :].rearrange("p (n c) -> p n c", c=2 * HV)
                nc.vector.tensor_tensor(u_ab[:, :, 0:HV], ab[:, :, 0:HV],
                                        hb[:, 1:2, :].to_broadcast((P, NT, HV)), ALU.add).then_inc(ab_chain, 1)
                nc.vector.tensor_scalar(u_ab[:, :, HV:], ab[:, :, HV:], -1.0, None, ALU.mult).then_inc(ab_chain, 1)
                dve.wait_ge(ab_chain, 2)
                nc.vector.tensor_scalar(v_ab[:, :, :], u_ab[:, :, :], -1.0, None, ALU.mult).then_inc(ab_chain, 1)
                dve.wait_ge(ab_chain, 3)
                nc.vector.tensor_tensor(v_ab[:, :, :], v_ab[:, :, :], u_ab[:, :, :], ALU.min).then_inc(ab_chain, 1)
                dve.wait_ge(ab_act, 3)
                nc.vector.scalar_tensor_tensor(u_ab[:, :, :], u_ab[:, :, :], 0.0, v_ab[:, :, :],
                                               ALU.max, ALU.add).then_inc(ab_chain, 1)
                dve.wait_ge(ab_chain, 5)
                for c in range(2):
                    nc.vector.scalar_tensor_tensor(
                        g_tok[:, c, :, :], u_ab[:, c::2, 0:HV], -1.0,
                        ea[:, :].rearrange("p (o h) -> p o h", o=1).to_broadcast((P, B, HV)),
                        ALU.mult, ALU.mult).then_inc(g_done, 1)
                dve.wait_ge(G_mm, 1)
                for c in range(2):
                    nc.vector.tensor_copy(G_tok[:, c::2, :], PB[0][:, c * P:(c + 1) * P].rearrange(
                        "p (b h) -> p b h", b=B)).then_inc(G_done, 1)
                dve.wait_ge(G_done, 2)
                nc.vector.scalar_tensor_tensor(bias[:, :, :], u_ab[:, :, HV:], -1.0, G_tok[:, :, :],
                                               ALU.mult, ALU.subtract).then_inc(G_done, 1)
                for n_ in range(NT):
                    dve.wait_ge(Gt_mm, n_ + 1)
                    nc.vector.tensor_copy(Grow[:, n_ * P:(n_ + 1) * P], PC[n_ % 2][0:HV, 0:P]).then_inc(Gt_done, 1)

            @block.tensor
            def _(pe):
                pe.wait_ge(in_x, 16)
                pe.wait_ge(in_c, 16)
                for q in range(KT * 2):
                    k, hf = q // 2, q % 2
                    if q >= 2:
                        pe.wait_ge(xt_done[q % 2], q // 2)
                    for n_ in range(4):
                        last = nc.tensor.transpose(PJ[q % 2][:, n_ * P:(n_ + 1) * P],
                                                   acc[:, hf * 4 + n_, k * P:(k + 1) * P], ident)
                    last.then_inc(xt_mm[q % 2], 1)
                pe.wait_ge(in_e, 80)
                for r in range(2):
                    pe.wait_ge(xt_done[r], 2)
                for n_ in range(NT):
                    for k in range(KT):
                        last = nc.tensor.matmul(PA[0][:, n_ * 2 * HV:(n_ + 1) * 2 * HV], xT[:, k, n_ * P:(n_ + 1) * P],
                                                wab[:, k, :], start=(k == 0), stop=(k == KT - 1))
                last.then_inc(ab_mm, 1)
                pe.wait_ge(g_done, 2)
                for c, tri in ((0, C_SUF), (1, C_PRE)):
                    last = nc.tensor.matmul(PB[0][:, c * P:(c + 1) * P], cst[:, tri:tri + P],
                                            g_tok[:, c, :, :].rearrange("p b h -> p (b h)"), start=True, stop=True)
                last.then_inc(G_mm, 1)
                pe.wait_ge(G_done, 2)
                for n_ in range(NT):
                    if n_ >= 2:
                        pe.wait_ge(Gt_done, n_ - 1)
                    nc.tensor.transpose(PC[n_ % 2][0:HV, 0:P], G_tok[:, n_, :], ident).then_inc(Gt_mm, 1)

        CJ = [("C", ct, hf) for ct in range(4) for hf in range(2)]
        NJ = [("N", t, hf) for t in range(2) for hf in range(2)]
        ZJ = [("Z", q, 0) for q in range(4)]
        OJ = [("O", q, 0) for q in range(4)]
        FULL = ZJ + CJ + NJ + OJ
        LASTJ = ZJ + OJ
        FIRST = CJ + NJ
        STEPS = (["T0"] + [x_ for n in range(1, LEVELS) for x_ in (("AT", n), ("TZ", n))]
                 + [("W0", 0), ("AW", 0), ("CO", 0), ("X", 1), ("W0", 1), ("AW", 1), ("CO", 1), "O", "SS", "YT"])

        def schedule(jobs):
            early = [j for j in jobs if j[0] != "O"]
            late = [j for j in jobs if j[0] == "O"]
            plan = {}
            slots = [(p, k) for p in range(2) for k in range(len(STEPS))]
            for n_, j in enumerate(early):
                at = slots[n_] if n_ < 4 else slots[4 + ((n_ - 4) * (len(slots) - 6)) // max(1, len(early) - 4)]
                plan.setdefault(at, []).append(j)
            plan.setdefault("end", []).extend(late)
            return plan

        def walk(jobs, base, each_set, job, all_groups):
            plan = schedule(jobs)
            at = [0]

            def run(some):
                for j in some:
                    job(j, at[0] % 2, base + at[0] // 2)
                    at[0] += 1
            for b in range(B):
                all_groups(b)
            for p in range(2):
                for k, step in enumerate(STEPS):
                    for s in range(2):
                        each_set(step, 2 * p + s, s, p)
                    run(plan.get((p, k), []))
            run(plan["end"])

        RING0, RING = len(FIRST) // 2, len(FULL) // 2
        NS = LEVELS
        RING_Z = 0

        def first(i):
            return isinstance(i, int) and i == 0

        with nc.Block() as block:
            @block.sync
            def _(sp):
                def load_A(i):
                    v = lambda a: a.rearrange("(k p) n -> p k n", p=P)
                    q_cols = Wqkv[:, ds(i * P, P)]
                    k_cols = Wqkv[:, ds(i * P + HK * P, P)]
                    v_cols = Wqkv[:, ds(i * 2 * P + 2 * HK * P, 2 * P)]
                    sp.dma_start(wA[:, :, 0, :], v(k_cols)).then_inc(wA_in, 16)
                    sp.dma_start(wA[:, :, 1, :], v(q_cols)).then_inc(wA_in, 16)
                    sp.dma_start(wA[:, :, 2:4, :].rearrange("p k a n -> p k (a n)"), v(v_cols)).then_inc(wA_in, 16)
                    sp.dma_start(cw[:, 0, :], conv_w[ds(i * P + HK * P, P), :]).then_inc(cw_in, 16)
                    sp.dma_start(cw[:, 1, :], conv_w[ds(i * P, P), :]).then_inc(cw_in, 16)
                    sp.dma_start(cw[:, 2:4, :], conv_w[ds(i * 2 * P + 2 * HK * P, 2 * P), :].rearrange(
                        "(a p) n -> p a n", p=P)).then_inc(cw_in, 16)

                def load_G(i):
                    for h in range(2):
                        sp.dma_start(Gb[:, h, :], g_rows[ds(i * 2 + h, 1), :].to_broadcast((P, T))).then_inc(Gb_in, 16)

                def load_Z(i):
                    sp.dma_start(wZ[:, :, :], Wz[:, ds(i * 2 * P, 2 * P)].rearrange("(k p) n -> p k n", p=P)).then_inc(wZ_in, 16)

                def load_O(i):
                    sp.dma_start(wO[:, :, :], Wout[ds(i * 2 * P, 2 * P), :].rearrange("(a p) n -> p a n", p=P)).then_inc(wO_in, 16)

                load_A(0)
                load_G(0)
                load_Z(0)
                load_O(0)

                def head(i):
                    for r in range(2):
                        sp.wait_ge(norm_done[r], (i + 1) * 2)
                    load_A(i + 1)
                    for s in range(2):
                        sp.wait_ge(gm_done[s], (i + 1) * 2)
                    load_G(i + 1)
                    sp.wait_ge(pj_full[1], RING0 + i * RING + len(ZJ) // 2)
                    apart(sp)
                    load_Z(i + 1)
                    sp.wait_ge(pj_full[1], RING0 + (i + 1) * RING)
                    apart(sp)
                    load_O(i + 1)

                with sp.Fori(0, HK - 1) as i:
                    head(i)

            @block.gpsimd
            def _(pool):
                def job(j, r, m, i):
                    kind, t, hf = j
                    if kind != "N":
                        return
                    pool.wait_ge(mix_done[hf], i * 4 + t + 1)
                    if not first(i) or t:
                        pool.wait_ge(norm_done[hf], i * 2 + t)
                    nc.gpsimd.tensor_tensor(sq[hf][:, :], KQ[:, t, hf * HALF:(hf + 1) * HALF],
                                            KQ[:, t, hf * HALF:(hf + 1) * HALF], ALU.mult).then_inc(sq_done[hf], 1)

                def group(b, i):
                    s, n = b % 2, b // 2
                    if b == 0:
                        nc.gpsimd.tensor_copy(bcur[:, :, :], bias[:, :, ds(i * 2, 2)]).then_inc(bcur_done, 1)
                        pool.wait_ge(Gb_in, i * 32 + 32)
                    if n:
                        pool.wait_ge(e_done[s], i * 2 + n)
                    Gv = Gb[:, :, b * S:(b + 1) * S]
                    nc.gpsimd.tensor_tensor(gm[s][:, :, 0:S], Gv, M0[:, :].rearrange("p (o t) -> p o t", o=1)
                                            .to_broadcast((P, 2, S)), ALU.add)
                    nc.gpsimd.tensor_tensor(gm[s][:, :, S:], Gv[:, :, P:S], M1[:, :].rearrange("p (o t) -> p o t", o=1)
                                            .to_broadcast((P, 2, P)), ALU.add).then_inc(gm_done[s], 1)
                    if b >= 1:
                        unit_diagonal(b - 1, i)
                    if b == B - 1:
                        unit_diagonal(b, i)

                def unit_diagonal(b, i):
                    s, n = b % 2, b // 2
                    pool.wait_ge(ap_done[s], i * 2 + n + 1)
                    apart(pool)
                    for c, a in ((0, AP0[b][:, :, 0, 0:P]), (1, AP1[b][:, :, 0, :])):
                        nc.gpsimd.affine_select(out=a, in_=a, compare_op=ALU.not_equal, fill=1.0, base=0,
                                                pattern=[[0, 2], [1, P]], channel_multiplier=-1).then_inc(diag_done[s], 1)
                    pool.wait_ge(diag_done[s], i * 4 + n * 2 + 2)
                    apart(pool)
                    nc.gpsimd.tensor_copy(Ah[b][:, :, 0, :], AP0[b][:, :, 0, 0:P]).then_inc(ah_done[s], 1)
                    nc.gpsimd.tensor_copy(Ah[b][:, :, 1, :], AP1[b][:, :, 0, :]).then_inc(ah_done[s], 1)

                def step(st, b, s, p, i):
                    if st == "T0":
                        pool.wait_ge(ah_done[s], i * 4 + 4)
                        pool.wait_ge(at_mm[s], (i * 2 + p) * NS + 1)
                        nc.gpsimd.tensor_tensor(
                            Tt[s][:, :, :], Ah[b][:, :, :, :].rearrange("p a c t -> p (a c) t"),
                            lev[:, LEVELS + 1:LEVELS + 2, :].to_broadcast((P, 4, P)), ALU.mult).then_inc(tt0_done[s], 1)
                    elif st == "O":
                        pool.wait_ge(y_done[s], i * 2 + p + 1)
                        nc.gpsimd.tensor_tensor(y2[s][:, :, :, :], y[s][:, :, :, :], y[s][:, :, :, :],
                                                ALU.mult).then_inc(ysq_done[s], 1)
                    elif st == "YT":
                        pool.wait_ge(rs_done[s], i * 2 + p + 1)
                        nc.gpsimd.tensor_tensor(
                            y2[s][:, :, :, :].rearrange("p a c t -> p (a c) t"),
                            y[s][:, :, :, :].rearrange("p a c t -> p (a c) t"),
                            rs[s][:, :].rearrange("p (u o) -> p u o", o=1).to_broadcast((P, 4, P)),
                            ALU.mult).then_inc(yn_done[s], 1)

                for n_, j in enumerate(FIRST):
                    job(j, n_ % 2, n_ // 2, 0)

                def head(i, jobs, base):
                    walk(jobs, base, lambda st, b, s, p: step(st, b, s, p, i),
                         lambda j, r, m: job(j, r, m, i + 1), lambda b: group(b, i))
                with pool.Fori(0, HK - 1) as i:
                    head(i, FULL, RING0 + i * RING)
                head(HK - 1, LASTJ, RING0 + (HK - 1) * RING)

            @block.scalar
            def _(act):
                def silu_mix(j, r, m, i):
                    kind, ct, hf = j
                    act.wait_ge(pj_free[r], m + 1)
                    dst = (KQ[:, ct, :] if ct < 2 else VV[:, ct - 2, :])[:, hf * HALF:(hf + 1) * HALF]
                    nc.scalar.activation(dst, cv[hf][:, :, :].rearrange("p b t -> p (b t)"), ACT.Silu).then_inc(
                        mix_done[hf], 1)

                hold = [None]

                def flush():
                    if hold[0]:
                        silu_mix(*hold[0])
                        hold[0] = None

                def job(j, r, m, i):
                    kind, t, hf = j
                    if kind == "C":
                        act.wait_ge(pj_full[r], m + 1)
                        act.wait_ge(cw_in, i * 48 + 48)
                        if not first(i) or t:
                            act.wait_ge(mix_done[hf], i * 4 + t)
                        nc.scalar.activation(cv[hf][:, :, :].rearrange("p b t -> p (b t)"), PJ[r][:, :], ACT.Copy,
                                             scale=cw[:, t, TAPS - 1:TAPS]).then_inc(tap_done[hf], 1)
                        flush()
                        hold[0] = (j, r, m, i)
                        return
                    flush()
                    if kind == "N":
                        act.wait_ge(pj_full[r], m + 1)
                        if not first(i) or t:
                            act.wait_ge(norm_done[hf], i * 2 + t)
                        nc.scalar.activation(ln[hf][:, :], PJ[r][:, :], ACT.Ln, bias=eps_q[:, :]).then_inc(pj_free[r], 1)
                        act.wait_ge(pj_free[r], m + 1)
                        kw = {"bias": eps_s[:, :]} if t == 1 else {}
                        nc.scalar.activation(ln[hf][:, :], ln[hf][:, :], ACT.Exp, scale=-0.5, **kw).then_inc(rn_done[hf], 1)
                    elif kind == "Z":
                        act.wait_ge(pj_full[r], m + 1)
                        nc.scalar.activation(sz[:, 2 * t:2 * t + 2, :].rearrange("p n d -> p (n d)"), PJ[r][:, :],
                                             ACT.Silu).then_inc(pj_free[r], 1)

                def group(b, i):
                    s, n = b % 2, b // 2
                    if b == 0:
                        act.wait_ge(bcur_done, i + 1)
                    act.wait_ge(gm_done[s], i * 2 + n + 1)
                    if n:
                        act.wait_ge(ap_done[s], i * 2 + n)
                    for h in range(2):
                        nc.scalar.activation(Ex[s][:, h, 0:S], gm[s][:, h, 0:S], ACT.Exp, bias=bcur[:, 2 * b, h:h + 1])
                        last = nc.scalar.activation(Ex[s][:, h, S:], gm[s][:, h, S:], ACT.Exp,
                                                    bias=bcur[:, 2 * b + 1, h:h + 1])
                    last.then_inc(e_done[s], 1)
                    act.wait_ge(vt_mm[s], i * 2 + n + 1)
                    src = PC[s][:, :]
                    nc.scalar.copy(Rh[b][:, :, :, :].rearrange("p a c t -> p (a c t)"), src)
                    nc.scalar.copy(R[b][:, :, :, :].rearrange("p a c t -> p (a c t)"), src).then_inc(r_done[s], 1)

                def step(st, b, s, p, i):
                    at = i * 2 + p
                    if st[0] == "TZ":
                        act.wait_ge(tt_mm[s], at * (LEVELS - 1) + st[1])
                        if st[1] < LEVELS - 1:
                            nc.scalar.copy(Tn[s][:, :, :].rearrange("p u t -> p (u t)"), PB[s][:, :])
                        nc.scalar.copy(Tt[s][:, :, :].rearrange("p u t -> p (u t)"), PC[s][:, :]).then_inc(t_done[s], 1)
                    elif st[0] == "W0":
                        act.wait_ge(w0_mm[s], at * 2 + st[1] + 1)
                        nc.scalar.copy(W[s][:, :, st[1], :], PA[s][:, 0:2 * P].rearrange("p (h t) -> p h t", h=2)).then_inc(
                            w0_done[s], 1)
                    elif st == "SS":
                        act.wait_ge(ss_done[s], at + 1)
                        nc.scalar.activation(sl[s][:, :], ss[s][:, :], ACT.Ln, bias=eps_n[:, :], scale=1.0 / P).then_inc(
                            sl_done[s], 1)
                        act.wait_ge(sl_done[s], at + 1)
                        nc.scalar.activation(rs[s][:, :], sl[s][:, :], ACT.Exp, scale=-0.5).then_inc(rs_done[s], 1)
                    elif st == "YT":
                        act.wait_ge(yt_mm[s], at + 1)
                        nc.scalar.activation(yT[:, :, b * S:(b + 1) * S],
                                             PA[s][:, :].rearrange("p (h t) -> p h t", h=2), ACT.Copy,
                                             scale=nw[:, 0:1]).then_inc(yt_done[s], 1)

                for n_, j in enumerate(FIRST):
                    job(j, n_ % 2, n_ // 2, 0)
                flush()

                def head(i, jobs, base):
                    walk(jobs, base, lambda st, b, s, p: step(st, b, s, p, i),
                         lambda j, r, m: job(j, r, m, i if j[0] in "ZO" else i + 1), lambda b: group(b, i))
                    flush()
                with act.Fori(0, HK - 1) as i:
                    head(i, FULL, RING0 + i * RING)
                head(HK - 1, LASTJ, RING0 + (HK - 1) * RING)

            @block.vector
            def _(dve):
                dve_flag = dve.value_load(flag[0:1, 0:1], min_val=0, max_val=1)
                hold = [None]

                def flush():
                    if hold[0]:
                        j, r, m, i = hold[0]
                        hold[0] = None
                        kind, t, hf = j
                        if kind == "C":
                            conv(r, m, t, hf, i)
                        elif kind == "N":
                            dve.wait_ge(rn_done[hf], i * 2 + t + 1)
                            kq = KQ[:, t, hf * HALF:(hf + 1) * HALF]
                            nc.vector.tensor_tensor(kq, kq, ln[hf][:, :], ALU.mult).then_inc(norm_done[hf], 1)
                        elif kind == "O":
                            dve.wait_ge(pj_full[r], m + 1)
                            at = acc[:, 2 * t:2 * t + 2, :].rearrange("p n d -> p (n d)")
                            nc.vector.tensor_tensor(at, at, PJ[r][:, :], ALU.add).then_inc(pj_free[r], 1)

                def job(j, r, m, i):
                    flush()
                    hold[0] = (j, r, m, i)

                def conv(r, m, t, hf, i):
                    dve.wait_ge(tap_done[hf], i * 4 + t + 1)
                    apart(dve)
                    n0 = (i * 8 + t * 2 + hf) * 5
                    src = PJ[r][:, :].rearrange("p (b t) -> p b t", b=2)

                    def tap(s, of):
                        return nc.vector.scalar_tensor_tensor(
                            cv[hf][:, :, s:S], of, cw[:, t, TAPS - 1 - s:TAPS - s], cv[hf][:, :, s:S],
                            ALU.mult, ALU.add)

                    with dve.If(dve_flag):
                        tap(1, src[:, :, 0:S - 1]).then_inc(conv_chain, 3)
                        dve.wait_ge(conv_chain, n0 + 3)
                        tap(2, src[:, :, 0:S - 2]).then_inc(conv_chain, 2)
                        dve.wait_ge(conv_chain, n0 + 5)
                        tap(3, src[:, :, 0:S - 3]).then_inc(pj_free[r], 1)
                    with dve.Else():
                        for s in range(1, TAPS):
                            masked = ct_[hf][:, :, s:S]
                            nc.vector.tensor_tensor(masked, src[:, :, 0:S - s],
                                                    cmask[:, s - 1:s, s:S].to_broadcast((P, 2, S - s)),
                                                    ALU.mult).then_inc(conv_chain, 1)
                            dve.wait_ge(conv_chain, n0 + 2 * s - 1)
                            if s < TAPS - 1:
                                tap(s, masked).then_inc(conv_chain, 1)
                                dve.wait_ge(conv_chain, n0 + 2 * s)
                            else:
                                tap(s, masked).then_inc(pj_free[r], 1)

                def group(b, i):
                    s, n = b % 2, b // 2
                    dve.wait_ge(kq_mm[s], i * 2 + n + 1)
                    dve.wait_ge(e_done[s], i * 2 + n + 1)
                    for h in range(2):
                        nc.vector.tensor_tensor(AP0[b][:, h, :, :], PA[s][:, :].rearrange("p (a t) -> p a t", a=2),
                                                Ex[s][:, h:h + 1, 0:S].to_broadcast((P, 2, S)), ALU.mult)
                        last = nc.vector.tensor_tensor(
                            AP1[b][:, h, :, :], PB[s][:, 0:S].rearrange("p (a t) -> p a t", a=2),
                            Ex[s][:, h:h + 1, S:].to_broadcast((P, 2, P)), ALU.mult)
                    last.then_inc(ap_done[s], 1)

                def step(st, b, s, p, i, base):
                    at = i * 2 + p
                    four = lambda n: lev[:, n:n + 1, :].to_broadcast((P, 4, P))
                    if st == "T0" or st[0] == "AT":
                        n = 0 if st == "T0" else st[1]
                        dve.wait_ge(at_mm[s], at * NS + n + 1)
                        nc.vector.tensor_tensor((Zn if n else Tn)[s][:, :, :],
                                                PA[s][:, :].rearrange("p (u t) -> p u t", u=4), four(n),
                                                ALU.mult).then_inc(z_done[s], 1)
                    elif st[0] == "AW":
                        dve.wait_ge(aw_mm[s], at * 2 + st[1] + 1)
                        nc.vector.tensor_tensor(rr[s][:, :, st[1], :], R[b][:, :, st[1], :],
                                                PB[s][:, 0:S].rearrange("p (h t) -> p h t", h=2),
                                                ALU.subtract).then_inc(rr_done[s], 1)
                    elif st[0] == "CO":
                        dve.wait_ge(cor_mm[s], at * 2 + st[1] + 1)
                        nc.vector.tensor_tensor(W[s][:, :, st[1], :], W[s][:, :, st[1], :],
                                                PA[s][:, S:].rearrange("p (h t) -> p h t", h=2),
                                                ALU.add).then_inc(w_done[s], 1)
                    elif st[0] == "X":
                        dve.wait_ge(x_mm[s], at + 1)
                        cross = PC[s][:, 0:S].rearrange("p (h t) -> p h t", h=2)
                        nc.vector.tensor_tensor(Rh[b][:, :, 1, :], R[b][:, :, 1, :], cross, ALU.subtract)
                        nc.vector.tensor_tensor(R[b][:, :, 1, :], R[b][:, :, 1, :], cross,
                                                ALU.subtract).then_inc(r2_done[s], 1)
                    elif st == "O":
                        dve.wait_ge(o_mm[s], at + 1)
                        dve.wait_ge(pj_free[b % 2], base + b // 2 + 1)
                        nc.vector.tensor_tensor(
                            y[s][:, :, :, :], PB[s][:, :].rearrange("p (h c t) -> p h c t", h=2, c=2),
                            sz[:, 2 * b:2 * b + 2, :].rearrange("p c (h t) -> p h c t", h=2),
                            ALU.mult).then_inc(y_done[s], 1)
                    elif st == "SS":
                        dve.wait_ge(ysq_done[s], at + 1)
                        nc.vector.tensor_reduce(ss[s][:, :], y2[s][:, :, :, :].rearrange("p a c t -> p (a c) t"),
                                                AX.X, ALU.add).then_inc(ss_done[s], 1)

                for n_, j in enumerate(FIRST):
                    job(j, n_ % 2, n_ // 2, 0)
                flush()

                def head(i, jobs, base):
                    walk(jobs, base, lambda st, b, s, p: step(st, b, s, p, i, base),
                         lambda j, r, m: job(j, r, m, i if j[0] in "ZO" else i + 1), lambda b: group(b, i))
                    flush()
                with dve.Fori(0, HK - 1) as i:
                    head(i, FULL, RING0 + i * RING)
                head(HK - 1, LASTJ, RING0 + (HK - 1) * RING)

            @block.tensor
            def _(pe):
                def job(j, r, m, i, base):
                    kind, t, hf = j
                    if not (isinstance(m, int) and m == 0):
                        pe.wait_ge(pj_free[r], m)
                    if kind == "C":
                        pe.wait_ge(wA_in, i * 48 + 48)
                        for k in range(KT):
                            last = nc.tensor.matmul(PJ[r][:, :], wA[:, k, t, :], xT[:, k, hf * HALF:(hf + 1) * HALF],
                                                    start=(k == 0), stop=(k == KT - 1))
                        last.then_inc(pj_full[r], 1)
                    elif kind == "N":
                        pe.wait_ge(sq_done[hf], i * 2 + t + 1)
                        nc.tensor.matmul(PJ[r][:, :], ones, sq[hf][:, :], start=True, stop=True).then_inc(pj_full[r], 1)
                    elif kind == "Z":
                        pe.wait_ge(wZ_in, i * 16 + 16)
                        for n_ in range(2):
                            for k in range(KT):
                                tok = (2 * t + n_) * P
                                last = nc.tensor.matmul(PJ[r][:, n_ * 2 * P:(n_ + 1) * 2 * P], xT[:, k, tok:tok + P],
                                                        wZ[:, k, :], start=(k == 0), stop=(k == KT - 1))
                        last.then_inc(pj_full[r], 1)
                    elif kind == "O":
                        pe.wait_ge(wO_in, i * 16 + 16)
                        pe.wait_ge(yt_done[t % 2], i * 2 + t // 2 + 1)
                        for n_ in range(2):
                            for h in range(2):
                                tok = (2 * t + n_) * P
                                last = nc.tensor.matmul(PJ[r][:, n_ * D:(n_ + 1) * D], yT[:, h, tok:tok + P],
                                                        wO[:, h, :], start=(h == 0), stop=(h == 1))
                        last.then_inc(pj_full[r], 1)

                def group(b, i):
                    s, n = b % 2, b // 2
                    pe.wait_ge(norm_done[b // 2], i * 2 + 2)
                    pe.wait_ge(mix_done[b // 2], i * 4 + 4)
                    if n:
                        pe.wait_ge(ap_done[s], i * 2 + n)
                        pe.wait_ge(r_done[s], i * 2 + n)
                    row = slice(b * S, (b + 1) * S)
                    nc.tensor.matmul(PA[s][:, :].rearrange("p (a t) -> p a t", a=2), KQ[:, 0, b * S:b * S + P],
                                     KQ[:, :, row], start=True, stop=True)
                    nc.tensor.matmul(PB[s][:, 0:S].rearrange("p (a t) -> p a t", a=2), KQ[:, 0, b * S + P:(b + 1) * S],
                                     KQ[:, :, b * S + P:(b + 1) * S], start=True, stop=True).then_inc(kq_mm[s], 1)
                    for h in range(2):
                        for c in range(2):
                            u = 2 * h + c
                            last = nc.tensor.transpose(PC[s][:, u * P:(u + 1) * P],
                                                       VV[:, h, b * S + c * P:b * S + (c + 1) * P], ident)
                    last.then_inc(vt_mm[s], 1)

                def step(st, b, s, p, i):
                    at = i * 2 + p
                    U = [(h, c) for h in range(2) for c in range(2)]
                    cols = lambda u: slice(u * P, (u + 1) * P)
                    if st == "T0" or st[0] == "AT":
                        n = 0 if st == "T0" else st[1]
                        if n == 0:
                            pe.wait_ge(ah_done[s], i * 4 + 4)
                            pe.wait_ge(ap_done[s], i * 2 + 2)
                            pe.wait_ge(r_done[s], i * 2 + 2)
                            if p:
                                pe.wait_ge(yt_done[s], i * 2 + 1)
                        elif n == 1:
                            pe.wait_ge(z_done[s], at * NS + 1)
                        else:
                            pe.wait_ge(t_done[s], at * (NS - 1) + n - 1)
                        for u, (h, c) in enumerate(U):
                            last = nc.tensor.matmul(PA[s][:, cols(u)], Ah[b][:, h, c, :],
                                                    Tn[s][:, u, :] if n else lev[:, LEVELS, :], start=True, stop=True)
                        last.then_inc(at_mm[s], 1)
                    elif st[0] == "TZ":
                        n = st[1]
                        pe.wait_ge(z_done[s], at * NS + n + 1)
                        if n == 1:
                            pe.wait_ge(tt0_done[s], at + 1)
                        for u in range(4):
                            if n < LEVELS - 1:
                                nc.tensor.matmul(PB[s][:, cols(u)], Tt[s][:, u, :], Zn[s][:, u, :], start=True, stop=True)
                            last = nc.tensor.matmul(PC[s][:, cols(u)], Zn[s][:, u, :], Tt[s][:, u, :],
                                                    start=True, stop=True)
                        last.then_inc(tt_mm[s], 1)
                    elif st[0] == "W0":
                        c = st[1]
                        if c == 0:
                            pe.wait_ge(t_done[s], at * (NS - 1) + NS - 1)
                        else:
                            pe.wait_ge(r2_done[s], at + 1)
                        for h in range(2):
                            last = nc.tensor.matmul(PA[s][:, cols(h)], Tt[s][:, 2 * h + c, :], Rh[b][:, h, c, :],
                                                    start=True, stop=True)
                        last.then_inc(w0_mm[s], 1)
                    elif st[0] == "AW":
                        c = st[1]
                        pe.wait_ge(w0_done[s], at * 2 + c + 1)
                        for h in range(2):
                            a = AP1[b][:, h, 0, :] if c else AP0[b][:, h, 0, 0:P]
                            last = nc.tensor.matmul(PB[s][:, cols(h)], a, W[s][:, h, c, :], start=True, stop=True)
                        last.then_inc(aw_mm[s], 1)
                    elif st[0] == "CO":
                        c = st[1]
                        pe.wait_ge(rr_done[s], at * 2 + c + 1)
                        for h in range(2):
                            last = nc.tensor.matmul(PA[s][:, cols(2 + h)], Tt[s][:, 2 * h + c, :], rr[s][:, h, c, :],
                                                    start=True, stop=True)
                        last.then_inc(cor_mm[s], 1)
                    elif st[0] == "X":
                        pe.wait_ge(w_done[s], at * 2 + 1)
                        for h in range(2):
                            last = nc.tensor.matmul(PC[s][:, cols(h)], AP0[b][:, h, 0, P:S], W[s][:, h, 0, :],
                                                    start=True, stop=True)
                        last.then_inc(x_mm[s], 1)
                    elif st == "O":
                        pe.wait_ge(w_done[s], at * 2 + 2)
                        for h in range(2):
                            nc.tensor.matmul(PB[s][:, cols(2 * h)], AP0[b][:, h, 1, 0:P], W[s][:, h, 0, :],
                                             start=True, stop=True)
                            nc.tensor.matmul(PB[s][:, cols(2 * h + 1)], AP0[b][:, h, 1, P:S], W[s][:, h, 0, :],
                                             start=True, stop=False)
                            last = nc.tensor.matmul(PB[s][:, cols(2 * h + 1)], AP1[b][:, h, 1, :], W[s][:, h, 1, :],
                                                    start=False, stop=True)
                        last.then_inc(o_mm[s], 1)
                    elif st == "YT":
                        pe.wait_ge(yn_done[s], at + 1)
                        for u, (h, c) in enumerate(U):
                            last = nc.tensor.transpose(PA[s][:, cols(u)], y2[s][:, h, c, :], ident)
                        last.then_inc(yt_mm[s], 1)

                for n_, j in enumerate(FIRST):
                    job(j, n_ % 2, n_ // 2, 0, 0)

                def head(i, jobs, base):
                    walk(jobs, base, lambda st, b, s, p: step(st, b, s, p, i),
                         lambda j, r, m: job(j, r, m, i if j[0] in "ZO" else i + 1, base), lambda b: group(b, i))
                with pe.Fori(0, HK - 1) as i:
                    head(i, FULL, RING0 + i * RING)
                head(HK - 1, LASTJ, RING0 + (HK - 1) * RING)

        attention.close()
        experts(nc, stack, dict(locals()))


def experts(nc, stack, v):
    f32, i32 = mybir.dt.float32, mybir.dt.int32
    ALU, ACT, AX = mybir.AluOpType, mybir.ActivationFunctionType, mybir.AxisListType
    ds = bass.ds
    sb, sem, two = v["sb"], v["sem"], v["two"]
    acc, xT, cst, ident = v["acc"], v["xT"], v["cst"], v["ident"]
    eps_l = v["eps_l"]
    PG, PU, PY, PX = v["PA"], v["PB"], v["PJ"], v["PC"]
    ids, ctx_in, Wr, Wg, Wu, Wd, out = (v[n] for n in ("ids", "ctx_in", "Wr", "Wg", "Wu", "Wd", "out"))

    id_i, id_f = sb("id_i", [P, NT], i32), sb("id_f", [P, NT])
    who = sb("who", [P, NT])
    me = sb("me", [P, E1, NT])
    wr = sb("wr", [P, KT, E2])
    wx = [sb(f"wx{q}", [P, KT, F]) for q in range(2)]
    wt = [sb(f"wt{q}", [P, KT, F]) for q in range(2)]
    wg = [sb(f"wg{q}", [P, KT, F]) for q in range(2)]
    wu = [sb(f"wu{q}", [P, KT, F]) for q in range(2)]
    wd = [sb(f"wd{q}", [P, KT, F]) for q in range(2)]
    sg = [sb(f"sg{r}", [P, HALF]) for r in range(2)]
    hh = [sb(f"hh{r}", [P, KT, HALF]) for r in range(2)]
    st6, mv = sb("st6", [P, NT, 6]), sb("mv", [P, NT, 2])
    sd, ri = sb("sd", [P, NT]), sb("ri", [P, NT])
    lg = sb("lg", [P, NT, E2])
    pr, q1, q2, q3 = (sb(n, [P, NT, E2]) for n in ("pr", "q1", "q2", "q3"))
    m1, m2, m3 = (sb(n, [P, NT]) for n in ("m1", "m2", "m3"))
    credit = sb("credit", [P, 4])
    wk = sb("wk", [P, E2, NT])

    id_in, wr_in, x_in, gud_in = sem("id_in"), sem("wr_in"), two("x_in"), two("gud_in")
    id_chain = sem("id_chain")
    ln_chain, var_done, sd_done, ln_ready = sem("ln_chain"), sem("var_done"), sem("sd_done"), sem("ln_ready")
    xr_mm, xr_done = two("xr_mm"), two("xr_done")
    ct_mm, ct_done = sem("ct_mm"), sem("ct_done")
    gu_mm, sg_done, h_done, y_mm, y_acc = two("gu_mm"), two("sg_done"), two("h_done"), two("y_mm"), two("y_acc")
    gu2, sg2, h2, y2m, ya2 = two("gu2_mm"), two("sg2_done"), two("h2_done"), two("y2_mm"), two("y2_acc")
    r_mm, re_done, rt_chain, rt_done = sem("r_mm"), sem("re_done"), sem("rt_chain"), sem("rt_done")
    stored = sem("stored")
    X1 = (gu_mm, sg_done, h_done, y_mm, y_acc)
    X2 = (gu2, sg2, h2, y2m, ya2)
    STEP = [("g", 0), ("g", 1), ("g", 2), ("y", 0), ("g", 3), ("y", 1)]

    with nc.Block() as block:
        @block.sync
        def _(sp):
            sp.dma_start(id_i[:, :], ids.rearrange("b (c p) -> p (b c)", p=P), allow_slow_non_contiguous=True).then_inc(id_in, 16)
            sp.dma_start(wr[:, :, :], Wr.rearrange("(k p) n -> p k n", p=P)).then_inc(wr_in, 16)

            def load_x(e, q):
                sp.dma_start(wx[q][:, :, :], ctx_in[ds(e, 1), :, :].rearrange("o (k p) n -> p (o k) n", p=P)).then_inc(x_in[q], 16)

            def load_w(e, q):
                for to, of in ((wg, Wg), (wu, Wu), (wd, Wd)):
                    sp.dma_start(to[q][:, :, :], of[ds(e, 1), :, :].rearrange("o (k p) n -> p (o k) n", p=P)).then_inc(
                        gud_in[q], 16)

            for q in range(2):
                load_x(q, q)
            for q in range(2):
                load_w(q, q)
            for e in range(2, E1):
                sp.wait_ge(ct_mm, e - 1)
                load_x(e, e % 2)
            with sp.Fori(0, E2 // 2 - 1) as j:
                for q in range(2):
                    sp.wait_ge(y2m[1], j * 4 + (q + 1) * 2)
                    load_w(j * 2 + (2 + q), q)
            of = out.rearrange("b s d -> (b s) d").rearrange("(n p) d -> p n d", p=P)
            sp.wait_ge(ln_ready, 3 * NT)
            sp.dma_start(of, acc[:, :, :]).then_inc(stored, 16)
            sp.wait_ge(stored, 16)

        def expert_steps(e, q, run):
            for kind, k in STEP:
                run(kind, k, e, q)

        @block.scalar
        def _(act):
            def norm(n):
                act.wait_ge(var_done, n + 1)
                nc.scalar.activation(sd[:, :], mv[:, :, 1], ACT.Sqrt, bias=eps_l[:, :]).then_inc(sd_done, 1)

            def gate(sems):
                gu, sgd, hd, ym, ya = sems

                def run(kind, k, e, q):
                    if kind == "g":
                        act.wait_ge(gu[k % 2], e * 2 + k // 2 + 1)
                        nc.scalar.activation(sg[k % 2][:, :], PG[k % 2][:, :], ACT.Silu).then_inc(sgd[k % 2], 1)
                return run

            norm(0)
            for e in range(E1):
                act.wait_ge(ct_mm, e + 1)
                nc.scalar.copy(wt[e % 2][:, :, :].rearrange("p k n -> p (k n)"), PX[e % 2][:, :]).then_inc(ct_done, 1)
                expert_steps(e, e % 2, gate(X1))
            norm(1)
            act.wait_ge(rt_chain, 2)
            nc.scalar.activation(pr[:, :, :], pr[:, :, :], ACT.Exp).then_inc(re_done, 1)
            with act.Fori(0, E2 // 2) as j:
                for q in range(2):
                    expert_steps(j * 2 + q, q, gate(X2))
            norm(2)

        @block.vector
        def _(dve):
            cc = [0]

            def link(ins, s=ln_chain, c=cc):
                c[0] += 1
                ins.then_inc(s, 1)
                dve.wait_ge(s, c[0])

            def norm(n):
                for t in range(NT):
                    last = nc.vector.bn_stats(st6[:, t, :], acc[:, t, :])
                link(last)
                for t in range(NT):
                    last = nc.vector.bn_aggr(mv[:, t, :], st6[:, t, :])
                last.then_inc(var_done, 1)
                dve.wait_ge(sd_done, n + 1)
                link(nc.vector.reciprocal(ri[:, :], sd[:, :]))
                for t in range(NT):
                    nc.vector.tensor_scalar(acc[:, t, :], acc[:, t, :], mv[:, t, 0:1], ri[:, t:t + 1],
                                            ALU.subtract, ALU.mult).then_inc(ln_ready, 1)
                dve.wait_ge(ln_ready, (n + 1) * NT)

            def transposed(n):
                for q in range(KT * 2):
                    k, hf = q // 2, q % 2
                    dve.wait_ge(xr_mm[q % 2], n * 2 + q // 2 + 1)
                    nc.vector.tensor_copy(xT[:, k, hf * HALF:(hf + 1) * HALF], PY[q % 2][:, :]).then_inc(xr_done[q % 2], 1)

            def hidden(sems, weight, up):
                gu, sgd, hd, ym, ya = sems

                def run(kind, k, e, q):
                    if kind == "g":
                        dve.wait_ge(sgd[k % 2], e * 2 + k // 2 + 1)
                        nc.vector.tensor_tensor(hh[k // 2][:, k % 2, :], sg[k % 2][:, :], up[k % 2][:, :],
                                                ALU.mult).then_inc(hd[k % 2], 1)
                    else:
                        for r in range(2):
                            dve.wait_ge(ym[r], e * 2 + k + 1)
                            for n_ in range(2):
                                t = k * 4 + r * 2 + n_
                                last = nc.vector.scalar_tensor_tensor(
                                    acc[:, t, :], PY[r][:, n_ * D:(n_ + 1) * D], weight(e, q, t), acc[:, t, :],
                                    ALU.mult, ALU.add)
                            last.then_inc(ya[r], 1)
                return run

            dve.wait_ge(id_in, 16)
            ic = [0]
            ln_i = lambda ins: link(ins, id_chain, ic)
            ln_i(nc.vector.tensor_copy(id_f[:, :], id_i[:, :]))
            ln_i(nc.vector.tensor_scalar(who[:, :], id_f[:, :], float(12500 // E1), None, ALU.is_ge))
            for m in range(2, E1):
                ln_i(nc.vector.scalar_tensor_tensor(who[:, :], id_f[:, :], float(m * (12500 // E1)), who[:, :],
                                                    ALU.is_ge, ALU.add))
            for e in range(E1):
                ln_i(nc.vector.tensor_scalar(me[:, e, :], who[:, :], float(e), None, ALU.is_equal))
            for n, sems in enumerate((X1, X2)):
                for r in range(2):
                    nc.vector.memset(credit[:, 2 * n + r:2 * n + r + 1], 0.0).then_inc(sems[4][r], 1)

            norm(0)
            transposed(0)
            for e in range(E1):
                expert_steps(e, e % 2, hidden(X1, lambda e_, q, t: me[:, e_, t:t + 1], PG))
            for r in range(2):
                dve.wait_ge(y_acc[r], 1 + 2 * E1)
            norm(1)
            transposed(1)
            rc = [0]
            ln_r = lambda ins: link(ins, rt_chain, rc)
            dve.wait_ge(r_mm, 1)
            bc = lambda a: a.rearrange("p (n o) -> p n o", o=1).to_broadcast((P, NT, E2))
            lgp = PX[0][:, 0:NT * E2].rearrange("p (n e) -> p n e", e=E2)
            ln_r(nc.vector.tensor_reduce(m1[:, :], lgp, AX.X, ALU.max))
            ln_r(nc.vector.tensor_tensor(pr[:, :, :], lgp, bc(m1[:, :]), ALU.subtract))
            dve.wait_ge(re_done, 1)
            iota = cst[:, C_E8:C_END].rearrange("p (n e) -> p n e", e=E2)
            ln_r(nc.vector.tensor_copy(q1[:, :, :], pr[:, :, :]))
            for best in range(2):
                ln_r(nc.vector.tensor_reduce(m1[:, :], q1[:, :, :], AX.X, ALU.max))
                ln_r(nc.vector.tensor_tensor(q2[:, :, :], q1[:, :, :], bc(m1[:, :]), ALU.is_lt))
                ln_r(nc.vector.scalar_tensor_tensor(q2[:, :, :], q2[:, :, :], 100.0, iota, ALU.mult, ALU.add))
                ln_r(nc.vector.tensor_reduce(m2[:, :], q2[:, :, :], AX.X, ALU.min))
                ln_r(nc.vector.tensor_tensor(q2[:, :, :], iota, bc(m2[:, :]), ALU.is_equal))
                if best == 0:
                    ln_r(nc.vector.tensor_tensor(q3[:, :, :], q2[:, :, :], pr[:, :, :], ALU.mult))
                    ln_r(nc.vector.scalar_tensor_tensor(q1[:, :, :], q2[:, :, :], -4.0, q1[:, :, :],
                                                        ALU.mult, ALU.add))
                else:
                    ln_r(nc.vector.tensor_tensor(q2[:, :, :], q2[:, :, :], pr[:, :, :], ALU.mult))
                    ln_r(nc.vector.tensor_tensor(q3[:, :, :], q3[:, :, :], q2[:, :, :], ALU.add))
            ln_r(nc.vector.tensor_reduce(m2[:, :], q3[:, :, :], AX.X, ALU.add))
            ln_r(nc.vector.reciprocal(m3[:, :], m2[:, :]))
            ln_r(nc.vector.tensor_tensor(wk[:, :, :].rearrange("p e n -> p n e"), q3[:, :, :], bc(m3[:, :]), ALU.mult))
            with dve.Fori(0, E2 // 2) as j:
                for q in range(2):
                    expert_steps(j * 2 + q, q, hidden(X2, lambda e_, q_, t: wk[:, ds(e_, 1), t], PU))
            for r in range(2):
                dve.wait_ge(ya2[r], 1 + 2 * E2)
            norm(2)

        @block.tensor
        def _(pe):
            def transposed(n):
                for q in range(KT * 2):
                    k, hf = q // 2, q % 2
                    pe.wait_ge(ln_ready, n * NT + hf * 4 + 4)
                    if n * 2 + q // 2 > 0:
                        pe.wait_ge(xr_done[q % 2], n * 2 + q // 2)
                    if n:
                        for r in range(2):
                            pe.wait_ge(y_acc[r], 1 + 2 * E1)
                    for t in range(4):
                        last = nc.tensor.transpose(PY[q % 2][:, t * P:(t + 1) * P],
                                                   acc[:, hf * 4 + t, k * P:(k + 1) * P], ident)
                    last.then_inc(xr_mm[q % 2], 1)
                for r in range(2):
                    pe.wait_ge(xr_done[r], n * 2 + 2)

            def products(sems, gate_w, up_w, down_w, used):
                gu, sgd, hd, ym, ya = sems

                def run(kind, k, e, q):
                    if kind == "g":
                        hf, ft = k // 2, k % 2
                        if k >= 2:
                            pe.wait_ge(hd[k % 2], e * 2 + 1)
                        for to, w in ((PG, gate_w),) + (((PU, up_w),) if up_w else ()):
                            for kt in range(KT):
                                last = nc.tensor.matmul(to[k % 2][:, :], w[q][:, kt, ft * P:(ft + 1) * P],
                                                        xT[:, kt, hf * HALF:(hf + 1) * HALF],
                                                        start=(kt == 0), stop=(kt == KT - 1))
                        last.then_inc(gu[k % 2], 1)
                    else:
                        for r in range(2):
                            pe.wait_ge(hd[r], e * 2 + k + 1)
                        for r in range(2):
                            pe.wait_ge(ya[r], e * 2 + k + 1)
                            for n_ in range(2):
                                for ft in range(KT):
                                    t = r * 2 + n_
                                    last = nc.tensor.matmul(PY[r][:, n_ * D:(n_ + 1) * D],
                                                            hh[k][:, ft, t * P:(t + 1) * P], down_w[q][:, ft, :],
                                                            start=(ft == 0), stop=(ft == KT - 1))
                            last.then_inc(ym[r], 1)
                return run

            transposed(0)
            for e in range(E1):
                pe.wait_ge(x_in[e % 2], 16 * (e // 2 + 1))
                for a in range(KT):
                    for k in range(KT):
                        last = nc.tensor.transpose(PX[e % 2][:, k * F + a * P:k * F + (a + 1) * P],
                                                   wx[e % 2][:, a, k * P:(k + 1) * P], ident)
                last.then_inc(ct_mm, 1)
                pe.wait_ge(ct_done, e + 1)
                expert_steps(e, e % 2, products(X1, wt, None, wt, None))
            transposed(1)
            pe.wait_ge(wr_in, 16)
            for t in range(NT):
                for k in range(KT):
                    last = nc.tensor.matmul(PX[0][:, t * E2:(t + 1) * E2], xT[:, k, t * P:(t + 1) * P], wr[:, k, :],
                                            start=(k == 0), stop=(k == KT - 1))
            last.then_inc(r_mm, 1)
            with pe.Fori(0, E2 // 2) as j:
                for q in range(2):
                    pe.wait_ge(gud_in[q], j * 48 + 48)
                    expert_steps(j * 2 + q, q, products(X2, wg, wu, wd, None))


def kernel(**inputs):
    import concourse.bacc as bacc
    from concourse.bass_utils import run_bass_kernel_spmd

    nc = bacc.Bacc("TRN2", target_bir_lowering=False, num_devices=1)
    consts, levels = constants()
    names = ["x", "itok_BxS_13_99985", "ctx_2048", "L0_attn_cu_seqlens", "L0_attn_Wqkv", "L0_attn_Wz", "L0_attn_Wa",
             "L0_attn_Wb", "L0_attn_conv_w", "L0_attn_A_log", "L0_attn_dt_bias", "L0_attn_norm_w", "L0_attn_Wout",
             "L0_ffn_Wr", "L0_ffn_Wg", "L0_ffn_Wu", "L0_ffn_Wd"]
    arrays, args = {}, []
    for name in names:
        a = np.ascontiguousarray(inputs[name])
        arrays["in_" + name] = a
        args.append(nc.dram_tensor("in_" + name, a.shape, mybir.dt.from_np(a.dtype), kind="ExternalInput").ap())
    for name, a in (("consts", consts), ("levels", levels)):
        arrays[name] = a
        args.append(nc.dram_tensor(name, a.shape, mybir.dt.from_np(a.dtype), kind="ExternalInput").ap())
    args.append(nc.dram_tensor("g_rows", (HV, T), mybir.dt.float32, kind="Internal").ap())
    args.append(nc.dram_tensor("result", (B, S, D), mybir.dt.float32, kind="ExternalOutput").ap())
    build(nc, *args)
    got = run_bass_kernel_spmd(nc, [arrays], core_ids=[0])
    return got.results[0]["result"]
```

```python
import math
from contextlib import ExitStack

import concourse.bass as bass
import numpy as np
from concourse import mybir

P = 128
B, S, D = 4, 256, 256
T = B * S
NT = T // P
KT = D // P
HK, HV = 16, 32
TAPS = 4
E1, E2 = 4, 8
F = 256
HALF = T // 2
LEVELS = 7
NEG = -30000.0
QEPS, NEPS, LEPS = 1e-6, 1e-6, 1e-5
NJB = 4
NC = 5

STEPS = (["T0"] + [x for n in range(1, LEVELS) for x in (("AT", n), ("TZ", n))]
         + [("W0", 0), ("AW", 0), ("CO", 0), ("X", 1), ("W0", 1), ("AW", 1), ("CO", 1), "O", "YT", "SS"])
STAGES = {
    "C": [("project", "pe", 0), ("tap0", "act", 0), ("tap1", "dve", 1), ("tap2", "dve", 2), ("tap3", "dve", 3),
          ("silu", "act", 4)],
    "N": [("square", "pool", 0), ("sum", "pe", 1), ("rsqrt", "act", 1), ("scale", "pool", 2)],
    "Z": [("project", "pe", 0), ("silu", "act", 0)],
    "K0": [("mask", "pool", 0), ("exp", "act", 1), ("product", "pe", 1), ("decay0", "dve", 2), ("decay1", "dve", 3)],
    "K1": [("product", "pe", 0), ("decay", "dve", 1), ("diagonal", "pool", 2)],
    "V": [("transpose", "pe", 0), ("half", "act", 0), ("full", "act", 1)],
    "O": [("project", "pe", 0), ("add0", "dve", 1), ("add1", "dve", 2)],
}
DVE_COPIES = {(n, s) for n in range(1, LEVELS - 1) for s in range(2)}
C_JOBS = [("C", t, half) for t in range(4) for half in range(2)]
N_JOBS = [("N", t, half) for t in range(2) for half in range(2)]
Z_JOBS = [("Z", b, 0) for b in range(B)]
O_JOBS = [("O", b, c) for b in range(B) for c in range(2)]
PREPARE = {b: [(kind, b, 0) for kind in ("K0", "K1", "V")] for b in range(B)}
FIRST = C_JOBS + N_JOBS + PREPARE[0] + PREPARE[1]
BODY = ([(j, 0) for j in PREPARE[2] + PREPARE[3] + Z_JOBS] + [(j, 1) for j in C_JOBS + N_JOBS]
        + [(j, 1) for j in PREPARE[0] + PREPARE[1]] + [(j, 0) for j in O_JOBS])
SLOTS = [0, 2, 4, 3, 6, 8, 5, 7, 9, 10,
         12, 14, 16, 18, 20, 22, 24, 26, 28, 30, 31, 32,
         33, 35, 36, 37, 39, 40, 41, 42, 42, 43, 46, 46, 46, 46]


def arrange(jobs, slots):
    end = 2 * len(STEPS)
    table = sorted((min(slot + lag, end), n, k, name, engine) for n, (job, slot) in enumerate(zip(jobs, slots))
                   for k, (name, engine, lag) in enumerate(STAGES[job[0]]))
    turn = [n for _, n, _, _, engine in table if engine == "pe"]
    return [(slot, n, name, engine) for slot, n, _, name, engine in table], {n: k for k, n in enumerate(turn)}


C_M0, C_M1, C_SUF, C_PRE, C_ROW, C_COL, C_ID, C_ONE, C_E8, C_END = np.cumsum(
    [0, 256, 128, 128, 128, 256, 2, 128, 128, 64]).tolist()


def constants():
    p = np.arange(P)[:, None]
    i = np.arange(S)[None, :]
    f = i[:, :P]
    c = np.zeros((P, C_END), np.float32)
    c[:, C_M0:C_M1] = np.where(p <= i, 0.0, NEG)
    c[:, C_M1:C_SUF] = np.where(p <= f, 0.0, NEG)
    c[:, C_SUF:C_PRE] = np.where(p > f, -1.0, 0.0)
    c[:, C_PRE:C_ROW] = np.where(p <= f, 1.0, 0.0)
    c[:, C_ROW:C_COL] = i
    c[:, C_COL:C_ID] = p + P * np.arange(2)[None, :]
    c[:, C_ID:C_ONE] = p == f
    c[:, C_ONE:C_E8] = 1.0
    c[:, C_E8:C_END] = np.tile(np.arange(E2), NT)[None, :]
    same = [(p >> n) == (f >> n) for n in range(LEVELS + 1)]
    h = np.zeros((P, LEVELS + 2, P), np.float16)
    for n in range(LEVELS):
        h[:, n] = same[0].astype(int) + same[n].astype(int) - same[n + 1].astype(int)
    h[:, LEVELS] = same[0]
    h[:, LEVELS + 1] = h[:, 0].T
    return c, h


def build(nc, x, ids, ctx_in, cu, Wqkv, Wz, Wa, Wb, conv_w, A_log, dt_bias, norm_w, Wout,
          Wr, Wg, Wu, Wd, consts, levels, g_rows, out):
    f32, f16, i32 = mybir.dt.float32, mybir.dt.float16, mybir.dt.int32
    ALU, ACT, AX = mybir.AluOpType, mybir.ActivationFunctionType, mybir.AxisListType
    ds = bass.ds
    stack = ExitStack()
    with stack:
        def sb(name, shape, dt=f32):
            return stack.enter_context(nc.sbuf_tensor(name, shape, dt))

        attention = stack.enter_context(ExitStack())

        def own(name, shape, dt=f32):
            return attention.enter_context(nc.sbuf_tensor(name, shape, dt))

        def sem(name):
            return stack.enter_context(nc.semaphore(name))

        waits_passed = sem("waits_passed")

        def apart(engine):
            engine.sem_inc(waits_passed, 1)

        def two(name):
            return [sem(f"{name}{r}") for r in range(2)]

        cst = sb("cst", [P, C_END])
        acc = sb("acc", [P, NT, D])
        xT = sb("xT", [P, KT, T])
        eps_l = sb("eps_l", [P, 1])
        lev = own("lev", [P, LEVELS + 2, P], f16)
        ident, ones = cst[:, C_ID:C_ONE], cst[:, C_ONE:C_E8]
        wA = own("wA", [P, KT, 4, P])
        wZ = own("wZ", [P, KT, 2 * P])
        wO = own("wO", [P, 2, D])
        cw = own("cw", [P, 4, TAPS])
        Gb = own("Gb", [P, 2, T])
        nw = own("nw", [P, 1])
        wab = own("wab", [P, KT, 2 * HV])
        hb = own("hb", [P, 2, HV])
        cu_i = own("cu_i", [P, NC], i32)
        cu_f = own("cu_f", [P, NC])
        cnt = own("cnt", [P, 2, S])
        cntc = own("cntc", [P, 2])
        M0 = own("M0", [P, S])
        M1 = own("M1", [P, P])
        tmpm = own("tmpm", [P, S])
        cmask = own("cmask", [P, TAPS - 1, S])
        bad = own("bad", [P, 1])
        flag = own("flag", [P, 1], i32)
        u_ab = own("u_ab", [P, NT, 2 * HV])
        v_ab = own("v_ab", [P, NT, 2 * HV])
        w_ab = own("w_ab", [P, NT, 2 * HV])
        ea = own("ea", [P, HV])
        g_tok = own("g_tok", [P, 2, B, HV])
        G_tok = own("G_tok", [P, NT, HV])
        bias = own("bias", [P, NT, HV])
        bcur = own("bcur", [P, NT, 2])
        Grow = own("Grow", [HV, T])
        cv = [own(f"cv{r}", [P, 2, S]) for r in range(2)]
        ct_ = [own(f"ct{r}", [P, 2, S]) for r in range(2)]
        KQ = own("KQ", [P, 2, T])
        VV = own("VV", [P, 2, T])
        sq = [own(f"sq{r}", [P, HALF]) for r in range(2)]
        ln = [own(f"ln{r}", [P, HALF]) for r in range(2)]
        sz = own("sz", [P, NT, 2 * P])
        gm = [own(f"gm{r}", [P, 2, 3 * P]) for r in range(2)]
        Ex = [own(f"Ex{r}", [P, 2, 3 * P]) for r in range(2)]
        AP0 = [own(f"AP0_{b}", [P, 2, 2, S]) for b in range(B)]
        AP1 = [own(f"AP1_{b}", [P, 2, 2, P]) for b in range(B)]
        Ah = [own(f"Ah{b}", [P, 2, 2, P], f16) for b in range(B)]
        R = [own(f"R{b}", [P, 2, 2, P]) for b in range(B)]
        Rh = [own(f"Rh{b}", [P, 2, 2, P], f16) for b in range(B)]
        Tn = [own(f"Tn{r}", [P, 4, P], f16) for r in range(2)]
        Tt = [own(f"Tt{r}", [P, 4, P], f16) for r in range(2)]
        Zn = [own(f"Zn{r}", [P, 4, P], f16) for r in range(2)]
        W = [own(f"W{r}", [P, 2, 2, P]) for r in range(2)]
        rr = [own(f"rr{r}", [P, 2, 2, P], f16) for r in range(2)]
        y = [own(f"y{r}", [P, 2, 2, P]) for r in range(2)]
        y2 = [own(f"y2{r}", [P, 2, 2, P]) for r in range(2)]
        ss = [own(f"ss{r}", [P, 4]) for r in range(2)]
        sl = [own(f"sl{r}", [P, 4]) for r in range(2)]
        rs = [own(f"rs{b}", [P, 4]) for b in range(B)]
        yT = own("yT", [P, 2, T])
        eps_q = own("eps_q", [P, 1])
        eps_s = own("eps_s", [P, 1])
        eps_n = own("eps_n", [P, 1])

        PJ = [stack.enter_context(nc.psum_tensor(f"PJ{r}", [P, 512], f32)) for r in range(NJB)]
        PB, PC = ([stack.enter_context(nc.psum_tensor(f"{n}{r}", [P, 512], f32))
                   for r in range(2)] for n in ("PB", "PC"))
        PA = PJ[2:]

        in_x, in_c, in_l, in_s, in_e = sem("in_x"), sem("in_c"), sem("in_l"), sem("in_s"), sem("in_e")
        mask_chain, masks_done = sem("mask_chain"), sem("masks_done")
        eps_done = sem("eps_done")
        xt_mm, xt_done = two("xt_mm"), two("xt_done")
        ab_mm, ab_act, ab_chain, g_done = sem("ab_mm"), sem("ab_act"), sem("ab_chain"), sem("g_done")
        G_mm, G_done, Gt_mm, Gt_done, G_out = sem("G_mm"), sem("G_done"), sem("Gt_mm"), sem("Gt_done"), sem("G_out")
        wA_in, wZ_in, wO_in, cw_in, Gb_in = sem("wA_in"), sem("wZ_in"), sem("wO_in"), sem("cw_in"), sem("Gb_in")
        nw_in = in_e
        pj_full, pj_free = ([sem(f"{n}{r}") for r in range(NJB)] for n in ("pj_full", "pj_free"))
        tap_done, mix_done = two("tap_done"), two("mix_done")
        conv_chain, mask_used = two("conv_chain"), two("mask_used")
        sq_done, ln_done, rn_done, norm_done = two("sq_done"), two("ln_done"), two("rn_done"), two("norm_done")
        bcur_done = sem("bcur_done")
        acc_chain = [sem(f"acc_chain{b}") for b in range(B)]
        gm_done, e_done, r_done = two("gm_done"), two("e_done"), two("r_done")
        diag_done, ah_done, tt0_done = two("diag_done"), two("ah_done"), two("tt0_done")
        at_mm, z_done, tt_mm, t_done = two("at_mm"), two("z_done"), two("tt_mm"), two("t_done")
        tn_done = two("tn_done")
        w0_mm, w0_done, aw_mm, rr_done = two("w0_mm"), two("w0_done"), two("aw_mm"), two("rr_done")
        cor_mm, w_done, x_mm, r2_done = two("cor_mm"), two("w_done"), two("x_mm"), two("r2_done")
        o_mm, y_done, ysq_done, ss_done = two("o_mm"), two("y_done"), two("ysq_done"), two("ss_done")
        sl_done, rs_done, yt_mm, yt_done = two("sl_done"), two("rs_done"), two("yt_mm"), two("yt_done")

        with nc.Block() as block:
            @block.sync
            def _(sp):
                xf = x.rearrange("b s d -> (b s) d").rearrange("(n p) d -> p n d", p=P)
                sp.dma_start(acc[:, :, :], xf).then_inc(in_x, 16)
                sp.dma_start(cst[:, :], consts).then_inc(in_c, 16)
                sp.dma_start(lev[:, :, :], levels).then_inc(in_l, 16)
                sp.dma_start(cu_i[:, :], cu.rearrange("(o n) -> o n", o=1).to_broadcast((P, NC))).then_inc(in_s, 16)
                sp.wait_ge(Gt_done, NT)
                sp.dma_start(g_rows, Grow[:, :]).then_inc(G_out, 16)
                sp.wait_ge(G_out, 16)

            @block.scalar
            def _(act):
                act.dma_start(wab[:, :, 0:HV], Wa.rearrange("(k p) n -> p k n", p=P)).then_inc(in_e, 16)
                act.dma_start(wab[:, :, HV:], Wb.rearrange("(k p) n -> p k n", p=P)).then_inc(in_e, 16)
                act.dma_start(hb[:, 0, :], A_log.rearrange("(o n) -> o n", o=1).to_broadcast((P, HV))).then_inc(in_e, 16)
                act.dma_start(hb[:, 1, :], dt_bias.rearrange("(o n) -> o n", o=1).to_broadcast((P, HV))).then_inc(in_e, 16)
                act.dma_start(nw[:, :], norm_w.rearrange("(p o) -> p o", o=1)).then_inc(in_e, 16)
                act.wait_ge(in_e, 80)
                nc.scalar.activation(ea[:, :], hb[:, 0, :], ACT.Exp).then_inc(ab_act, 1)
                act.wait_ge(ab_chain, 4)
                nc.scalar.activation(w_ab[:, :, :], v_ab[:, :, :], ACT.Exp).then_inc(ab_act, 1)
                act.wait_ge(ab_act, 2)
                act.wait_ge(eps_done, 1)
                nc.scalar.activation(v_ab[:, :, :], w_ab[:, :, :], ACT.Ln, bias=ones[:, 0:1]).then_inc(ab_act, 1)

            @block.gpsimd
            def _(pool):
                nc.gpsimd.memset(eps_q[:, :], QEPS)
                nc.gpsimd.memset(eps_s[:, :], -0.5 * math.log(P))
                nc.gpsimd.memset(eps_l[:, :], LEPS)
                nc.gpsimd.memset(eps_n[:, :], NEPS).then_inc(eps_done, 1)

            @block.vector
            def _(dve):
                n = [0]

                def link(ins):
                    n[0] += 1
                    ins.then_inc(mask_chain, 1)
                    dve.wait_ge(mask_chain, n[0])

                dve.wait_ge(in_c, 16)
                dve.wait_ge(in_s, 16)
                link(nc.vector.tensor_copy(cu_f[:, :], cu_i[:, :]))
                row = cst[:, C_ROW:C_COL]
                link(nc.vector.tensor_scalar(cnt[:, 1, :], row, cu_f[:, 1:2], None, ALU.is_ge))
                for m in (2, 3):
                    link(nc.vector.scalar_tensor_tensor(cnt[:, 1, :], row, cu_f[:, m:m + 1], cnt[:, 1, :],
                                                        ALU.is_ge, ALU.add))
                link(nc.vector.scalar_tensor_tensor(cnt[:, 0, :], row, cu_f[:, 0:1], cnt[:, 1, :],
                                                    ALU.is_ge, ALU.add))
                col = cst[:, C_COL:C_ID]
                link(nc.vector.tensor_scalar(cntc[:, :], col, cu_f[:, 0:1], None, ALU.is_ge))
                for m in (1, 2, 3):
                    link(nc.vector.scalar_tensor_tensor(cntc[:, :], col, cu_f[:, m:m + 1], cntc[:, :],
                                                        ALU.is_ge, ALU.add))
                link(nc.vector.tensor_scalar(tmpm[:, :], cnt[:, 0, :], cntc[:, 0:1], NEG, ALU.not_equal, ALU.mult))
                link(nc.vector.tensor_tensor(M0[:, :], tmpm[:, :], cst[:, C_M0:C_M1], ALU.add))
                link(nc.vector.tensor_scalar(tmpm[:, 0:P], cnt[:, 0, P:S], cntc[:, 1:2], NEG, ALU.not_equal, ALU.mult))
                link(nc.vector.tensor_tensor(M1[:, :], tmpm[:, 0:P], cst[:, C_M1:C_SUF], ALU.add))
                link(nc.vector.memset(cmask[:, :, :], 1.0))
                for s in range(1, TAPS):
                    link(nc.vector.tensor_tensor(cmask[:, s - 1, s:S], cnt[:, 1, s:S], cnt[:, 1, 0:S - s],
                                                 ALU.is_equal))
                link(nc.vector.tensor_reduce(bad[:, :], cmask[:, :, :], AX.XY, ALU.min))
                link(nc.vector.tensor_copy(flag[:, :], bad[:, :]))

                for q in range(KT * 2):
                    dve.wait_ge(xt_mm[q % 2], q // 2 + 1)
                    k, hf = q // 2, q % 2
                    nc.vector.tensor_copy(xT[:, k, hf * HALF:(hf + 1) * HALF], PJ[q % 2][:, :]).then_inc(xt_done[q % 2], 1)

                dve.wait_ge(in_e, 80)
                dve.wait_ge(ab_mm, 1)
                ab = PA[0][:, :].rearrange("p (n c) -> p n c", c=2 * HV)
                nc.vector.tensor_tensor(u_ab[:, :, 0:HV], ab[:, :, 0:HV],
                                        hb[:, 1:2, :].to_broadcast((P, NT, HV)), ALU.add).then_inc(ab_chain, 1)
                nc.vector.tensor_scalar(u_ab[:, :, HV:], ab[:, :, HV:], -1.0, None, ALU.mult).then_inc(ab_chain, 1)
                dve.wait_ge(ab_chain, 2)
                nc.vector.tensor_scalar(v_ab[:, :, :], u_ab[:, :, :], -1.0, None, ALU.mult).then_inc(ab_chain, 1)
                dve.wait_ge(ab_chain, 3)
                nc.vector.tensor_tensor(v_ab[:, :, :], v_ab[:, :, :], u_ab[:, :, :], ALU.min).then_inc(ab_chain, 1)
                dve.wait_ge(ab_act, 3)
                nc.vector.scalar_tensor_tensor(u_ab[:, :, :], u_ab[:, :, :], 0.0, v_ab[:, :, :],
                                               ALU.max, ALU.add).then_inc(ab_chain, 1)
                dve.wait_ge(ab_chain, 5)
                for c in range(2):
                    nc.vector.scalar_tensor_tensor(
                        g_tok[:, c, :, :], u_ab[:, c::2, 0:HV], -1.0,
                        ea[:, :].rearrange("p (o h) -> p o h", o=1).to_broadcast((P, B, HV)),
                        ALU.mult, ALU.mult).then_inc(g_done, 1)
                dve.wait_ge(G_mm, 1)
                for c in range(2):
                    nc.vector.tensor_copy(G_tok[:, c::2, :], PB[0][:, c * P:(c + 1) * P].rearrange(
                        "p (b h) -> p b h", b=B)).then_inc(G_done, 1)
                dve.wait_ge(G_done, 2)
                nc.vector.scalar_tensor_tensor(bias[:, :, :], u_ab[:, :, HV:], -1.0, G_tok[:, :, :],
                                               ALU.mult, ALU.subtract).then_inc(G_done, 1)
                for n_ in range(NT):
                    dve.wait_ge(Gt_mm, n_ + 1)
                    nc.vector.tensor_copy(Grow[:, n_ * P:(n_ + 1) * P], PC[n_ % 2][0:HV, 0:P]).then_inc(Gt_done, 1)

            @block.tensor
            def _(pe):
                pe.wait_ge(in_x, 16)
                pe.wait_ge(in_c, 16)
                for q in range(KT * 2):
                    k, hf = q // 2, q % 2
                    if q >= 2:
                        pe.wait_ge(xt_done[q % 2], q // 2)
                    for n_ in range(4):
                        last = nc.tensor.transpose(PJ[q % 2][:, n_ * P:(n_ + 1) * P],
                                                   acc[:, hf * 4 + n_, k * P:(k + 1) * P], ident)
                    last.then_inc(xt_mm[q % 2], 1)
                pe.wait_ge(in_e, 80)
                for r in range(2):
                    pe.wait_ge(xt_done[r], 2)
                for n_ in range(NT):
                    for k in range(KT):
                        last = nc.tensor.matmul(PA[0][:, n_ * 2 * HV:(n_ + 1) * 2 * HV], xT[:, k, n_ * P:(n_ + 1) * P],
                                                wab[:, k, :], start=(k == 0), stop=(k == KT - 1))
                last.then_inc(ab_mm, 1)
                pe.wait_ge(g_done, 2)
                for c, tri in ((0, C_SUF), (1, C_PRE)):
                    last = nc.tensor.matmul(PB[0][:, c * P:(c + 1) * P], cst[:, tri:tri + P],
                                            g_tok[:, c, :, :].rearrange("p b h -> p (b h)"), start=True, stop=True)
                last.then_inc(G_mm, 1)
                pe.wait_ge(G_done, 2)
                for n_ in range(NT):
                    if n_ >= 2:
                        pe.wait_ge(Gt_done, n_ - 1)
                    nc.tensor.transpose(PC[n_ % 2][0:HV, 0:P], G_tok[:, n_, :], ident).then_inc(Gt_mm, 1)

        LN_EXP = "natural_log_exp_and_others"
        NS = LEVELS
        RING = len(BODY) // NJB

        def bank(number, i):
            return number % NJB, number // NJB + i * RING

        FIRST_TABLE, FIRST_TURN = arrange(FIRST, [2 * n for n in range(len(FIRST))])
        TABLES = []
        for last_ in (False, True):
            kept = [(j, ahead, slot) for (j, ahead), slot in zip(BODY, SLOTS, strict=True) if not (ahead and last_)]
            jobs_ = [j for j, _, _ in kept]
            table_, turn_ = arrange(jobs_, [slot for _, _, slot in kept])
            TABLES.append((jobs_, [ahead for _, ahead, _ in kept], table_,
                           {n: k + len(FIRST) for n, k in turn_.items()}))

        def place(job, last):
            jobs, ahead, _, turn = TABLES[last]
            return turn[next(n for n, j in enumerate(jobs) if j == job and not ahead[n])]

        def walk(i, last, me, each_set, stage):
            jobs, ahead, table, turn = TABLES[last]
            for slot in range(2 * len(STEPS) + 1):
                if slot < 2 * len(STEPS):
                    p, n = divmod(slot, len(STEPS))
                    for s in range(2):
                        each_set(STEPS[n], 2 * p + s, s, p)
                for at, n, name, engine in table:
                    if at == slot and engine == me:
                        stage(jobs[n], name, *bank(turn[n], i), i + ahead[n])

        def walk_first(me, stage):
            for _, n, name, engine in FIRST_TABLE:
                if engine == me:
                    stage(FIRST[n], name, *bank(FIRST_TURN[n], 0), 0)

        def first(i):
            return isinstance(i, int) and i == 0

        with nc.Block() as block:
            @block.sync
            def _(sp):
                def load_A(i):
                    v = lambda a: a.rearrange("(k p) n -> p k n", p=P)
                    q_cols = Wqkv[:, ds(i * P, P)]
                    k_cols = Wqkv[:, ds(i * P + HK * P, P)]
                    v_cols = Wqkv[:, ds(i * 2 * P + 2 * HK * P, 2 * P)]
                    sp.dma_start(wA[:, :, 0, :], v(k_cols)).then_inc(wA_in, 16)
                    sp.dma_start(wA[:, :, 1, :], v(q_cols)).then_inc(wA_in, 16)
                    sp.dma_start(wA[:, :, 2:4, :].rearrange("p k a n -> p k (a n)"), v(v_cols)).then_inc(wA_in, 16)
                    sp.dma_start(cw[:, 0, :], conv_w[ds(i * P + HK * P, P), :]).then_inc(cw_in, 16)
                    sp.dma_start(cw[:, 1, :], conv_w[ds(i * P, P), :]).then_inc(cw_in, 16)
                    sp.dma_start(cw[:, 2:4, :], conv_w[ds(i * 2 * P + 2 * HK * P, 2 * P), :].rearrange(
                        "(a p) n -> p a n", p=P)).then_inc(cw_in, 16)

                def load_G(i):
                    for h in range(2):
                        sp.dma_start(Gb[:, h, :], g_rows[ds(i * 2 + h, 1), :].to_broadcast((P, T))).then_inc(Gb_in, 16)

                def load_Z(i):
                    sp.dma_start(wZ[:, :, :], Wz[:, ds(i * 2 * P, 2 * P)].rearrange("(k p) n -> p k n", p=P)).then_inc(wZ_in, 16)

                def load_O(i):
                    sp.dma_start(wO[:, :, :], Wout[ds(i * 2 * P, 2 * P), :].rearrange("(a p) n -> p a n", p=P)).then_inc(wO_in, 16)

                load_A(0)
                load_G(0)
                load_Z(0)
                load_O(0)

                def head(i):
                    for r in range(2):
                        sp.wait_ge(mix_done[r], (i + 1) * 4)
                    apart(sp)
                    load_A(i + 1)
                    for s in range(2):
                        sp.wait_ge(gm_done[s], (i + 1) * 2)
                    apart(sp)
                    load_G(i + 1)
                    for jobs, load in ((Z_JOBS, load_Z), (O_JOBS, load_O)):
                        r, m = bank(max(place(j, False) for j in jobs), i)
                        sp.wait_ge(pj_full[r], m + 1)
                        apart(sp)
                        load(i + 1)

                with sp.Fori(0, HK - 1) as i:
                    head(i)

            @block.gpsimd
            def _(pool):
                def stage(j, name, r, m, i):
                    kind, t, hf = j
                    if kind == "N":
                        kq = KQ[:, t, hf * HALF:(hf + 1) * HALF]
                        if name == "square":
                            pool.wait_ge(mix_done[hf], i * 4 + t + 1)
                            if not first(i) or t:
                                pool.wait_ge(norm_done[hf], i * 2 + t)
                            nc.gpsimd.tensor_tensor(sq[hf][:, :], kq, kq, ALU.mult).then_inc(sq_done[hf], 1)
                        else:
                            pool.wait_ge(rn_done[hf], i * 2 + t + 1)
                            nc.gpsimd.tensor_tensor(kq, kq, ln[hf][:, :], ALU.mult).then_inc(norm_done[hf], 1)
                    elif kind == "K0":
                        masked_decays(t, i)
                    elif kind == "K1":
                        unit_diagonal(t, r, m, i)

                def masked_decays(b, i):
                    s, n = b % 2, b // 2
                    if b == 0:
                        if not first(i):
                            for q in range(2):
                                pool.wait_ge(e_done[q], i * 2)
                            apart(pool)
                        nc.gpsimd.tensor_copy(bcur[:, :, :], bias[:, :, ds(i * 2, 2)]).then_inc(bcur_done, 1)
                        pool.wait_ge(Gb_in, i * 32 + 32)
                    if not first(i) or n:
                        pool.wait_ge(e_done[s], i * 2 + n)
                    Gv = Gb[:, :, b * S:(b + 1) * S]
                    nc.gpsimd.tensor_tensor(gm[s][:, :, 0:S], Gv, M0[:, :].rearrange("p (o t) -> p o t", o=1)
                                            .to_broadcast((P, 2, S)), ALU.add)
                    nc.gpsimd.tensor_tensor(gm[s][:, :, S:], Gv[:, :, P:S], M1[:, :].rearrange("p (o t) -> p o t", o=1)
                                            .to_broadcast((P, 2, P)), ALU.add).then_inc(gm_done[s], 1)

                def unit_diagonal(b, r, m, i):
                    s, n = b % 2, b // 2
                    pool.wait_ge(pj_free[r], m + 1)
                    apart(pool)
                    for c, a in ((0, AP0[b][:, :, 0, 0:P]), (1, AP1[b][:, :, 0, :])):
                        nc.gpsimd.affine_select(out=a, in_=a, compare_op=ALU.not_equal, fill=1.0, base=0,
                                                pattern=[[0, 2], [1, P]], channel_multiplier=-1).then_inc(diag_done[s], 1)
                    pool.wait_ge(diag_done[s], i * 4 + n * 2 + 2)
                    apart(pool)
                    nc.gpsimd.tensor_copy(Ah[b][:, :, 0, :], AP0[b][:, :, 0, 0:P]).then_inc(ah_done[s], 1)
                    nc.gpsimd.tensor_copy(Ah[b][:, :, 1, :], AP1[b][:, :, 0, :]).then_inc(ah_done[s], 1)

                def step(st, b, s, p, i):
                    if st == "T0":
                        pool.wait_ge(ah_done[s], i * 4 + 2 * p + 2)
                        pool.wait_ge(at_mm[s], (i * 2 + p) * NS + 1)
                        nc.gpsimd.tensor_tensor(
                            Tt[s][:, :, :], Ah[b][:, :, :, :].rearrange("p a c t -> p (a c) t"),
                            lev[:, LEVELS + 1:LEVELS + 2, :].to_broadcast((P, 4, P)), ALU.mult).then_inc(tt0_done[s], 1)
                    elif st == "O":
                        pool.wait_ge(y_done[s], i * 2 + p + 1)
                        nc.gpsimd.tensor_tensor(y2[s][:, :, :, :], y[s][:, :, :, :], y[s][:, :, :, :],
                                                ALU.mult).then_inc(ysq_done[s], 1)

                walk_first("pool", stage)

                def head(i, last=False):
                    walk(i, last, "pool", lambda st, b, s, p: step(st, b, s, p, i), stage)
                with pool.Fori(0, HK - 1) as i:
                    head(i)
                head(HK - 1, last=True)

            @block.scalar
            def _(act):
                def silu_mix(j, r, m, i):
                    kind, ct, hf = j
                    act.wait_ge(pj_free[r], m + 1)
                    dst = (KQ[:, ct, :] if ct < 2 else VV[:, ct - 2, :])[:, hf * HALF:(hf + 1) * HALF]
                    nc.scalar.activation(dst, cv[hf][:, :, :].rearrange("p b t -> p (b t)"), ACT.Silu).then_inc(
                        mix_done[hf], 1)

                table = [None]

                def ln_exp():
                    if table[0] != LN_EXP:
                        nc.scalar.preload_act_table_set(LN_EXP)
                    table[0] = LN_EXP

                def stage(j, name, r, m, i):
                    kind, t, hf = j
                    if name == "tap0":
                        act.wait_ge(pj_full[r], m + 1)
                        act.wait_ge(cw_in, i * 48 + 48)
                        if not first(i) or t:
                            act.wait_ge(mix_done[hf], i * 4 + t)
                        nc.scalar.activation(cv[hf][:, :, :].rearrange("p b t -> p (b t)"), PJ[r][:, :], ACT.Copy,
                                             scale=cw[:, t, TAPS - 1:TAPS]).then_inc(tap_done[hf], 1)
                    elif kind == "C":
                        table[0] = None
                        act.wait_ge(pj_free[r], m + 1)
                        dst = (KQ[:, t, :] if t < 2 else VV[:, t - 2, :])[:, hf * HALF:(hf + 1) * HALF]
                        nc.scalar.activation(dst, cv[hf][:, :, :].rearrange("p b t -> p (b t)"), ACT.Silu).then_inc(
                            mix_done[hf], 1)
                    elif kind == "N":
                        ln_exp()
                        act.wait_ge(pj_full[r], m + 1)
                        if not first(i) or t:
                            act.wait_ge(norm_done[hf], i * 2 + t)
                        nc.scalar.activation(ln[hf][:, :], PJ[r][:, :], ACT.Ln, bias=eps_q[:, :]).then_inc(pj_free[r], 1)
                        act.wait_ge(pj_free[r], m + 1)
                        kw = {"bias": eps_s[:, :]} if t == 1 else {}
                        nc.scalar.activation(ln[hf][:, :], ln[hf][:, :], ACT.Exp, scale=-0.5, **kw).then_inc(rn_done[hf], 1)
                    elif kind == "Z":
                        table[0] = None
                        act.wait_ge(pj_full[r], m + 1)
                        nc.scalar.activation(sz[:, 2 * t:2 * t + 2, :].rearrange("p n d -> p (n d)"), PJ[r][:, :],
                                             ACT.Silu).then_inc(pj_free[r], 1)
                    elif kind == "K0":
                        decays(t, i)
                    elif name == "half":
                        act.wait_ge(pj_full[r], m + 1)
                        nc.scalar.copy(Rh[t][:, :, :, :].rearrange("p a c t -> p (a c t)"), PJ[r][:, :]).then_inc(
                            r_done[t % 2], 1)
                    elif name == "full":
                        nc.scalar.copy(R[t][:, :, :, :].rearrange("p a c t -> p (a c t)"), PJ[r][:, :]).then_inc(
                            pj_free[r], 1)

                def decays(b, i):
                    s, n = b % 2, b // 2
                    ln_exp()
                    if b == 0:
                        act.wait_ge(bcur_done, i + 1)
                    act.wait_ge(gm_done[s], i * 2 + n + 1)
                    if not first(i) or n:
                        act.wait_ge(ah_done[s], i * 4 + n * 2)
                    for h in range(2):
                        nc.scalar.activation(Ex[s][:, h, 0:S], gm[s][:, h, 0:S], ACT.Exp, bias=bcur[:, 2 * b, h:h + 1])
                        last = nc.scalar.activation(Ex[s][:, h, S:], gm[s][:, h, S:], ACT.Exp,
                                                    bias=bcur[:, 2 * b + 1, h:h + 1])
                    last.then_inc(e_done[s], 1)

                def step(st, b, s, p, i):
                    at = i * 2 + p
                    if st[0] == "TZ":
                        act.wait_ge(tt_mm[s], at * (LEVELS - 1) + st[1])
                        if st[1] < LEVELS - 1 and (st[1], s) not in DVE_COPIES:
                            nc.scalar.copy(Tn[s][:, :, :].rearrange("p u t -> p (u t)"), PB[s][:, :])
                        nc.scalar.copy(Tt[s][:, :, :].rearrange("p u t -> p (u t)"), PC[s][:, :]).then_inc(t_done[s], 1)
                    elif st[0] == "W0":
                        act.wait_ge(w0_mm[s], at * 2 + st[1] + 1)
                        nc.scalar.copy(W[s][:, :, st[1], :], PB[s][:, 0:2 * P].rearrange("p (h t) -> p h t", h=2)).then_inc(
                            w0_done[s], 1)
                    elif st == "SS":
                        ln_exp()
                        act.wait_ge(ss_done[s], at + 1)
                        nc.scalar.activation(sl[s][:, :], ss[s][:, :], ACT.Ln, bias=eps_n[:, :], scale=1.0 / P).then_inc(
                            sl_done[s], 1)
                        act.wait_ge(sl_done[s], at + 1)
                        nc.scalar.activation(rs[b][:, :], sl[s][:, :], ACT.Exp, scale=-0.5).then_inc(rs_done[s], 1)
                    elif st == "YT":
                        act.wait_ge(yt_mm[s], at + 1)
                        nc.scalar.activation(yT[:, :, b * S:(b + 1) * S],
                                             PB[s][:, :].rearrange("p (h t) -> p h t", h=2), ACT.Copy,
                                             scale=nw[:, 0:1]).then_inc(yt_done[s], 1)

                walk_first("act", stage)

                def head(i, last=False):
                    table[0] = None
                    walk(i, last, "act", lambda st, b, s, p: step(st, b, s, p, i), stage)
                with act.Fori(0, HK - 1) as i:
                    head(i)
                head(HK - 1, last=True)

            @block.vector
            def _(dve):
                unbroken = dve.value_load(flag[0:1, 0:1], min_val=0, max_val=1)
                def stage(j, name, r, m, i):
                    kind, t, hf = j
                    if kind == "C":
                        tap(int(name[3]), r, m, t, hf, i)
                    elif kind == "O":
                        h, at = int(name[3]), acc[:, 2 * t + hf, :]
                        if h == 0:
                            dve.wait_ge(pj_full[r], m + 1)
                            dve.wait_ge(rs_done[t % 2], i * 2 + t // 2 + 1)
                        else:
                            dve.wait_ge(acc_chain[t], i * 2 + hf + 1)
                        nc.vector.scalar_tensor_tensor(at, PJ[r][:, h * D:(h + 1) * D], rs[t][:, 2 * h + hf:2 * h + hf + 1],
                                                       at, ALU.mult, ALU.add).then_inc(
                            pj_free[r] if h else acc_chain[t], 1)
                    else:
                        s, n = t % 2, t // 2
                        dve.wait_ge(pj_full[r], m + 1)
                        dve.wait_ge(e_done[s], i * 2 + n + 1)
                        to, width, of = (AP1, P, S) if kind == "K1" else (AP0, S, 0)
                        for h in {"decay0": [0], "decay1": [1], "decay": [0, 1]}[name]:
                            last = nc.vector.tensor_tensor(
                                to[t][:, h, :, :], PJ[r][:, 0:2 * width].rearrange("p (a t) -> p a t", a=2),
                                Ex[s][:, h:h + 1, of:of + width].to_broadcast((P, 2, width)), ALU.mult)
                        if name != "decay0":
                            last.then_inc(pj_free[r], 1)

                def tap(s, r, m, t, hf, i):
                    n0 = (i * 4 + t) * 5
                    if s == 1:
                        dve.wait_ge(tap_done[hf], i * 4 + t + 1)
                    else:
                        dve.wait_ge(conv_chain[hf], n0 + (3 if s == 2 else 5))
                    apart(dve)
                    src = PJ[r][:, :].rearrange("p (b t) -> p b t", b=2)[:, :, 0:S - s]

                    def add(of):
                        return nc.vector.scalar_tensor_tensor(
                            cv[hf][:, :, s:S], of, cw[:, t, TAPS - 1 - s:TAPS - s], cv[hf][:, :, s:S],
                            ALU.mult, ALU.add)

                    out_sem, whole = (pj_free[r], 1) if s == TAPS - 1 else (conv_chain[hf], 4 - s)
                    with dve.If(unbroken):
                        add(src).then_inc(out_sem, whole)
                    with dve.Else():
                        masked = ct_[hf][:, :, s:S]
                        nc.vector.tensor_tensor(masked, src, cmask[:, s - 1:s, s:S].to_broadcast((P, 2, S - s)),
                                                ALU.mult).then_inc(mask_used[hf], 1)
                        dve.wait_ge(mask_used[hf], (i * 4 + t) * 3 + s)
                        add(masked).then_inc(out_sem, whole)

                def step(st, b, s, p, i, last):
                    at = i * 2 + p
                    four = lambda n: lev[:, n:n + 1, :].to_broadcast((P, 4, P))
                    if st == "T0" or st[0] == "AT":
                        n = 0 if st == "T0" else st[1]
                        dve.wait_ge(at_mm[s], at * NS + n + 1)
                        nc.vector.tensor_tensor((Zn if n else Tn)[s][:, :, :],
                                                PB[s][:, :].rearrange("p (u t) -> p u t", u=4), four(n),
                                                ALU.mult).then_inc(z_done[s], 1)
                    elif st[0] == "TZ" and (st[1], s) in DVE_COPIES:
                        dve.wait_ge(tt_mm[s], at * (NS - 1) + st[1])
                        nc.vector.tensor_copy(Tn[s][:, :, :].rearrange("p u t -> p (u t)"), PB[s][:, :]).then_inc(
                            tn_done[s], 1)
                    elif st[0] == "AW":
                        dve.wait_ge(aw_mm[s], at * 2 + st[1] + 1)
                        nc.vector.tensor_tensor(rr[s][:, :, st[1], :], R[b][:, :, st[1], :],
                                                PC[s][:, 0:S].rearrange("p (h t) -> p h t", h=2),
                                                ALU.subtract).then_inc(rr_done[s], 1)
                    elif st[0] == "CO":
                        dve.wait_ge(cor_mm[s], at * 2 + st[1] + 1)
                        nc.vector.tensor_tensor(W[s][:, :, st[1], :], W[s][:, :, st[1], :],
                                                PB[s][:, S:].rearrange("p (h t) -> p h t", h=2),
                                                ALU.add).then_inc(w_done[s], 1)
                    elif st[0] == "X":
                        dve.wait_ge(x_mm[s], at + 1)
                        cross = PC[s][:, S:].rearrange("p (h t) -> p h t", h=2)
                        nc.vector.tensor_tensor(Rh[b][:, :, 1, :], R[b][:, :, 1, :], cross, ALU.subtract)
                        nc.vector.tensor_tensor(R[b][:, :, 1, :], R[b][:, :, 1, :], cross,
                                                ALU.subtract).then_inc(r2_done[s], 1)
                    elif st == "O":
                        dve.wait_ge(o_mm[s], at + 1)
                        r, m = bank(place(Z_JOBS[b], last), i)
                        dve.wait_ge(pj_free[r], m + 1)
                        nc.vector.tensor_tensor(
                            y[s][:, :, :, :], PC[s][:, :].rearrange("p (h c t) -> p h c t", h=2, c=2),
                            sz[:, 2 * b:2 * b + 2, :].rearrange("p c (h t) -> p h c t", h=2),
                            ALU.mult).then_inc(y_done[s], 1)
                    elif st == "SS":
                        dve.wait_ge(ysq_done[s], at + 1)
                        nc.vector.tensor_reduce(ss[s][:, :], y2[s][:, :, :, :].rearrange("p a c t -> p (a c) t"),
                                                AX.X, ALU.add).then_inc(ss_done[s], 1)

                walk_first("dve", stage)

                def head(i, last=False):
                    walk(i, last, "dve", lambda st, b, s, p: step(st, b, s, p, i, last), stage)
                with dve.Fori(0, HK - 1) as i:
                    head(i)
                head(HK - 1, last=True)

            @block.tensor
            def _(pe):
                def stage(j, name, r, m, i):
                    kind, t, hf = j
                    if not (isinstance(m, int) and m == 0):
                        pe.wait_ge(pj_free[r], m)
                    if kind == "C":
                        pe.wait_ge(wA_in, i * 48 + 48)
                        for k in range(KT):
                            last = nc.tensor.matmul(PJ[r][:, :], wA[:, k, t, :], xT[:, k, hf * HALF:(hf + 1) * HALF],
                                                    start=(k == 0), stop=(k == KT - 1))
                        last.then_inc(pj_full[r], 1)
                    elif kind == "N":
                        pe.wait_ge(sq_done[hf], i * 2 + t + 1)
                        nc.tensor.matmul(PJ[r][:, :], ones, sq[hf][:, :], start=True, stop=True).then_inc(pj_full[r], 1)
                    elif kind == "Z":
                        pe.wait_ge(wZ_in, i * 16 + 16)
                        for n_ in range(2):
                            for k in range(KT):
                                tok = (2 * t + n_) * P
                                last = nc.tensor.matmul(PJ[r][:, n_ * 2 * P:(n_ + 1) * 2 * P], xT[:, k, tok:tok + P],
                                                        wZ[:, k, :], start=(k == 0), stop=(k == KT - 1))
                        last.then_inc(pj_full[r], 1)
                    elif kind in ("K0", "K1"):
                        pe.wait_ge(norm_done[t // 2], i * 2 + 2)
                        j0, width = t * S + P * int(kind[1]), (S, P)[int(kind[1])]
                        nc.tensor.matmul(PJ[r][:, 0:2 * width].rearrange("p (a t) -> p a t", a=2), KQ[:, 0, j0:j0 + P],
                                         KQ[:, :, j0:j0 + width], start=True, stop=True).then_inc(pj_full[r], 1)
                    elif kind == "V":
                        pe.wait_ge(mix_done[t // 2], i * 4 + 4)
                        for h in range(2):
                            for c in range(2):
                                u, tok = 2 * h + c, t * S + c * P
                                last = nc.tensor.transpose(PJ[r][:, u * P:(u + 1) * P], VV[:, h, tok:tok + P], ident)
                        last.then_inc(pj_full[r], 1)
                    elif kind == "O":
                        pe.wait_ge(wO_in, i * 16 + 16)
                        pe.wait_ge(yt_done[t % 2], i * 2 + t // 2 + 1)
                        tok = (2 * t + hf) * P
                        for h in range(2):
                            last = nc.tensor.matmul(PJ[r][:, h * D:(h + 1) * D], yT[:, h, tok:tok + P],
                                                    wO[:, h, :], start=True, stop=True)
                        last.then_inc(pj_full[r], 1)

                def step(st, b, s, p, i):
                    at = i * 2 + p
                    U = [(h, c) for h in range(2) for c in range(2)]
                    cols = lambda u: slice(u * P, (u + 1) * P)
                    if st == "T0" or st[0] == "AT":
                        n = 0 if st == "T0" else st[1]
                        if n == 0:
                            pe.wait_ge(ah_done[s], i * 4 + 2 * p + 2)
                            if p:
                                pe.wait_ge(yt_done[s], i * 2 + 1)
                        elif n == 1:
                            pe.wait_ge(z_done[s], at * NS + 1)
                        else:
                            pe.wait_ge(t_done[s], at * (NS - 1) + n - 1)
                            if (n - 1, s) in DVE_COPIES:
                                per = [q for q, s_ in sorted(DVE_COPIES) if s_ == s]
                                pe.wait_ge(tn_done[s], at * len(per) + per.index(n - 1) + 1)
                        for u, (h, c) in enumerate(U):
                            last = nc.tensor.matmul(PB[s][:, cols(u)], Ah[b][:, h, c, :],
                                                    Tn[s][:, u, :] if n else lev[:, LEVELS, :], start=True, stop=True)
                        last.then_inc(at_mm[s], 1)
                    elif st[0] == "TZ":
                        n = st[1]
                        pe.wait_ge(z_done[s], at * NS + n + 1)
                        if n == 1:
                            pe.wait_ge(tt0_done[s], at + 1)
                        for u in range(4):
                            if n < LEVELS - 1:
                                nc.tensor.matmul(PB[s][:, cols(u)], Tt[s][:, u, :], Zn[s][:, u, :], start=True, stop=True)
                            last = nc.tensor.matmul(PC[s][:, cols(u)], Zn[s][:, u, :], Tt[s][:, u, :],
                                                    start=True, stop=True)
                        last.then_inc(tt_mm[s], 1)
                    elif st[0] == "W0":
                        c = st[1]
                        if c == 0:
                            pe.wait_ge(t_done[s], at * (NS - 1) + NS - 1)
                            pe.wait_ge(r_done[s], at + 1)
                        else:
                            pe.wait_ge(r2_done[s], at + 1)
                        for h in range(2):
                            last = nc.tensor.matmul(PB[s][:, cols(h)], Tt[s][:, 2 * h + c, :], Rh[b][:, h, c, :],
                                                    start=True, stop=True)
                        last.then_inc(w0_mm[s], 1)
                    elif st[0] == "AW":
                        c = st[1]
                        pe.wait_ge(w0_done[s], at * 2 + c + 1)
                        for h in range(2):
                            a = AP1[b][:, h, 0, :] if c else AP0[b][:, h, 0, 0:P]
                            last = nc.tensor.matmul(PC[s][:, cols(h)], a, W[s][:, h, c, :], start=True, stop=True)
                        last.then_inc(aw_mm[s], 1)
                    elif st[0] == "CO":
                        c = st[1]
                        pe.wait_ge(rr_done[s], at * 2 + c + 1)
                        for h in range(2):
                            last = nc.tensor.matmul(PB[s][:, cols(2 + h)], Tt[s][:, 2 * h + c, :], rr[s][:, h, c, :],
                                                    start=True, stop=True)
                        last.then_inc(cor_mm[s], 1)
                    elif st[0] == "X":
                        pe.wait_ge(w_done[s], at * 2 + 1)
                        for h in range(2):
                            last = nc.tensor.matmul(PC[s][:, cols(2 + h)], AP0[b][:, h, 0, P:S], W[s][:, h, 0, :],
                                                    start=True, stop=True)
                        last.then_inc(x_mm[s], 1)
                    elif st == "O":
                        pe.wait_ge(w_done[s], at * 2 + 2)
                        for h in range(2):
                            nc.tensor.matmul(PC[s][:, cols(2 * h)], AP0[b][:, h, 1, 0:P], W[s][:, h, 0, :],
                                             start=True, stop=True)
                            nc.tensor.matmul(PC[s][:, cols(2 * h + 1)], AP0[b][:, h, 1, P:S], W[s][:, h, 0, :],
                                             start=True, stop=False)
                            last = nc.tensor.matmul(PC[s][:, cols(2 * h + 1)], AP1[b][:, h, 1, :], W[s][:, h, 1, :],
                                                    start=False, stop=True)
                        last.then_inc(o_mm[s], 1)
                    elif st == "YT":
                        pe.wait_ge(y_done[s], at + 1)
                        for u, (h, c) in enumerate(U):
                            last = nc.tensor.transpose(PB[s][:, cols(u)], y[s][:, h, c, :], ident)
                        last.then_inc(yt_mm[s], 1)

                walk_first("pe", stage)

                def head(i, last=False):
                    walk(i, last, "pe", lambda st, b, s, p: step(st, b, s, p, i), stage)
                with pe.Fori(0, HK - 1) as i:
                    head(i)
                head(HK - 1, last=True)

        attention.close()
        experts(nc, stack, dict(locals()))


def experts(nc, stack, v):
    f32, i32 = mybir.dt.float32, mybir.dt.int32
    ALU, ACT, AX = mybir.AluOpType, mybir.ActivationFunctionType, mybir.AxisListType
    ds = bass.ds
    sb, sem, two = v["sb"], v["sem"], v["two"]
    acc, xT, cst, ident = v["acc"], v["xT"], v["cst"], v["ident"]
    eps_l = v["eps_l"]
    PG, PU, PY, PX = v["PA"], v["PB"], v["PJ"], v["PC"]
    ids, ctx_in, Wr, Wg, Wu, Wd, out = (v[n] for n in ("ids", "ctx_in", "Wr", "Wg", "Wu", "Wd", "out"))

    id_i, id_f = sb("id_i", [P, NT], i32), sb("id_f", [P, NT])
    who = sb("who", [P, NT])
    me = sb("me", [P, E1, NT])
    wr = sb("wr", [P, KT, E2])
    wx = [sb(f"wx{q}", [P, KT, F]) for q in range(2)]
    wt = [sb(f"wt{q}", [P, KT, F]) for q in range(2)]
    wg = [sb(f"wg{q}", [P, KT, F]) for q in range(2)]
    wu = [sb(f"wu{q}", [P, KT, F]) for q in range(2)]
    wd = [sb(f"wd{q}", [P, KT, F]) for q in range(2)]
    sg = [sb(f"sg{r}", [P, HALF]) for r in range(2)]
    hh = [sb(f"hh{r}", [P, KT, HALF]) for r in range(2)]
    st6, mv = sb("st6", [P, NT, 6]), sb("mv", [P, NT, 2])
    sd, ri = sb("sd", [P, NT]), sb("ri", [P, NT])
    lg = sb("lg", [P, NT, E2])
    pr, q1, q2, q3 = (sb(n, [P, NT, E2]) for n in ("pr", "q1", "q2", "q3"))
    m1, m2, m3 = (sb(n, [P, NT]) for n in ("m1", "m2", "m3"))
    credit = sb("credit", [P, 4])
    wk = sb("wk", [P, E2, NT])

    id_in, wr_in, x_in, gud_in = sem("id_in"), sem("wr_in"), two("x_in"), two("gud_in")
    id_chain = sem("id_chain")
    ln_chain, var_done, sd_done, ln_ready = sem("ln_chain"), sem("var_done"), sem("sd_done"), sem("ln_ready")
    xr_mm, xr_done = two("xr_mm"), two("xr_done")
    ct_mm, ct_done = sem("ct_mm"), sem("ct_done")
    gu_mm, sg_done, h_done, y_mm, y_acc = two("gu_mm"), two("sg_done"), two("h_done"), two("y_mm"), two("y_acc")
    gu2, sg2, h2, y2m, ya2 = two("gu2_mm"), two("sg2_done"), two("h2_done"), two("y2_mm"), two("y2_acc")
    r_mm, re_done, rt_chain, rt_done = sem("r_mm"), sem("re_done"), sem("rt_chain"), sem("rt_done")
    stored = sem("stored")
    X1 = (gu_mm, sg_done, h_done, y_mm, y_acc)
    X2 = (gu2, sg2, h2, y2m, ya2)
    STEP = [("g", 0), ("g", 1), ("g", 2), ("y", 0), ("g", 3), ("y", 1)]

    with nc.Block() as block:
        @block.sync
        def _(sp):
            sp.dma_start(id_i[:, :], ids.rearrange("b (c p) -> p (b c)", p=P), allow_slow_non_contiguous=True).then_inc(id_in, 16)
            sp.dma_start(wr[:, :, :], Wr.rearrange("(k p) n -> p k n", p=P)).then_inc(wr_in, 16)

            def load_x(e, q):
                sp.dma_start(wx[q][:, :, :], ctx_in[ds(e, 1), :, :].rearrange("o (k p) n -> p (o k) n", p=P)).then_inc(x_in[q], 16)

            def load_w(e, q):
                for to, of in ((wg, Wg), (wu, Wu), (wd, Wd)):
                    sp.dma_start(to[q][:, :, :], of[ds(e, 1), :, :].rearrange("o (k p) n -> p (o k) n", p=P)).then_inc(
                        gud_in[q], 16)

            for q in range(2):
                load_x(q, q)
            for q in range(2):
                load_w(q, q)
            for e in range(2, E1):
                sp.wait_ge(ct_mm, e - 1)
                load_x(e, e % 2)
            with sp.Fori(0, E2 // 2 - 1) as j:
                for q in range(2):
                    sp.wait_ge(y2m[1], j * 4 + (q + 1) * 2)
                    load_w(j * 2 + (2 + q), q)
            of = out.rearrange("b s d -> (b s) d").rearrange("(n p) d -> p n d", p=P)
            sp.wait_ge(ln_ready, 3 * NT)
            sp.dma_start(of, acc[:, :, :]).then_inc(stored, 16)
            sp.wait_ge(stored, 16)

        def expert_steps(e, q, run):
            for kind, k in STEP:
                run(kind, k, e, q)

        @block.scalar
        def _(act):
            def norm(n):
                act.wait_ge(var_done, n + 1)
                nc.scalar.activation(sd[:, :], mv[:, :, 1], ACT.Sqrt, bias=eps_l[:, :]).then_inc(sd_done, 1)

            def gate(sems):
                gu, sgd, hd, ym, ya = sems

                def run(kind, k, e, q):
                    if kind == "g":
                        act.wait_ge(gu[k % 2], e * 2 + k // 2 + 1)
                        nc.scalar.activation(sg[k % 2][:, :], PG[k % 2][:, :], ACT.Silu).then_inc(sgd[k % 2], 1)
                return run

            norm(0)
            for e in range(E1):
                act.wait_ge(ct_mm, e + 1)
                nc.scalar.copy(wt[e % 2][:, :, :].rearrange("p k n -> p (k n)"), PX[e % 2][:, :]).then_inc(ct_done, 1)
                expert_steps(e, e % 2, gate(X1))
            norm(1)
            act.wait_ge(rt_chain, 2)
            nc.scalar.activation(pr[:, :, :], pr[:, :, :], ACT.Exp).then_inc(re_done, 1)
            with act.Fori(0, E2 // 2) as j:
                for q in range(2):
                    expert_steps(j * 2 + q, q, gate(X2))
            norm(2)

        @block.vector
        def _(dve):
            cc = [0]

            def link(ins, s=ln_chain, c=cc):
                c[0] += 1
                ins.then_inc(s, 1)
                dve.wait_ge(s, c[0])

            def norm(n):
                for t in range(NT):
                    last = nc.vector.bn_stats(st6[:, t, :], acc[:, t, :])
                link(last)
                for t in range(NT):
                    last = nc.vector.bn_aggr(mv[:, t, :], st6[:, t, :])
                last.then_inc(var_done, 1)
                dve.wait_ge(sd_done, n + 1)
                link(nc.vector.reciprocal(ri[:, :], sd[:, :]))
                for t in range(NT):
                    nc.vector.tensor_scalar(acc[:, t, :], acc[:, t, :], mv[:, t, 0:1], ri[:, t:t + 1],
                                            ALU.subtract, ALU.mult).then_inc(ln_ready, 1)
                dve.wait_ge(ln_ready, (n + 1) * NT)

            def transposed(n):
                for q in range(KT * 2):
                    k, hf = q // 2, q % 2
                    dve.wait_ge(xr_mm[q % 2], n * 2 + q // 2 + 1)
                    nc.vector.tensor_copy(xT[:, k, hf * HALF:(hf + 1) * HALF], PY[q % 2][:, :]).then_inc(xr_done[q % 2], 1)

            def hidden(sems, weight, up):
                gu, sgd, hd, ym, ya = sems

                def run(kind, k, e, q):
                    if kind == "g":
                        dve.wait_ge(sgd[k % 2], e * 2 + k // 2 + 1)
                        nc.vector.tensor_tensor(hh[k // 2][:, k % 2, :], sg[k % 2][:, :], up[k % 2][:, :],
                                                ALU.mult).then_inc(hd[k % 2], 1)
                    else:
                        for r in range(2):
                            dve.wait_ge(ym[r], e * 2 + k + 1)
                            for n_ in range(2):
                                t = k * 4 + r * 2 + n_
                                last = nc.vector.scalar_tensor_tensor(
                                    acc[:, t, :], PY[r][:, n_ * D:(n_ + 1) * D], weight(e, q, t), acc[:, t, :],
                                    ALU.mult, ALU.add)
                            last.then_inc(ya[r], 1)
                return run

            dve.wait_ge(id_in, 16)
            ic = [0]
            ln_i = lambda ins: link(ins, id_chain, ic)
            ln_i(nc.vector.tensor_copy(id_f[:, :], id_i[:, :]))
            ln_i(nc.vector.tensor_scalar(who[:, :], id_f[:, :], float(12500 // E1), None, ALU.is_ge))
            for m in range(2, E1):
                ln_i(nc.vector.scalar_tensor_tensor(who[:, :], id_f[:, :], float(m * (12500 // E1)), who[:, :],
                                                    ALU.is_ge, ALU.add))
            for e in range(E1):
                ln_i(nc.vector.tensor_scalar(me[:, e, :], who[:, :], float(e), None, ALU.is_equal))
            for n, sems in enumerate((X1, X2)):
                for r in range(2):
                    nc.vector.memset(credit[:, 2 * n + r:2 * n + r + 1], 0.0).then_inc(sems[4][r], 1)

            norm(0)
            transposed(0)
            for e in range(E1):
                expert_steps(e, e % 2, hidden(X1, lambda e_, q, t: me[:, e_, t:t + 1], PG))
            for r in range(2):
                dve.wait_ge(y_acc[r], 1 + 2 * E1)
            norm(1)
            transposed(1)
            rc = [0]
            ln_r = lambda ins: link(ins, rt_chain, rc)
            dve.wait_ge(r_mm, 1)
            bc = lambda a: a.rearrange("p (n o) -> p n o", o=1).to_broadcast((P, NT, E2))
            lgp = PX[0][:, 0:NT * E2].rearrange("p (n e) -> p n e", e=E2)
            ln_r(nc.vector.tensor_reduce(m1[:, :], lgp, AX.X, ALU.max))
            ln_r(nc.vector.tensor_tensor(pr[:, :, :], lgp, bc(m1[:, :]), ALU.subtract))
            dve.wait_ge(re_done, 1)
            iota = cst[:, C_E8:C_END].rearrange("p (n e) -> p n e", e=E2)
            ln_r(nc.vector.tensor_copy(q1[:, :, :], pr[:, :, :]))
            for best in range(2):
                ln_r(nc.vector.tensor_reduce(m1[:, :], q1[:, :, :], AX.X, ALU.max))
                ln_r(nc.vector.tensor_tensor(q2[:, :, :], q1[:, :, :], bc(m1[:, :]), ALU.is_lt))
                ln_r(nc.vector.scalar_tensor_tensor(q2[:, :, :], q2[:, :, :], 100.0, iota, ALU.mult, ALU.add))
                ln_r(nc.vector.tensor_reduce(m2[:, :], q2[:, :, :], AX.X, ALU.min))
                ln_r(nc.vector.tensor_tensor(q2[:, :, :], iota, bc(m2[:, :]), ALU.is_equal))
                if best == 0:
                    ln_r(nc.vector.tensor_tensor(q3[:, :, :], q2[:, :, :], pr[:, :, :], ALU.mult))
                    ln_r(nc.vector.scalar_tensor_tensor(q1[:, :, :], q2[:, :, :], -4.0, q1[:, :, :],
                                                        ALU.mult, ALU.add))
                else:
                    ln_r(nc.vector.tensor_tensor(q2[:, :, :], q2[:, :, :], pr[:, :, :], ALU.mult))
                    ln_r(nc.vector.tensor_tensor(q3[:, :, :], q3[:, :, :], q2[:, :, :], ALU.add))
            ln_r(nc.vector.tensor_reduce(m2[:, :], q3[:, :, :], AX.X, ALU.add))
            ln_r(nc.vector.reciprocal(m3[:, :], m2[:, :]))
            ln_r(nc.vector.tensor_tensor(wk[:, :, :].rearrange("p e n -> p n e"), q3[:, :, :], bc(m3[:, :]), ALU.mult))
            with dve.Fori(0, E2 // 2) as j:
                for q in range(2):
                    expert_steps(j * 2 + q, q, hidden(X2, lambda e_, q_, t: wk[:, ds(e_, 1), t], PU))
            for r in range(2):
                dve.wait_ge(ya2[r], 1 + 2 * E2)
            norm(2)

        @block.tensor
        def _(pe):
            def transposed(n):
                for q in range(KT * 2):
                    k, hf = q // 2, q % 2
                    pe.wait_ge(ln_ready, n * NT + hf * 4 + 4)
                    if n * 2 + q // 2 > 0:
                        pe.wait_ge(xr_done[q % 2], n * 2 + q // 2)
                    if n:
                        for r in range(2):
                            pe.wait_ge(y_acc[r], 1 + 2 * E1)
                    for t in range(4):
                        last = nc.tensor.transpose(PY[q % 2][:, t * P:(t + 1) * P],
                                                   acc[:, hf * 4 + t, k * P:(k + 1) * P], ident)
                    last.then_inc(xr_mm[q % 2], 1)
                for r in range(2):
                    pe.wait_ge(xr_done[r], n * 2 + 2)

            def products(sems, gate_w, up_w, down_w, used):
                gu, sgd, hd, ym, ya = sems

                def run(kind, k, e, q):
                    if kind == "g":
                        hf, ft = k // 2, k % 2
                        if k >= 2:
                            pe.wait_ge(hd[k % 2], e * 2 + 1)
                        for to, w in ((PG, gate_w),) + (((PU, up_w),) if up_w else ()):
                            for kt in range(KT):
                                last = nc.tensor.matmul(to[k % 2][:, :], w[q][:, kt, ft * P:(ft + 1) * P],
                                                        xT[:, kt, hf * HALF:(hf + 1) * HALF],
                                                        start=(kt == 0), stop=(kt == KT - 1))
                        last.then_inc(gu[k % 2], 1)
                    else:
                        for r in range(2):
                            pe.wait_ge(hd[r], e * 2 + k + 1)
                        for r in range(2):
                            pe.wait_ge(ya[r], e * 2 + k + 1)
                            for n_ in range(2):
                                for ft in range(KT):
                                    t = r * 2 + n_
                                    last = nc.tensor.matmul(PY[r][:, n_ * D:(n_ + 1) * D],
                                                            hh[k][:, ft, t * P:(t + 1) * P], down_w[q][:, ft, :],
                                                            start=(ft == 0), stop=(ft == KT - 1))
                            last.then_inc(ym[r], 1)
                return run

            transposed(0)
            for e in range(E1):
                pe.wait_ge(x_in[e % 2], 16 * (e // 2 + 1))
                for a in range(KT):
                    for k in range(KT):
                        last = nc.tensor.transpose(PX[e % 2][:, k * F + a * P:k * F + (a + 1) * P],
                                                   wx[e % 2][:, a, k * P:(k + 1) * P], ident)
                last.then_inc(ct_mm, 1)
                pe.wait_ge(ct_done, e + 1)
                expert_steps(e, e % 2, products(X1, wt, None, wt, None))
            transposed(1)
            pe.wait_ge(wr_in, 16)
            for t in range(NT):
                for k in range(KT):
                    last = nc.tensor.matmul(PX[0][:, t * E2:(t + 1) * E2], xT[:, k, t * P:(t + 1) * P], wr[:, k, :],
                                            start=(k == 0), stop=(k == KT - 1))
            last.then_inc(r_mm, 1)
            with pe.Fori(0, E2 // 2) as j:
                for q in range(2):
                    pe.wait_ge(gud_in[q], j * 48 + 48)
                    expert_steps(j * 2 + q, q, products(X2, wg, wu, wd, None))


def kernel(**inputs):
    import concourse.bacc as bacc
    from concourse.bass_utils import run_bass_kernel_spmd

    nc = bacc.Bacc("TRN2", target_bir_lowering=False, num_devices=1)
    consts, levels = constants()
    names = ["x", "itok_BxS_13_99985", "ctx_2048", "L0_attn_cu_seqlens", "L0_attn_Wqkv", "L0_attn_Wz", "L0_attn_Wa",
             "L0_attn_Wb", "L0_attn_conv_w", "L0_attn_A_log", "L0_attn_dt_bias", "L0_attn_norm_w", "L0_attn_Wout",
             "L0_ffn_Wr", "L0_ffn_Wg", "L0_ffn_Wu", "L0_ffn_Wd"]
    arrays, args = {}, []
    for name in names:
        a = np.ascontiguousarray(inputs[name])
        arrays["in_" + name] = a
        args.append(nc.dram_tensor("in_" + name, a.shape, mybir.dt.from_np(a.dtype), kind="ExternalInput").ap())
    for name, a in (("consts", consts), ("levels", levels)):
        arrays[name] = a
        args.append(nc.dram_tensor(name, a.shape, mybir.dt.from_np(a.dtype), kind="ExternalInput").ap())
    args.append(nc.dram_tensor("g_rows", (HV, T), mybir.dt.float32, kind="Internal").ap())
    args.append(nc.dram_tensor("result", (B, S, D), mybir.dt.float32, kind="ExternalOutput").ap())
    build(nc, *args)
    got = run_bass_kernel_spmd(nc, [arrays], core_ids=[0])
    return got.results[0]["result"]
```

```python
import math
from contextlib import ExitStack

import concourse.bass as bass
import numpy as np
from concourse import mybir

P = 128
B, S, D = 4, 256, 256
T = B * S
NT = T // P
KT = D // P
HK, HV = 16, 32
TAPS = 4
E1, E2 = 4, 8
F = 256
HALF = T // 2
LEVELS = 7
NEG = -30000.0
QEPS, NEPS, LEPS = 1e-6, 1e-6, 1e-5
NJB = 4
NC = 5

STEPS = (["T0"] + [x for n in range(1, LEVELS) for x in (("AT", n), ("TZ", n))]
         + [("W0", 0), ("AW", 0), ("CO", 0), ("X", 1), ("W0", 1), ("AW", 1), ("CO", 1), "O", "YT", "SS"])
SKEW = 10
STAGES = {
    "C": [("project", "pe", 0), ("tap0", "act", 0), ("tap1", "dve", 1), ("tap2", "dve", 1), ("tap3", "dve", 2),
          ("silu", "act", 4)],
    "N": [("square", "pool", 0), ("sum", "pe", 1), ("rsqrt", "act", 1), ("scale", "pool", 2)],
    "Z": [("project", "pe", 0), ("silu", "act", 0)],
    "K0": [("mask", "pool", 0), ("exp", "act", 1), ("product", "pe", 2), ("decay0", "dve", 2), ("decay1", "dve", 3)],
    "K1": [("product", "pe", 0), ("decay", "dve", 1), ("diagonal", "pool", 1), ("float16", "act", 2)],
    "V": [("transpose", "pe", 0), ("half", "act", 0), ("full", "act", 1)],
    "O": [("project", "pe", 1), ("add0", "dve", 1), ("add1", "dve", 2)],
    "A": [("project", "pe", 0), ("split", "dve", 0), ("softplus", "act", 0), ("decay", "dve", 1)],
    "G": [("sum", "pe", 0), ("bias", "dve", 0)],
    "R": [("transpose", "pe", 0), ("rows", "dve", 1)],
    "M": [("masks", "dve", 0)],
}
DVE_COPIES = {(1, 0), (1, 1), (2, 1), (3, 0), (4, 1), (5, 1)}
C_JOBS = [("C", t, half) for t in range(4) for half in range(2)]
N_JOBS = [("N", t, half) for t in range(2) for half in range(2)]
Z_JOBS = [("Z", b, 0) for b in range(B)]
O_JOBS = [("O", b, c) for b in range(B) for c in range(2)]
PREPARE = {b: [(kind, b, 0) for kind in ("K0", "K1", "V")] for b in range(B)}
FIRST = C_JOBS + [("A", 0, 0), ("G", 0, 0), ("R", 0, 0), ("R", 0, 1), ("M", 0, 0)] + N_JOBS + PREPARE[0]
FIRST_SLOTS = [0, 2, 4, 6, 8, 10, 12, 14, 1, 3, 4, 5, 7, 16, 21,
         17, 22, 18, 20, 18]
BODY = ([(j, -1) for j in O_JOBS[4:]] + [(j, 0) for j in PREPARE[1] + PREPARE[2] + PREPARE[3] + Z_JOBS]
        + [(j, 1) for j in C_JOBS + N_JOBS + PREPARE[0]] + [(j, 0) for j in O_JOBS[:4]])
BEHIND = sum(ahead < 0 for _, ahead in BODY)
SLOTS = [1, 2, 12, 15, 1, 6, 4, 2, 4, 6, 9, 11, 11, 5, 9,
         17, 27, 12, 14, 16, 18, 20, 22, 24, 26, 24, 27, 29, 32, 30,
         35, 41, 22, 25, 33, 37]


def arrange(jobs, slots, end):
    table = sorted((min(slot + lag, end), n, k, name, engine) for n, (job, slot) in enumerate(zip(jobs, slots))
                   for k, (name, engine, lag) in enumerate(STAGES[job[0]]))
    turn = [n for _, n, _, _, engine in table if engine == "pe"]
    return [(slot, n, name, engine) for slot, n, _, name, engine in table], {n: k for k, n in enumerate(turn)}


C_M0, C_M1, C_SUF, C_PRE, C_ROW, C_COL, C_ID, C_ONE, C_E8, C_END = np.cumsum(
    [0, 256, 128, 128, 128, 256, 2, 128, 128, 64]).tolist()


def constants():
    p = np.arange(P)[:, None]
    i = np.arange(S)[None, :]
    f = i[:, :P]
    c = np.zeros((P, C_END), np.float32)
    c[:, C_M0:C_M1] = np.where(p <= i, 0.0, NEG)
    c[:, C_M1:C_SUF] = np.where(p <= f, 0.0, NEG)
    c[:, C_SUF:C_PRE] = np.where(p > f, -1.0, 0.0)
    c[:, C_PRE:C_ROW] = np.where(p <= f, 1.0, 0.0)
    c[:, C_ROW:C_COL] = i
    c[:, C_COL:C_ID] = p + P * np.arange(2)[None, :]
    c[:, C_ID:C_ONE] = p == f
    c[:, C_ONE:C_E8] = 1.0
    c[:, C_E8:C_END] = np.tile(np.arange(E2), NT)[None, :]
    same = [(p >> n) == (f >> n) for n in range(LEVELS + 1)]
    h = np.zeros((P, LEVELS + 2, P), np.float16)
    for n in range(LEVELS):
        h[:, n] = same[0].astype(int) + same[n].astype(int) - same[n + 1].astype(int)
    h[:, LEVELS] = same[0]
    h[:, LEVELS + 1] = h[:, 0].T
    return c, h


def build(nc, x, ids, ctx_in, cu, Wqkv, Wz, Wa, Wb, conv_w, A_log, dt_bias, norm_w, Wout,
          Wr, Wg, Wu, Wd, consts, levels, g_rows, out):
    f32, f16, i32 = mybir.dt.float32, mybir.dt.float16, mybir.dt.int32
    ALU, ACT, AX = mybir.AluOpType, mybir.ActivationFunctionType, mybir.AxisListType
    ds = bass.ds
    stack = ExitStack()
    with stack:
        def sb(name, shape, dt=f32):
            return stack.enter_context(nc.sbuf_tensor(name, shape, dt))

        attention = stack.enter_context(ExitStack())

        def own(name, shape, dt=f32):
            return attention.enter_context(nc.sbuf_tensor(name, shape, dt))

        def sem(name):
            return stack.enter_context(nc.semaphore(name))

        waits_passed = sem("waits_passed")

        def apart(engine):
            engine.sem_inc(waits_passed, 1)

        def two(name):
            return [sem(f"{name}{r}") for r in range(2)]

        cst = sb("cst", [P, C_END])
        acc = sb("acc", [P, NT, D])
        xT = sb("xT", [P, KT, T])
        eps_l = sb("eps_l", [P, 1])
        lev = own("lev", [P, LEVELS + 2, P], f16)
        ident, ones = cst[:, C_ID:C_ONE], cst[:, C_ONE:C_E8]
        wA = own("wA", [P, KT, 4, P])
        wZ = own("wZ", [P, KT, 2 * P])
        wO = own("wO", [P, 2, D])
        cw = own("cw", [P, 4, TAPS])
        Gb = own("Gb", [P, 2, T])
        nw, nws = own("nw", [P, 1]), own("nws", [P, 1])
        wab = own("wab", [P, KT, 2 * HV])
        hb = own("hb", [P, 2, HV])
        cu_i = own("cu_i", [P, NC], i32)
        cu_f = own("cu_f", [P, NC])
        cnt = own("cnt", [P, 2, S])
        cntc = own("cntc", [P, 2])
        M0 = own("M0", [P, S])
        M1 = own("M1", [P, P])
        tmpm = own("tmpm", [P, S])
        cmask = own("cmask", [P, TAPS - 1, S])
        bad = own("bad", [P, 1])
        flag = own("flag", [P, 1], i32)
        u_ab = own("u_ab", [P, NT, 2 * HV])
        v_ab = own("v_ab", [P, NT, 2 * HV])
        w_ab = own("w_ab", [P, NT, 2 * HV])
        ea = own("ea", [P, HV])
        g_tok = own("g_tok", [P, 2, B, HV])
        G_tok = own("G_tok", [P, NT, HV])
        bias = own("bias", [P, NT, HV])
        bcur = own("bcur", [P, NT, 2])
        Grow = own("Grow", [HV, T])
        cv = [own(f"cv{r}", [P, 2, S]) for r in range(2)]
        ct_ = [own(f"ct{r}", [P, 2, S]) for r in range(2)]
        KQ = own("KQ", [P, 2, T])
        VV = own("VV", [P, 2, T])
        sq = [own(f"sq{r}", [P, HALF]) for r in range(4)]
        ln = [own(f"ln{r}", [P, HALF]) for r in range(2)]
        sz = own("sz", [P, NT, 2 * P])
        gm = [own(f"gm{r}", [P, 2, 3 * P]) for r in range(2)]
        Ex = [own(f"Ex{r}", [P, 2, 3 * P]) for r in range(2)]
        AP0 = [own(f"AP0_{b}", [P, 2, 2, S]) for b in range(B)]
        AP1 = [own(f"AP1_{b}", [P, 2, 2, P]) for b in range(B)]
        Ah = [own(f"Ah{b}", [P, 2, 2, P], f16) for b in range(B)]
        R = [own(f"R{b}", [P, 2, 2, P]) for b in range(B)]
        Rh = [own(f"Rh{b}", [P, 2, 2, P], f16) for b in range(B)]
        Tn = [own(f"Tn{r}", [P, 4, P], f16) for r in range(2)]
        Tt = [own(f"Tt{r}", [P, 4, P], f16) for r in range(2)]
        Zn = [own(f"Zn{r}", [P, 4, P], f16) for r in range(2)]
        W = [own(f"W{r}", [P, 2, 2, P]) for r in range(2)]
        rr = [own(f"rr{r}", [P, 2, 2, P], f16) for r in range(2)]
        y = [own(f"y{r}", [P, 2, 2, P]) for r in range(2)]
        y2 = [own(f"y2{r}", [P, 2, 2, P]) for r in range(2)]
        ss = [own(f"ss{r}", [P, 4]) for r in range(2)]
        rs = [own(f"rs{b}", [P, 4]) for b in range(B)]
        yT = own("yT", [P, 2, T])
        eps_q = own("eps_q", [P, 1])
        eps_s = own("eps_s", [P, 1])
        power = own("power", [P, 1])

        PJ = [stack.enter_context(nc.psum_tensor(f"PJ{r}", [P, 512], f32)) for r in range(NJB)]
        PB, PC = ([stack.enter_context(nc.psum_tensor(f"{n}{r}", [P, 512], f32))
                   for r in range(2)] for n in ("PB", "PC"))

        in_x, in_c, in_l, in_s, in_e = sem("in_x"), sem("in_c"), sem("in_l"), sem("in_s"), sem("in_e")
        mask_chain, masks_done = sem("mask_chain"), sem("masks_done")
        eps_done = sem("eps_done")
        xt_mm, xt_done = two("xt_mm"), two("xt_done")
        ab_act, ab_chain, g_done = sem("ab_act"), sem("ab_chain"), sem("g_done")
        G_done, G_out = sem("G_done"), sem("G_out")
        wA_in, wZ_in, wO_in, cw_in, Gb_in = sem("wA_in"), sem("wZ_in"), sem("wO_in"), sem("cw_in"), sem("Gb_in")
        pj_full, pj_free = ([sem(f"{n}{r}") for r in range(NJB)] for n in ("pj_full", "pj_free"))
        tap_done, mix_done = two("tap_done"), two("mix_done")
        conv_chain, mask_used = two("conv_chain"), two("mask_used")
        sq_done, rn_done, norm_done = two("sq_done"), two("rn_done"), two("norm_done")
        bcur_done = sem("bcur_done")
        acc_chain = [sem(f"acc_chain{b}") for b in range(B)]
        gm_done, e_done, r_done = two("gm_done"), two("e_done"), two("r_done")
        diag_done, ah_done, tt0_done = two("diag_done"), two("ah_done"), two("tt0_done")
        at_mm, z_done, tt_mm, t_done = two("at_mm"), two("z_done"), two("tt_mm"), two("t_done")
        tn_done = two("tn_done")
        w0_mm, w0_done, aw_mm, rr_done = two("w0_mm"), two("w0_done"), two("aw_mm"), two("rr_done")
        cor_mm, w_done, x_mm, r2_done = two("cor_mm"), two("w_done"), two("x_mm"), two("r2_done")
        o_mm, y_done, ysq_done, ss_done = two("o_mm"), two("y_done"), two("ysq_done"), two("ss_done")
        sl_done, rs_done, yt_mm, yt_done = two("sl_done"), two("rs_done"), two("yt_mm"), two("yt_done")

        LN_EXP = "natural_log_exp_and_others"
        NS = LEVELS
        RING = len(BODY) // NJB

        def bank(number, i):
            return number % NJB, number // NJB + i * RING

        ALL = 2 * len(STEPS)
        FIRST_TABLE, FIRST_TURN = arrange(FIRST, FIRST_SLOTS, 100)
        TABLES = {}
        for part in ("first", "loop", "last"):
            kept = [(j, ahead, slot) for (j, ahead), slot in zip(BODY, SLOTS, strict=True)
                    if not (ahead < 0 and part == "first" or ahead > 0 and part == "last")]
            if part == "last":
                kept += [(j, 0, slot + ALL) for (j, ahead), slot in zip(BODY, SLOTS) if ahead < 0]
            jobs_ = [j for j, _, _ in kept]
            table_, turn_ = arrange(jobs_, [slot for _, _, slot in kept], ALL + (SKEW + 4 if part == "last" else 0))
            base = len(FIRST_TURN) - (0 if part == "first" else BEHIND)
            TABLES[part] = (jobs_, [ahead for _, ahead, _ in kept], table_, {n: k + base for n, k in turn_.items()})

        def place(job, part, whose=0):
            jobs, ahead, _, turn = TABLES[part]
            return turn[next(n for n, j in enumerate(jobs) if j == job and ahead[n] == whose)]

        def walk(i, part, me, each_set, stage):
            jobs, ahead, table, turn = TABLES[part]
            for slot in range(ALL + (SKEW + 5 if part == "last" else 1)):
                for s in range(2):
                    at = slot - SKEW * s
                    if 0 <= at < ALL and (slot < ALL or part == "last"):
                        p, n = divmod(at, len(STEPS))
                        each_set(STEPS[n], 2 * p + s, s, p, i, part)
                    elif at < 0 and part != "first":
                        each_set(STEPS[at + len(STEPS)], 2 + s, s, 1, i - 1, "loop")
                for to, n, name, engine in table:
                    if to == slot and engine == me:
                        stage(jobs[n], name, *bank(turn[n], i), i + ahead[n])

        def walk_first(me, stage):
            for _, n, name, engine in FIRST_TABLE:
                if engine == me:
                    stage(FIRST[n], name, *bank(FIRST_TURN.get(n, 0), 0), 0)

        def first(i):
            return isinstance(i, int) and i == 0

        with nc.Block() as block:
            @block.sync
            def _(sp):
                xf = x.rearrange("b s d -> (b s) d").rearrange("(n p) d -> p n d", p=P)
                for hf in range(2):
                    sp.dma_start(acc[:, 4 * hf:4 * hf + 4, :], xf[:, 4 * hf:4 * hf + 4, :]).then_inc(in_x, 16)
                sp.dma_start(cst[:, :], consts).then_inc(in_c, 16)
                sp.dma_start(cu_i[:, :], cu.rearrange("(o n) -> o n", o=1).to_broadcast((P, NC))).then_inc(in_s, 16)

                def load_A(i):
                    v = lambda a: a.rearrange("(k p) n -> p k n", p=P)
                    q_cols = Wqkv[:, ds(i * P, P)]
                    k_cols = Wqkv[:, ds(i * P + HK * P, P)]
                    v_cols = Wqkv[:, ds(i * 2 * P + 2 * HK * P, 2 * P)]
                    sp.dma_start(wA[:, :, 0, :], v(k_cols)).then_inc(wA_in, 16)
                    sp.dma_start(wA[:, :, 1, :], v(q_cols)).then_inc(wA_in, 16)
                    sp.dma_start(wA[:, :, 2:4, :].rearrange("p k a n -> p k (a n)"), v(v_cols)).then_inc(wA_in, 16)
                    sp.dma_start(cw[:, 0, :], conv_w[ds(i * P + HK * P, P), :]).then_inc(cw_in, 16)
                    sp.dma_start(cw[:, 1, :], conv_w[ds(i * P, P), :]).then_inc(cw_in, 16)
                    sp.dma_start(cw[:, 2:4, :], conv_w[ds(i * 2 * P + 2 * HK * P, 2 * P), :].rearrange(
                        "(a p) n -> p a n", p=P)).then_inc(cw_in, 16)

                def load_G(i):
                    for h in range(2):
                        sp.dma_start(Gb[:, h, :], g_rows[ds(i * 2 + h, 1), :].to_broadcast((P, T))).then_inc(Gb_in, 16)

                def load_Z(i):
                    sp.dma_start(wZ[:, :, :], Wz[:, ds(i * 2 * P, 2 * P)].rearrange("(k p) n -> p k n", p=P)).then_inc(wZ_in, 16)

                def load_O(i):
                    sp.dma_start(wO[:, :, :], Wout[ds(i * 2 * P, 2 * P), :].rearrange("(a p) n -> p a n", p=P)).then_inc(wO_in, 16)

                load_A(0)
                sp.dma_start(lev[:, :, :], levels).then_inc(in_l, 16)
                load_Z(0)
                load_O(0)
                for n, j in enumerate(FIRST):
                    if j[0] == "R":
                        r, m = bank(FIRST_TURN[n], 0)
                        sp.wait_ge(pj_free[r], m + 1)
                sp.dma_start(g_rows, Grow[:, :]).then_inc(G_out, 16)
                sp.wait_ge(G_out, 16)
                load_G(0)

                def behind(number, i):
                    r, m = bank(number, i)
                    sp.wait_ge(pj_full[r], m + 1)
                    apart(sp)

                def next_O(i, part):
                    behind(max(place(j, part, -1) for j, ahead in BODY if ahead < 0), i)
                    load_O(i)

                def head(i, part):
                    for r in range(2):
                        sp.wait_ge(mix_done[r], (i + 1) * 4)
                    apart(sp)
                    load_A(i + 1)
                    if part != "first":
                        next_O(i, part)
                    for s in range(2):
                        sp.wait_ge(gm_done[s], (i + 1) * 2)
                    apart(sp)
                    load_G(i + 1)
                    behind(max(place(j, part) for j in Z_JOBS), i)
                    load_Z(i + 1)

                head(0, "first")
                with sp.Fori(1, HK - 1) as i:
                    head(i, "loop")
                next_O(HK - 1, "last")

            @block.gpsimd
            def _(pool):
                nc.gpsimd.memset(eps_q[:, :], QEPS)
                nc.gpsimd.memset(eps_s[:, :], -0.5 * math.log(P))
                nc.gpsimd.memset(eps_l[:, :], LEPS)
                nc.gpsimd.memset(power[:, :], -0.5).then_inc(eps_done, 1)
                pool.wait_ge(in_e, 80)
                nc.gpsimd.tensor_scalar(nws[:, :], nw[:, :], math.sqrt(P), None, ALU.mult).then_inc(eps_done, 1)

                def stage(j, name, r, m, i):
                    kind, t, hf = j
                    if kind == "N":
                        kq = KQ[:, t, hf * HALF:(hf + 1) * HALF]
                        if name == "square":
                            pool.wait_ge(mix_done[hf], i * 4 + t + 1)
                            if not first(i):
                                pool.wait_ge(norm_done[hf], i * 2 + (t - 1))
                            nc.gpsimd.tensor_tensor(sq[2 * t + hf][:, :], kq, kq, ALU.mult).then_inc(sq_done[hf], 1)
                        else:
                            pool.wait_ge(rn_done[hf], i * 2 + t + 1)
                            nc.gpsimd.tensor_tensor(kq, kq, ln[hf][:, :], ALU.mult).then_inc(norm_done[hf], 1)
                    elif kind == "K0":
                        masked_decays(t, i)
                    elif kind == "K1":
                        unit_diagonal(t, r, m, i)

                def masked_decays(b, i):
                    s, n = b % 2, b // 2
                    if b == 0:
                        if not first(i):
                            for q in range(2):
                                pool.wait_ge(e_done[q], i * 2)
                        else:
                            pool.wait_ge(G_done, 2)
                            pool.wait_ge(masks_done, 1)
                            pool.wait_ge(in_l, 16)
                        apart(pool)
                        nc.gpsimd.tensor_copy(bcur[:, :, :], bias[:, :, ds(i * 2, 2)]).then_inc(bcur_done, 1)
                        pool.wait_ge(Gb_in, i * 32 + 32)
                    if not first(i) or n:
                        pool.wait_ge(e_done[s], i * 2 + n)
                    Gv = Gb[:, :, b * S:(b + 1) * S]
                    nc.gpsimd.tensor_tensor(gm[s][:, :, 0:S], Gv, M0[:, :].rearrange("p (o t) -> p o t", o=1)
                                            .to_broadcast((P, 2, S)), ALU.add)
                    nc.gpsimd.tensor_tensor(gm[s][:, :, S:], Gv[:, :, P:S], M1[:, :].rearrange("p (o t) -> p o t", o=1)
                                            .to_broadcast((P, 2, P)), ALU.add).then_inc(gm_done[s], 1)

                def unit_diagonal(b, r, m, i):
                    s, n = b % 2, b // 2
                    pool.wait_ge(pj_free[r], m + 1)
                    apart(pool)
                    for c, a in ((0, AP0[b][:, :, 0, 0:P]), (1, AP1[b][:, :, 0, :])):
                        nc.gpsimd.affine_select(out=a, in_=a, compare_op=ALU.not_equal, fill=1.0, base=0,
                                                pattern=[[0, 2], [1, P]], channel_multiplier=-1).then_inc(diag_done[s], 1)

                def step(st, b, s, p, i, part):
                    if st == "T0":
                        pool.wait_ge(ah_done[s], i * 4 + 2 * p + 2)
                        pool.wait_ge(at_mm[s], (i * 2 + p) * NS + 1)
                        nc.gpsimd.tensor_tensor(
                            Tt[s][:, :, :], Ah[b][:, :, :, :].rearrange("p a c t -> p (a c) t"),
                            lev[:, LEVELS + 1:LEVELS + 2, :].to_broadcast((P, 4, P)), ALU.mult).then_inc(tt0_done[s], 1)
                    elif st == "O":
                        pool.wait_ge(y_done[s], i * 2 + p + 1)
                        nc.gpsimd.tensor_tensor(y2[s][:, :, :, :], y[s][:, :, :, :], y[s][:, :, :, :],
                                                ALU.mult).then_inc(ysq_done[s], 1)
                    elif st == "SS":
                        pool.wait_ge(ss_done[s], i * 2 + p + 1)
                        apart(pool)
                        nc.gpsimd.tensor_scalar(ss[s][:, :], ss[s][:, :], P * NEPS, None,
                                                ALU.add).then_inc(sl_done[s], 1)
                        pool.wait_ge(sl_done[s], i * 2 + p + 1)
                        nc.gpsimd.tensor_tensor(rs[b][:, :], ss[s][:, :], power[:, :].to_broadcast((P, 4)),
                                                ALU.pow).then_inc(rs_done[s], 1)

                walk_first("pool", stage)

                walk(0, "first", "pool", step, stage)
                with pool.Fori(1, HK - 1) as i:
                    walk(i, "loop", "pool", step, stage)
                walk(HK - 1, "last", "pool", step, stage)

            @block.scalar
            def _(act):
                act.dma_start(wab[:, :, 0:HV], Wa.rearrange("(k p) n -> p k n", p=P)).then_inc(in_e, 16)
                act.dma_start(wab[:, :, HV:], Wb.rearrange("(k p) n -> p k n", p=P)).then_inc(in_e, 16)
                act.dma_start(hb[:, 0, :], A_log.rearrange("(o n) -> o n", o=1).to_broadcast((P, HV))).then_inc(in_e, 16)
                act.dma_start(hb[:, 1, :], dt_bias.rearrange("(o n) -> o n", o=1).to_broadcast((P, HV))).then_inc(in_e, 16)
                act.dma_start(nw[:, :], norm_w.rearrange("(p o) -> p o", o=1)).then_inc(in_e, 16)
                table = [None]

                def ln_exp():
                    if table[0] != LN_EXP:
                        nc.scalar.preload_act_table_set(LN_EXP)
                    table[0] = LN_EXP

                def stage(j, name, r, m, i):
                    kind, t, hf = j
                    if name == "tap0":
                        act.wait_ge(pj_full[r], m + 1)
                        act.wait_ge(cw_in, i * 48 + 48)
                        if not first(i) or t:
                            act.wait_ge(mix_done[hf], i * 4 + t)
                        nc.scalar.activation(cv[hf][:, :, :].rearrange("p b t -> p (b t)"), PJ[r][:, :], ACT.Copy,
                                             scale=cw[:, t, TAPS - 1:TAPS]).then_inc(tap_done[hf], 1)
                    elif kind == "A":
                        ln_exp()
                        act.wait_ge(in_e, 80)
                        nc.scalar.activation(ea[:, :], hb[:, 0, :], ACT.Exp).then_inc(ab_act, 1)
                        act.wait_ge(ab_chain, 3)
                        nc.scalar.activation(w_ab[:, :, :], v_ab[:, :, :], ACT.Exp).then_inc(ab_act, 1)
                        act.wait_ge(ab_act, 2)
                        act.wait_ge(eps_done, 1)
                        nc.scalar.activation(v_ab[:, :, :], w_ab[:, :, :], ACT.Ln, bias=ones[:, 0:1]).then_inc(ab_act, 1)
                    elif kind == "C":
                        table[0] = None
                        act.wait_ge(pj_free[r], m + 1)
                        dst = (KQ[:, t, :] if t < 2 else VV[:, t - 2, :])[:, hf * HALF:(hf + 1) * HALF]
                        nc.scalar.activation(dst, cv[hf][:, :, :].rearrange("p b t -> p (b t)"), ACT.Silu).then_inc(
                            mix_done[hf], 1)
                    elif kind == "N":
                        ln_exp()
                        act.wait_ge(pj_full[r], m + 1)
                        if not first(i) or t:
                            act.wait_ge(norm_done[hf], i * 2 + t)
                        nc.scalar.activation(ln[hf][:, :], PJ[r][:, :], ACT.Ln, bias=eps_q[:, :]).then_inc(pj_free[r], 1)
                        act.wait_ge(pj_free[r], m + 1)
                        kw = {"bias": eps_s[:, :]} if t == 1 else {}
                        nc.scalar.activation(ln[hf][:, :], ln[hf][:, :], ACT.Exp, scale=-0.5, **kw).then_inc(rn_done[hf], 1)
                    elif kind == "Z":
                        table[0] = None
                        act.wait_ge(pj_full[r], m + 1)
                        nc.scalar.activation(sz[:, 2 * t:2 * t + 2, :].rearrange("p n d -> p (n d)"), PJ[r][:, :],
                                             ACT.Silu).then_inc(pj_free[r], 1)
                    elif kind == "K0":
                        decays(t, i)
                    elif name == "half":
                        act.wait_ge(pj_full[r], m + 1)
                        nc.scalar.copy(Rh[t][:, :, :, :].rearrange("p a c t -> p (a c t)"), PJ[r][:, :]).then_inc(
                            r_done[t % 2], 1)
                    elif name == "float16":
                        act.wait_ge(diag_done[t % 2], i * 4 + t // 2 * 2 + 2)
                        nc.scalar.copy(Ah[t][:, :, 0, :], AP0[t][:, :, 0, 0:P]).then_inc(ah_done[t % 2], 1)
                        nc.scalar.copy(Ah[t][:, :, 1, :], AP1[t][:, :, 0, :]).then_inc(ah_done[t % 2], 1)
                    elif name == "full":
                        nc.scalar.copy(R[t][:, :, :, :].rearrange("p a c t -> p (a c t)"), PJ[r][:, :]).then_inc(
                            pj_free[r], 1)

                def decays(b, i):
                    s, n = b % 2, b // 2
                    ln_exp()
                    if b == 0:
                        act.wait_ge(bcur_done, i + 1)
                    act.wait_ge(gm_done[s], i * 2 + n + 1)
                    if not first(i) or n:
                        act.wait_ge(diag_done[s], i * 4 + n * 2)
                    for h in range(2):
                        nc.scalar.activation(Ex[s][:, h, 0:S], gm[s][:, h, 0:S], ACT.Exp, bias=bcur[:, 2 * b, h:h + 1])
                        last = nc.scalar.activation(Ex[s][:, h, S:], gm[s][:, h, S:], ACT.Exp,
                                                    bias=bcur[:, 2 * b + 1, h:h + 1])
                    last.then_inc(e_done[s], 1)

                def step(st, b, s, p, i, part):
                    at = i * 2 + p
                    if st[0] == "TZ":
                        act.wait_ge(tt_mm[s], at * (LEVELS - 1) + st[1])
                        if st[1] < LEVELS - 1 and (st[1], s) not in DVE_COPIES:
                            nc.scalar.copy(Tn[s][:, :, :].rearrange("p u t -> p (u t)"), PB[s][:, :])
                        nc.scalar.copy(Tt[s][:, :, :].rearrange("p u t -> p (u t)"), PC[s][:, :]).then_inc(t_done[s], 1)
                    elif st[0] == "W0":
                        act.wait_ge(w0_mm[s], at * 2 + st[1] + 1)
                        nc.scalar.copy(W[s][:, :, st[1], :], PB[s][:, 0:2 * P].rearrange("p (h t) -> p h t", h=2)).then_inc(
                            w0_done[s], 1)
                    elif st == "YT":
                        if first(i) and p == 0:
                            act.wait_ge(eps_done, 2)
                        act.wait_ge(yt_mm[s], at + 1)
                        nc.scalar.activation(yT[:, :, b * S:(b + 1) * S],
                                             PB[s][:, :].rearrange("p (h t) -> p h t", h=2), ACT.Copy,
                                             scale=nws[:, 0:1]).then_inc(yt_done[s], 1)

                walk_first("act", stage)

                walk(0, "first", "act", step, stage)
                with act.Fori(1, HK - 1) as i:
                    table[0] = None
                    walk(i, "loop", "act", step, stage)
                walk(HK - 1, "last", "act", step, stage)

            @block.vector
            def _(dve):
                for q in range(KT * 2):
                    k, hf = q % 2, q // 2
                    dve.wait_ge(xt_mm[q % 2], q // 2 + 1)
                    nc.vector.tensor_copy(xT[:, k, hf * HALF:(hf + 1) * HALF], PJ[q][:, :]).then_inc(xt_done[hf], 1)

                n = [0]

                def link(ins):
                    n[0] += 1
                    ins.then_inc(mask_chain, 1)
                    dve.wait_ge(mask_chain, n[0])

                dve.wait_ge(in_c, 16)
                dve.wait_ge(in_s, 16)
                link(nc.vector.tensor_copy(cu_f[:, :], cu_i[:, :]))
                row = cst[:, C_ROW:C_COL]
                link(nc.vector.tensor_scalar(cnt[:, 1, :], row, cu_f[:, 1:2], None, ALU.is_ge))
                for m in (2, 3):
                    link(nc.vector.scalar_tensor_tensor(cnt[:, 1, :], row, cu_f[:, m:m + 1], cnt[:, 1, :],
                                                        ALU.is_ge, ALU.add))
                link(nc.vector.memset(cmask[:, :, :], 1.0))
                for s in range(1, TAPS):
                    link(nc.vector.tensor_tensor(cmask[:, s - 1, s:S], cnt[:, 1, s:S], cnt[:, 1, 0:S - s],
                                                 ALU.is_equal))
                link(nc.vector.tensor_reduce(bad[:, :], cmask[:, :, :], AX.XY, ALU.min))
                link(nc.vector.tensor_copy(flag[:, :], bad[:, :]))

                before = n[0]

                def decay_masks():
                    n[0] = before
                    link(nc.vector.scalar_tensor_tensor(cnt[:, 0, :], row, cu_f[:, 0:1], cnt[:, 1, :],
                                                        ALU.is_ge, ALU.add))
                    col = cst[:, C_COL:C_ID]
                    link(nc.vector.tensor_scalar(cntc[:, :], col, cu_f[:, 0:1], None, ALU.is_ge))
                    for m in (1, 2, 3):
                        link(nc.vector.scalar_tensor_tensor(cntc[:, :], col, cu_f[:, m:m + 1], cntc[:, :],
                                                            ALU.is_ge, ALU.add))
                    link(nc.vector.tensor_scalar(tmpm[:, :], cnt[:, 0, :], cntc[:, 0:1], NEG, ALU.not_equal, ALU.mult))
                    link(nc.vector.tensor_tensor(M0[:, :], tmpm[:, :], cst[:, C_M0:C_M1], ALU.add))
                    link(nc.vector.tensor_scalar(tmpm[:, 0:P], cnt[:, 0, P:S], cntc[:, 1:2], NEG, ALU.not_equal, ALU.mult))
                    nc.vector.tensor_tensor(M1[:, :], tmpm[:, 0:P], cst[:, C_M1:C_SUF], ALU.add).then_inc(masks_done, 1)

                def shared(kind, name, r, m, hf):
                    if name == "split":
                        dve.wait_ge(in_e, 80)
                        dve.wait_ge(pj_full[r], m + 1)
                        ab = PJ[r][:, :].rearrange("p (n c) -> p n c", c=2 * HV)
                        nc.vector.tensor_tensor(u_ab[:, :, 0:HV], ab[:, :, 0:HV],
                                                hb[:, 1:2, :].to_broadcast((P, NT, HV)), ALU.add).then_inc(ab_chain, 1)
                        nc.vector.tensor_scalar(u_ab[:, :, HV:], ab[:, :, HV:], -1.0, None, ALU.mult).then_inc(pj_free[r], 1)
                        dve.wait_ge(ab_chain, 1)
                        dve.wait_ge(pj_free[r], m + 1)
                        nc.vector.tensor_scalar(v_ab[:, :, :], u_ab[:, :, :], -1.0, None, ALU.mult).then_inc(ab_chain, 1)
                        dve.wait_ge(ab_chain, 2)
                        nc.vector.tensor_tensor(v_ab[:, :, :], v_ab[:, :, :], u_ab[:, :, :], ALU.min).then_inc(ab_chain, 1)
                    elif name == "decay":
                        dve.wait_ge(ab_act, 3)
                        nc.vector.scalar_tensor_tensor(u_ab[:, :, :], u_ab[:, :, :], 0.0, v_ab[:, :, :],
                                                       ALU.max, ALU.add).then_inc(ab_chain, 1)
                        dve.wait_ge(ab_chain, 4)
                        for c in range(2):
                            nc.vector.scalar_tensor_tensor(
                                g_tok[:, c, :, :], u_ab[:, c::2, 0:HV], -1.0,
                                ea[:, :].rearrange("p (o h) -> p o h", o=1).to_broadcast((P, B, HV)),
                                ALU.mult, ALU.mult).then_inc(g_done, 1)
                    elif name == "bias":
                        dve.wait_ge(pj_full[r], m + 1)
                        for c in range(2):
                            nc.vector.tensor_copy(G_tok[:, c::2, :], PJ[r][:, c * P:(c + 1) * P].rearrange(
                                "p (b h) -> p b h", b=B)).then_inc(G_done if c == 0 else pj_free[r], 1)
                        dve.wait_ge(G_done, 1)
                        dve.wait_ge(pj_free[r], m + 1)
                        nc.vector.scalar_tensor_tensor(bias[:, :, :], u_ab[:, :, HV:], -1.0, G_tok[:, :, :],
                                                       ALU.mult, ALU.subtract).then_inc(G_done, 1)
                    elif name == "rows":
                        dve.wait_ge(pj_full[r], m + 1)
                        nc.vector.tensor_copy(Grow[:, hf * HALF:(hf + 1) * HALF], PJ[r][0:HV, :]).then_inc(pj_free[r], 1)
                    else:
                        decay_masks()

                def stage(j, name, r, m, i, whole_rows):
                    kind, t, hf = j
                    if kind in ("A", "G", "R", "M"):
                        shared(kind, name, r, m, hf)
                    elif kind == "C":
                        tap(int(name[3]), r, m, t, hf, i, whole_rows)
                    elif kind == "O":
                        h, at = int(name[3]), acc[:, 2 * t + hf, :]
                        if h == 0:
                            dve.wait_ge(pj_full[r], m + 1)
                            dve.wait_ge(rs_done[t % 2], i * 2 + t // 2 + 1)
                        else:
                            dve.wait_ge(acc_chain[t], i * 2 + hf + 1)
                        nc.vector.scalar_tensor_tensor(at, PJ[r][:, h * D:(h + 1) * D], rs[t][:, 2 * h + hf:2 * h + hf + 1],
                                                       at, ALU.mult, ALU.add).then_inc(
                            pj_free[r] if h else acc_chain[t], 1)
                    else:
                        s, n = t % 2, t // 2
                        dve.wait_ge(pj_full[r], m + 1)
                        dve.wait_ge(e_done[s], i * 2 + n + 1)
                        to, width, of = (AP1, P, S) if kind == "K1" else (AP0, S, 0)
                        for h in {"decay0": [0], "decay1": [1], "decay": [0, 1]}[name]:
                            last = nc.vector.tensor_tensor(
                                to[t][:, h, :, :], PJ[r][:, 0:2 * width].rearrange("p (a t) -> p a t", a=2),
                                Ex[s][:, h:h + 1, of:of + width].to_broadcast((P, 2, width)), ALU.mult)
                        if name != "decay0":
                            last.then_inc(pj_free[r], 1)

                def tap(s, r, m, t, hf, i, whole_rows):
                    n0 = (i * 4 + t) * 2
                    if s == 1:
                        dve.wait_ge(tap_done[hf], i * 4 + t + 1)
                    else:
                        dve.wait_ge(conv_chain[hf], n0 + s - 1)
                    src = PJ[r][:, :].rearrange("p (b t) -> p b t", b=2)[:, :, 0:S - s]
                    if not whole_rows:
                        masked = ct_[hf][:, :, s:S]
                        nc.vector.tensor_tensor(masked, src, cmask[:, s - 1:s, s:S].to_broadcast((P, 2, S - s)),
                                                ALU.mult).then_inc(mask_used[hf], 1)
                        dve.wait_ge(mask_used[hf], (i * 4 + t) * 3 + s)
                        src = masked
                    nc.vector.scalar_tensor_tensor(
                        cv[hf][:, :, s:S], src, cw[:, t, TAPS - 1 - s:TAPS - s], cv[hf][:, :, s:S],
                        ALU.mult, ALU.add).then_inc(pj_free[r] if s == TAPS - 1 else conv_chain[hf], 1)

                def step(st, b, s, p, i, part):
                    at = i * 2 + p
                    four = lambda n: lev[:, n:n + 1, :].to_broadcast((P, 4, P))
                    if st == "T0" or st[0] == "AT":
                        n = 0 if st == "T0" else st[1]
                        if first(i) and n == 0:
                            dve.wait_ge(in_l, 16)
                        dve.wait_ge(at_mm[s], at * NS + n + 1)
                        nc.vector.tensor_tensor((Zn if n else Tn)[s][:, :, :],
                                                PB[s][:, :].rearrange("p (u t) -> p u t", u=4), four(n),
                                                ALU.mult).then_inc(z_done[s], 1)
                    elif st[0] == "TZ" and (st[1], s) in DVE_COPIES:
                        dve.wait_ge(tt_mm[s], at * (NS - 1) + st[1])
                        nc.vector.tensor_copy(Tn[s][:, :, :].rearrange("p u t -> p (u t)"), PB[s][:, :]).then_inc(
                            tn_done[s], 1)
                    elif st[0] == "AW":
                        dve.wait_ge(aw_mm[s], at * 2 + st[1] + 1)
                        nc.vector.tensor_tensor(rr[s][:, :, st[1], :], R[b][:, :, st[1], :],
                                                PC[s][:, 0:S].rearrange("p (h t) -> p h t", h=2),
                                                ALU.subtract).then_inc(rr_done[s], 1)
                    elif st[0] == "CO":
                        dve.wait_ge(cor_mm[s], at * 2 + st[1] + 1)
                        nc.vector.tensor_tensor(W[s][:, :, st[1], :], W[s][:, :, st[1], :],
                                                PB[s][:, S:].rearrange("p (h t) -> p h t", h=2),
                                                ALU.add).then_inc(w_done[s], 1)
                    elif st[0] == "X":
                        dve.wait_ge(x_mm[s], at + 1)
                        cross = PC[s][:, S:].rearrange("p (h t) -> p h t", h=2)
                        nc.vector.tensor_tensor(Rh[b][:, :, 1, :], R[b][:, :, 1, :], cross, ALU.subtract)
                        nc.vector.tensor_tensor(R[b][:, :, 1, :], R[b][:, :, 1, :], cross,
                                                ALU.subtract).then_inc(r2_done[s], 1)
                    elif st == "O":
                        dve.wait_ge(o_mm[s], at + 1)
                        r, m = bank(place(Z_JOBS[b], part), i)
                        dve.wait_ge(pj_free[r], m + 1)
                        nc.vector.tensor_tensor(
                            y[s][:, :, :, :], PC[s][:, :].rearrange("p (h c t) -> p h c t", h=2, c=2),
                            sz[:, 2 * b:2 * b + 2, :].rearrange("p c (h t) -> p h c t", h=2),
                            ALU.mult).then_inc(y_done[s], 1)
                    elif st == "SS":
                        dve.wait_ge(ysq_done[s], at + 1)
                        nc.vector.tensor_reduce(ss[s][:, :], y2[s][:, :, :, :].rearrange("p a c t -> p (a c) t"),
                                                AX.X, ALU.add).then_inc(ss_done[s], 1)

                def heads(whole_rows):
                    mine = lambda *job: stage(*job, whole_rows)
                    walk_first("dve", mine)

                    walk(0, "first", "dve", step, mine)
                    with dve.Fori(1, HK - 1) as i:
                        walk(i, "loop", "dve", step, mine)
                    walk(HK - 1, "last", "dve", step, mine)

                unbroken = dve.value_load(flag[0:1, 0:1], min_val=0, max_val=1)
                with dve.If(unbroken):
                    heads(True)
                with dve.Else():
                    heads(False)

            @block.tensor
            def _(pe):
                pe.wait_ge(in_c, 16)
                for q in range(KT * 2):
                    k, hf = q % 2, q // 2
                    pe.wait_ge(in_x, 32)
                    for n_ in range(4):
                        last = nc.tensor.transpose(PJ[q][:, n_ * P:(n_ + 1) * P],
                                                   acc[:, hf * 4 + n_, k * P:(k + 1) * P], ident)
                    last.then_inc(xt_mm[q % 2], 1)
                for hf in range(2):
                    pe.wait_ge(xt_done[hf], 2)

                def stage(j, name, r, m, i):
                    kind, t, hf = j
                    if not (isinstance(m, int) and m == 0):
                        pe.wait_ge(pj_free[r], m)
                    if kind == "C":
                        pe.wait_ge(wA_in, i * 48 + 48)
                        for k in range(KT):
                            last = nc.tensor.matmul(PJ[r][:, :], wA[:, k, t, :], xT[:, k, hf * HALF:(hf + 1) * HALF],
                                                    start=(k == 0), stop=(k == KT - 1))
                        last.then_inc(pj_full[r], 1)
                    elif kind == "A":
                        pe.wait_ge(in_e, 80)
                        for n_ in range(NT):
                            for k in range(KT):
                                last = nc.tensor.matmul(PJ[r][:, n_ * 2 * HV:(n_ + 1) * 2 * HV],
                                                        xT[:, k, n_ * P:(n_ + 1) * P], wab[:, k, :],
                                                        start=(k == 0), stop=(k == KT - 1))
                        last.then_inc(pj_full[r], 1)
                    elif kind == "G":
                        pe.wait_ge(g_done, 2)
                        for c, tri in ((0, C_SUF), (1, C_PRE)):
                            last = nc.tensor.matmul(PJ[r][:, c * P:(c + 1) * P], cst[:, tri:tri + P],
                                                    g_tok[:, c, :, :].rearrange("p b h -> p (b h)"), start=True, stop=True)
                        last.then_inc(pj_full[r], 1)
                    elif kind == "R":
                        pe.wait_ge(G_done, 2)
                        for n_ in range(4):
                            last = nc.tensor.transpose(PJ[r][0:HV, n_ * P:(n_ + 1) * P], G_tok[:, 4 * hf + n_, :], ident)
                        last.then_inc(pj_full[r], 1)
                    elif kind == "N":
                        pe.wait_ge(sq_done[hf], i * 2 + t + 1)
                        nc.tensor.matmul(PJ[r][:, :], ones, sq[2 * t + hf][:, :], start=True, stop=True).then_inc(pj_full[r], 1)
                    elif kind == "Z":
                        pe.wait_ge(wZ_in, i * 16 + 16)
                        for n_ in range(2):
                            for k in range(KT):
                                tok = (2 * t + n_) * P
                                last = nc.tensor.matmul(PJ[r][:, n_ * 2 * P:(n_ + 1) * 2 * P], xT[:, k, tok:tok + P],
                                                        wZ[:, k, :], start=(k == 0), stop=(k == KT - 1))
                        last.then_inc(pj_full[r], 1)
                    elif kind in ("K0", "K1"):
                        pe.wait_ge(norm_done[t // 2], i * 2 + 2)
                        j0, width = t * S + P * int(kind[1]), (S, P)[int(kind[1])]
                        nc.tensor.matmul(PJ[r][:, 0:2 * width].rearrange("p (a t) -> p a t", a=2), KQ[:, 0, j0:j0 + P],
                                         KQ[:, :, j0:j0 + width], start=True, stop=True).then_inc(pj_full[r], 1)
                    elif kind == "V":
                        pe.wait_ge(mix_done[t // 2], i * 4 + 4)
                        for h in range(2):
                            for c in range(2):
                                u, tok = 2 * h + c, t * S + c * P
                                last = nc.tensor.transpose(PJ[r][:, u * P:(u + 1) * P], VV[:, h, tok:tok + P], ident)
                        last.then_inc(pj_full[r], 1)
                    elif kind == "O":
                        pe.wait_ge(wO_in, i * 16 + 16)
                        pe.wait_ge(yt_done[t % 2], i * 2 + t // 2 + 1)
                        tok = (2 * t + hf) * P
                        for h in range(2):
                            last = nc.tensor.matmul(PJ[r][:, h * D:(h + 1) * D], yT[:, h, tok:tok + P],
                                                    wO[:, h, :], start=True, stop=True)
                        last.then_inc(pj_full[r], 1)

                def step(st, b, s, p, i, part):
                    at = i * 2 + p
                    U = [(h, c) for h in range(2) for c in range(2)]
                    cols = lambda u: slice(u * P, (u + 1) * P)
                    if st == "T0" or st[0] == "AT":
                        n = 0 if st == "T0" else st[1]
                        if n == 0:
                            pe.wait_ge(ah_done[s], i * 4 + 2 * p + 2)
                            if first(i):
                                pe.wait_ge(in_l, 16)
                            if p or not first(i):
                                pe.wait_ge(yt_done[s], i * 2 + p)
                        elif n == 1:
                            pe.wait_ge(z_done[s], at * NS + 1)
                        else:
                            pe.wait_ge(t_done[s], at * (NS - 1) + n - 1)
                            if (n - 1, s) in DVE_COPIES:
                                per = [q for q, s_ in sorted(DVE_COPIES) if s_ == s]
                                pe.wait_ge(tn_done[s], at * len(per) + per.index(n - 1) + 1)
                        for u, (h, c) in enumerate(U):
                            last = nc.tensor.matmul(PB[s][:, cols(u)], Ah[b][:, h, c, :],
                                                    Tn[s][:, u, :] if n else lev[:, LEVELS, :], start=True, stop=True)
                        last.then_inc(at_mm[s], 1)
                    elif st[0] == "TZ":
                        n = st[1]
                        pe.wait_ge(z_done[s], at * NS + n + 1)
                        if n == 1:
                            pe.wait_ge(tt0_done[s], at + 1)
                        for u in range(4):
                            if n < LEVELS - 1:
                                nc.tensor.matmul(PB[s][:, cols(u)], Tt[s][:, u, :], Zn[s][:, u, :], start=True, stop=True)
                            last = nc.tensor.matmul(PC[s][:, cols(u)], Zn[s][:, u, :], Tt[s][:, u, :],
                                                    start=True, stop=True)
                        last.then_inc(tt_mm[s], 1)
                    elif st[0] == "W0":
                        c = st[1]
                        if c == 0:
                            pe.wait_ge(t_done[s], at * (NS - 1) + NS - 1)
                            pe.wait_ge(r_done[s], at + 1)
                        else:
                            pe.wait_ge(r2_done[s], at + 1)
                        for h in range(2):
                            last = nc.tensor.matmul(PB[s][:, cols(h)], Tt[s][:, 2 * h + c, :], Rh[b][:, h, c, :],
                                                    start=True, stop=True)
                        last.then_inc(w0_mm[s], 1)
                    elif st[0] == "AW":
                        c = st[1]
                        pe.wait_ge(w0_done[s], at * 2 + c + 1)
                        for h in range(2):
                            a = AP1[b][:, h, 0, :] if c else AP0[b][:, h, 0, 0:P]
                            last = nc.tensor.matmul(PC[s][:, cols(h)], a, W[s][:, h, c, :], start=True, stop=True)
                        last.then_inc(aw_mm[s], 1)
                    elif st[0] == "CO":
                        c = st[1]
                        pe.wait_ge(rr_done[s], at * 2 + c + 1)
                        for h in range(2):
                            last = nc.tensor.matmul(PB[s][:, cols(2 + h)], Tt[s][:, 2 * h + c, :], rr[s][:, h, c, :],
                                                    start=True, stop=True)
                        last.then_inc(cor_mm[s], 1)
                    elif st[0] == "X":
                        pe.wait_ge(w_done[s], at * 2 + 1)
                        for h in range(2):
                            last = nc.tensor.matmul(PC[s][:, cols(2 + h)], AP0[b][:, h, 0, P:S], W[s][:, h, 0, :],
                                                    start=True, stop=True)
                        last.then_inc(x_mm[s], 1)
                    elif st == "O":
                        pe.wait_ge(w_done[s], at * 2 + 2)
                        for h in range(2):
                            nc.tensor.matmul(PC[s][:, cols(2 * h)], AP0[b][:, h, 1, 0:P], W[s][:, h, 0, :],
                                             start=True, stop=True)
                            nc.tensor.matmul(PC[s][:, cols(2 * h + 1)], AP0[b][:, h, 1, P:S], W[s][:, h, 0, :],
                                             start=True, stop=False)
                            last = nc.tensor.matmul(PC[s][:, cols(2 * h + 1)], AP1[b][:, h, 1, :], W[s][:, h, 1, :],
                                                    start=False, stop=True)
                        last.then_inc(o_mm[s], 1)
                    elif st == "YT":
                        pe.wait_ge(y_done[s], at + 1)
                        for u, (h, c) in enumerate(U):
                            last = nc.tensor.transpose(PB[s][:, cols(u)], y[s][:, h, c, :], ident)
                        last.then_inc(yt_mm[s], 1)

                walk_first("pe", stage)

                walk(0, "first", "pe", step, stage)
                with pe.Fori(1, HK - 1) as i:
                    walk(i, "loop", "pe", step, stage)
                walk(HK - 1, "last", "pe", step, stage)

        attention.close()
        experts(nc, stack, dict(locals()))


def experts(nc, stack, v):
    f32, f32r, i32 = mybir.dt.float32, mybir.dt.float32r, mybir.dt.int32
    ALU, ACT, AX = mybir.AluOpType, mybir.ActivationFunctionType, mybir.AxisListType
    ds = bass.ds
    sb, sem, two, apart = v["sb"], v["sem"], v["two"], v["apart"]
    acc, xT, cst, ident = v["acc"], v["xT"], v["cst"], v["ident"]
    eps_l = v["eps_l"]
    PT = v["PJ"][2:] + v["PJ"][:2]
    PG, PU, PY, PX = v["PJ"][2:], v["PB"], v["PJ"][:2], v["PC"]
    ids, ctx_in, Wr, Wg, Wu, Wd, out = (v[n] for n in ("ids", "ctx_in", "Wr", "Wg", "Wu", "Wd", "out"))

    id_i, id_f = sb("id_i", [P, NT], i32), sb("id_f", [P, NT])
    who = sb("who", [P, NT])
    me = sb("me", [P, E1, NT])
    wr = sb("wr", [P, KT, E2])
    wx = [sb(f"wx{q}", [P, KT, F]) for q in range(2)]
    wt = [sb(f"wt{q}", [P, KT, F]) for q in range(2)]
    wg = [sb(f"wg{q}", [P, KT, F]) for q in range(2)]
    wu = [sb(f"wu{q}", [P, KT, F]) for q in range(2)]
    wd = [sb(f"wd{q}", [P, KT, F]) for q in range(2)]
    xh, xl = (sb(n, [P, KT, T], f32r) for n in ("xh", "xl"))
    th, tl, gh, gl, uh, ul = ([sb(f"{n}{q}", [P, KT, F], f32r) for q in range(2)]
                              for n in ("th", "tl", "gh", "gl", "uh", "ul"))
    sg = [sb(f"sg{r}", [P, HALF]) for r in range(2)]
    hh = [sb(f"hh{r}", [P, KT, HALF]) for r in range(2)]
    st6, mv = sb("st6", [P, NT, 6]), sb("mv", [P, NT, 2])
    sd, ri = sb("sd", [P, NT]), sb("ri", [P, NT])
    pr, q1, q2, q3 = (sb(n, [P, NT, E2]) for n in ("pr", "q1", "q2", "q3"))
    m1, m2, m3 = (sb(n, [P, NT]) for n in ("m1", "m2", "m3"))
    credit = sb("credit", [P, 4])
    wk = sb("wk", [P, E2, NT])

    id_in, wr_in, x_in, gu_in = sem("id_in"), sem("wr_in"), two("x_in"), two("gu_in")
    wd_in = two("wd_in")
    id_chain = sem("id_chain")
    ln_chain, var_done, sd_done, ln_ready = sem("ln_chain"), sem("var_done"), sem("sd_done"), sem("ln_ready")
    xr_mm, xr_done, xh_done = two("xr_mm"), two("xr_done"), two("xh_done")
    ct_mm, ct_high, ct_done, ct_low = sem("ct_mm"), sem("ct_high"), sem("ct_done"), sem("ct_low")
    w_high, w_low = two("w_high"), two("w_low")
    gu_mm, sg_done, h_done, y_mm, y_acc = two("gu_mm"), two("sg_done"), two("h_done"), two("y_mm"), two("y_acc")
    gu2, sg2, h2, y2m, ya2 = two("gu2_mm"), two("sg2_done"), two("h2_done"), two("y2_mm"), two("y2_acc")
    r_mm, re_done, rt_chain = sem("r_mm"), sem("re_done"), sem("rt_chain")
    stored = sem("stored")
    X1 = (gu_mm, sg_done, h_done, y_mm, y_acc)
    X2 = (gu2, sg2, h2, y2m, ya2)

    def steps(e, q, run, last=False, between=None):
        for kind, k in (("g", 1), ("g", 2), ("y", 0), ("g", 3)):
            run(kind, k, e, q)
        if between:
            between()
        if not last:
            run("g", 0, e + 1, 1 - q)
        run("y", 1, e, q)

    def third(run, split=None, ready=None, at_end=None):
        if ready:
            ready(0, 0)
        run("g", 0, 0, 0)

        def pair(j, last=False):
            for q in range(2):
                end = last and q == 1
                if split and not end:
                    split(j + q, 1 - q)
                between = at_end if end else ready and (lambda: ready(j + q, 1 - q))
                steps(j * 2 + q, q, run, end, between)
        return pair

    with nc.Block() as block:
        @block.sync
        def _(sp):
            sp.dma_start(id_i[:, :], ids.rearrange("b (c p) -> p (b c)", p=P), allow_slow_non_contiguous=True).then_inc(id_in, 16)
            sp.dma_start(wr[:, :, :], Wr.rearrange("(k p) n -> p k n", p=P)).then_inc(wr_in, 16)

            def load_x(e, q):
                sp.dma_start(wx[q][:, :, :], ctx_in[ds(e, 1), :, :].rearrange("o (k p) n -> p (o k) n", p=P)).then_inc(x_in[q], 16)

            def load(parts, into, e, q):
                for to, of in parts:
                    sp.dma_start(to[q][:, :, :], of[ds(e, 1), :, :].rearrange("o (k p) n -> p (o k) n", p=P)).then_inc(
                        into[q], 16)

            gate_up, down = ((wg, Wg), (wu, Wu)), ((wd, Wd),)
            for q in range(2):
                load_x(q, q)
            for q in range(2):
                load(gate_up, gu_in, q, q)
                load(down, wd_in, q, q)
            for e in range(2, E1):
                sp.wait_ge(ct_mm, e - 1)
                load_x(e, e % 2)
            with sp.Fori(0, E2 // 2 - 1) as j:
                for q in range(2):
                    sp.wait_ge(w_low[q], j + 1)
                    apart(sp)
                    load(gate_up, gu_in, j * 2 + (2 + q), q)
                    sp.wait_ge(y2m[1], j * 4 + (q + 1) * 2)
                    apart(sp)
                    load(down, wd_in, j * 2 + (2 + q), q)
            of = out.rearrange("b s d -> (b s) d").rearrange("(n p) d -> p n d", p=P)
            for hf in range(2):
                sp.wait_ge(ln_ready, 2 * NT + 4 * hf + 4)
                sp.dma_start(of[:, 4 * hf:4 * hf + 4, :], acc[:, 4 * hf:4 * hf + 4, :]).then_inc(stored, 16)
            sp.wait_ge(stored, 32)

        @block.scalar
        def _(act):
            def root(n, hf):
                act.wait_ge(var_done, n * 2 + hf + 1)
                of = slice(4 * hf, 4 * hf + 4)
                nc.scalar.activation(sd[:, of], mv[:, of, 1], ACT.Sqrt, bias=eps_l[:, :]).then_inc(sd_done, 1)

            def transposed(n):
                for q in range(KT * 2):
                    hf, k = q // 2, q % 2
                    act.wait_ge(xr_mm[k], n * 2 + hf + 1)
                    nc.scalar.copy(xh[:, k, hf * HALF:(hf + 1) * HALF], PT[q][:, :]).then_inc(xh_done[k], 1)

            def gate(sems):
                gu, sgd, hd, ym, ya = sems

                def run(kind, k, e, q):
                    if kind == "g":
                        act.wait_ge(gu[k % 2], e * 2 + k // 2 + 1)
                        nc.scalar.activation(sg[k % 2][:, :], PG[k % 2][:, :], ACT.Silu).then_inc(sgd[k % 2], 1)
                return run

            def matrix(e):
                act.wait_ge(ct_mm, e + 1)
                nc.scalar.copy(wt[e % 2][:, :, :].rearrange("p k n -> p (k n)"), PX[e % 2][:, :]).then_inc(ct_done, 1)
                act.wait_ge(ct_done, e + 1)
                nc.scalar.copy(th[e % 2][:, :, :], wt[e % 2][:, :, :]).then_inc(ct_high, 1)

            def split(j, q):
                act.wait_ge(gu_in[q], j * 32 + 32)
                nc.scalar.copy(gh[q][:, :, :], wg[q][:, :, :])
                nc.scalar.copy(uh[q][:, :, :], wu[q][:, :, :]).then_inc(w_high[q], 1)

            for hf in range(2):
                root(0, hf)
            matrix(0)
            transposed(0)
            gate(X1)("g", 0, 0, 0)
            for e in range(E1):
                if e < E1 - 1:
                    matrix(e + 1)
                steps(e, e % 2, gate(X1), e == E1 - 1, (lambda: root(1, 0)) if e == E1 - 1 else None)
            root(1, 1)
            transposed(1)
            split(0, 0)
            act.wait_ge(rt_chain, 2)
            nc.scalar.activation(pr[:, :, :], pr[:, :, :], ACT.Exp).then_inc(re_done, 1)
            pair = third(gate(X2), split=split, at_end=lambda: root(2, 0))
            with act.Fori(0, E2 // 2 - 1) as j:
                pair(j)
            pair(E2 // 2 - 1, last=True)
            root(2, 1)

        @block.gpsimd
        def _(pool):
            def split(j, q):
                pool.wait_ge(w_high[q], j + 1)
                nc.gpsimd.tensor_tensor(gl[q][:, :, :], wg[q][:, :, :], gh[q][:, :, :], ALU.subtract)
                nc.gpsimd.tensor_tensor(ul[q][:, :, :], wu[q][:, :, :], uh[q][:, :, :], ALU.subtract).then_inc(w_low[q], 1)

            for e in range(E1):
                pool.wait_ge(ct_high, e + 1)
                nc.gpsimd.tensor_tensor(tl[e % 2][:, :, :], wt[e % 2][:, :, :], th[e % 2][:, :, :],
                                        ALU.subtract).then_inc(ct_low, 1)
            split(0, 0)
            pair = third(lambda *step: None, split=split)
            with pool.Fori(0, E2 // 2 - 1) as j:
                pair(j)
            pair(E2 // 2 - 1, last=True)

        @block.vector
        def _(dve):
            cc = [0]

            def link(ins, s=ln_chain, c=cc):
                c[0] += 1
                ins.then_inc(s, 1)
                dve.wait_ge(s, c[0])

            def statistics(n, hf):
                if n:
                    for r in range(2):
                        dve.wait_ge((y_acc, ya2)[n - 1][r], 2 * (E1, E2)[n - 1] + hf)
                tiles = range(4 * hf, 4 * hf + 4)
                for t in tiles:
                    last = nc.vector.bn_stats(st6[:, t, :], acc[:, t, :])
                link(last)
                for t in tiles:
                    last = nc.vector.bn_aggr(mv[:, t, :], st6[:, t, :])
                last.then_inc(var_done, 1)

            def normalise(n, hf):
                dve.wait_ge(sd_done, n * 2 + hf + 1)
                of = slice(4 * hf, 4 * hf + 4)
                link(nc.vector.reciprocal(ri[:, of], sd[:, of]))
                for t in range(4 * hf, 4 * hf + 4):
                    nc.vector.tensor_scalar(acc[:, t, :], acc[:, t, :], mv[:, t, 0:1], ri[:, t:t + 1],
                                            ALU.subtract, ALU.mult).then_inc(ln_ready, 1)

            def norm_half(n, hf):
                statistics(n, hf)
                normalise(n, hf)

            def transposed(n):
                for q in range(KT * 2):
                    hf, k = q // 2, q % 2
                    of = slice(hf * HALF, (hf + 1) * HALF)
                    dve.wait_ge(xh_done[k], n * 2 + hf + 1)
                    low = nc.vector.tensor_tensor(xl[:, k, of], PT[q][:, :], xh[:, k, of], ALU.subtract)
                    if n:
                        low = nc.vector.tensor_copy(xT[:, k, of], PT[q][:, :])
                    low.then_inc(xr_done[k], 1)
                dve.wait_ge(ln_ready, (n + 1) * NT)

            def hidden(sems, weight, up):
                gu, sgd, hd, ym, ya = sems

                def run(kind, k, e, q):
                    if kind == "g":
                        dve.wait_ge(sgd[k % 2], e * 2 + k // 2 + 1)
                        nc.vector.tensor_tensor(hh[k // 2][:, k % 2, :], sg[k % 2][:, :], up[k % 2][:, :],
                                                ALU.mult).then_inc(hd[k % 2], 1)
                    else:
                        for r in range(2):
                            dve.wait_ge(ym[r], e * 2 + k + 1)
                            for n_ in range(2):
                                t = k * 4 + r * 2 + n_
                                last = nc.vector.scalar_tensor_tensor(
                                    acc[:, t, :], PY[r][:, n_ * D:(n_ + 1) * D], weight(e, q, t), acc[:, t, :],
                                    ALU.mult, ALU.add)
                            last.then_inc(ya[r], 1)
                return run

            for n, sems in enumerate((X1, X2)):
                for r in range(2):
                    nc.vector.memset(credit[:, 2 * n + r:2 * n + r + 1], 0.0).then_inc(sems[4][r], 1)

            for of_half in (statistics, normalise):
                for hf in range(2):
                    of_half(0, hf)
            transposed(0)

            dve.wait_ge(id_in, 16)
            ic = [0]
            ln_i = lambda ins: link(ins, id_chain, ic)
            ln_i(nc.vector.tensor_copy(id_f[:, :], id_i[:, :]))
            ln_i(nc.vector.tensor_scalar(who[:, :], id_f[:, :], float(12500 // E1), None, ALU.is_ge))
            for m in range(2, E1):
                ln_i(nc.vector.scalar_tensor_tensor(who[:, :], id_f[:, :], float(m * (12500 // E1)), who[:, :],
                                                    ALU.is_ge, ALU.add))
            for e in range(E1):
                ln_i(nc.vector.tensor_scalar(me[:, e, :], who[:, :], float(e), None, ALU.is_equal))

            run = hidden(X1, lambda e_, q, t: me[:, e_, t:t + 1], PG)
            run("g", 0, 0, 0)
            for e in range(E1):
                steps(e, e % 2, run, e == E1 - 1, (lambda: norm_half(1, 0)) if e == E1 - 1 else None)
            norm_half(1, 1)
            transposed(1)
            rc = [0]
            ln_r = lambda ins: link(ins, rt_chain, rc)
            dve.wait_ge(r_mm, 1)
            bc = lambda a: a.rearrange("p (n o) -> p n o", o=1).to_broadcast((P, NT, E2))
            lgp = PX[0][:, 0:NT * E2].rearrange("p (n e) -> p n e", e=E2)
            ln_r(nc.vector.tensor_reduce(m1[:, :], lgp, AX.X, ALU.max))
            ln_r(nc.vector.tensor_tensor(pr[:, :, :], lgp, bc(m1[:, :]), ALU.subtract))
            dve.wait_ge(re_done, 1)
            iota = cst[:, C_E8:C_END].rearrange("p (n e) -> p n e", e=E2)
            ln_r(nc.vector.tensor_copy(q1[:, :, :], pr[:, :, :]))
            for best in range(2):
                ln_r(nc.vector.tensor_reduce(m1[:, :], q1[:, :, :], AX.X, ALU.max))
                ln_r(nc.vector.tensor_tensor(q2[:, :, :], q1[:, :, :], bc(m1[:, :]), ALU.is_lt))
                ln_r(nc.vector.scalar_tensor_tensor(q2[:, :, :], q2[:, :, :], 100.0, iota, ALU.mult, ALU.add))
                ln_r(nc.vector.tensor_reduce(m2[:, :], q2[:, :, :], AX.X, ALU.min))
                ln_r(nc.vector.tensor_tensor(q2[:, :, :], iota, bc(m2[:, :]), ALU.is_equal))
                if best == 0:
                    ln_r(nc.vector.tensor_tensor(q3[:, :, :], q2[:, :, :], pr[:, :, :], ALU.mult))
                    ln_r(nc.vector.scalar_tensor_tensor(q1[:, :, :], q2[:, :, :], -4.0, q1[:, :, :],
                                                        ALU.mult, ALU.add))
                else:
                    ln_r(nc.vector.tensor_tensor(q2[:, :, :], q2[:, :, :], pr[:, :, :], ALU.mult))
                    ln_r(nc.vector.tensor_tensor(q3[:, :, :], q3[:, :, :], q2[:, :, :], ALU.add))
            ln_r(nc.vector.tensor_reduce(m2[:, :], q3[:, :, :], AX.X, ALU.add))
            ln_r(nc.vector.reciprocal(m3[:, :], m2[:, :]))
            ln_r(nc.vector.tensor_tensor(wk[:, :, :].rearrange("p e n -> p n e"), q3[:, :, :], bc(m3[:, :]), ALU.mult))
            pair = third(hidden(X2, lambda e_, q_, t: wk[:, ds(e_, 1), t], PU), at_end=lambda: norm_half(2, 0))
            with dve.Fori(0, E2 // 2 - 1) as j:
                pair(j)
            pair(E2 // 2 - 1, last=True)
            norm_half(2, 1)

        @block.tensor
        def _(pe):
            def transposed(n):
                for q in range(KT * 2):
                    hf, k = q // 2, q % 2
                    pe.wait_ge(ln_ready, n * NT + hf * 4 + 4)
                    for t in range(4):
                        last = nc.tensor.transpose(PT[q][:, t * P:(t + 1) * P],
                                                   acc[:, hf * 4 + t, k * P:(k + 1) * P], ident)
                    last.then_inc(xr_mm[k], 1)

            def taken(n, hf):
                for k in range(KT):
                    pe.wait_ge(xr_done[k], n * 2 + hf + 1)

            def products(sems, splits, down_w):
                gu, sgd, hd, ym, ya = sems

                def run(kind, k, e, q):
                    if kind == "g":
                        hf, ft = k // 2, k % 2
                        if k >= 2:
                            pe.wait_ge(hd[k % 2], e * 2 + 1)
                        elif k == 0 and not (isinstance(e, int) and e == 0):
                            pe.wait_ge(hd[0], e * 2)
                        of = slice(hf * HALF, (hf + 1) * HALF)
                        for to, (high, low) in zip((PG, PU), splits):
                            terms = [(w, xx, kt) for w, xx in ((high, xh), (low, xh), (high, xl)) for kt in range(KT)]
                            for n_, (w, xx, kt) in enumerate(terms):
                                last = nc.tensor.matmul(to[k % 2][:, :], w[q][:, kt, ft * P:(ft + 1) * P], xx[:, kt, of],
                                                        start=(n_ == 0), stop=(n_ == len(terms) - 1))
                        last.then_inc(gu[k % 2], 1)
                    else:
                        if sems is X2 and k == 0:
                            pe.wait_ge(wd_in[q], (e - q) * 8 + 16)
                        for r in range(2):
                            pe.wait_ge(hd[r], e * 2 + k + 1)
                        for r in range(2):
                            pe.wait_ge(ya[r], e * 2 + k + 1)
                            for n_ in range(2):
                                for ft in range(KT):
                                    t = r * 2 + n_
                                    last = nc.tensor.matmul(PY[r][:, n_ * D:(n_ + 1) * D],
                                                            hh[k][:, ft, t * P:(t + 1) * P], down_w[q][:, ft, :],
                                                            start=(ft == 0), stop=(ft == KT - 1))
                            last.then_inc(ym[r], 1)
                return run

            def matrix(e):
                pe.wait_ge(x_in[e % 2], 16 * (e // 2 + 1))
                if e >= 2:
                    pe.wait_ge(ct_done, e - 1)
                    pe.wait_ge(ct_low, e - 1)
                for a in range(KT):
                    for k in range(KT):
                        last = nc.tensor.transpose(PX[e % 2][:, k * F + a * P:k * F + (a + 1) * P],
                                                   wx[e % 2][:, a, k * P:(k + 1) * P], ident)
                last.then_inc(ct_mm, 1)

            matrix(0)
            transposed(0)
            taken(0, 1)
            pe.wait_ge(ct_low, 1)
            run = products(X1, ((th, tl),), wt)
            run("g", 0, 0, 0)
            for e in range(E1):
                if e < E1 - 1:
                    matrix(e + 1)
                pe.wait_ge(ct_done, e + 1)
                steps(e, e % 2, run, e == E1 - 1, (lambda: pe.wait_ge(ct_low, e + 2)) if e < E1 - 1 else None)
            transposed(1)
            pe.wait_ge(wr_in, 16)
            for t in range(NT):
                if t % 4 == 0:
                    taken(1, t // 4)
                for k in range(KT):
                    last = nc.tensor.matmul(PX[0][:, t * E2:(t + 1) * E2], xT[:, k, t * P:(t + 1) * P], wr[:, k, :],
                                            start=(k == 0), stop=(k == KT - 1))
            last.then_inc(r_mm, 1)
            pair = third(products(X2, ((gh, gl), (uh, ul)), wd), ready=lambda j, q: pe.wait_ge(w_low[q], j + 1))
            with pe.Fori(0, E2 // 2 - 1) as j:
                pair(j)
            pair(E2 // 2 - 1, last=True)


def kernel(**inputs):
    import concourse.bacc as bacc
    from concourse.bass_utils import run_bass_kernel_spmd

    nc = bacc.Bacc("TRN2", target_bir_lowering=False, num_devices=1)
    consts, levels = constants()
    names = ["x", "itok_BxS_13_99985", "ctx_2048", "L0_attn_cu_seqlens", "L0_attn_Wqkv", "L0_attn_Wz", "L0_attn_Wa",
             "L0_attn_Wb", "L0_attn_conv_w", "L0_attn_A_log", "L0_attn_dt_bias", "L0_attn_norm_w", "L0_attn_Wout",
             "L0_ffn_Wr", "L0_ffn_Wg", "L0_ffn_Wu", "L0_ffn_Wd"]
    arrays, args = {}, []
    for name in names:
        a = np.ascontiguousarray(inputs[name])
        arrays["in_" + name] = a
        args.append(nc.dram_tensor("in_" + name, a.shape, mybir.dt.from_np(a.dtype), kind="ExternalInput").ap())
    for name, a in (("consts", consts), ("levels", levels)):
        arrays[name] = a
        args.append(nc.dram_tensor(name, a.shape, mybir.dt.from_np(a.dtype), kind="ExternalInput").ap())
    args.append(nc.dram_tensor("g_rows", (HV, T), mybir.dt.float32, kind="Internal").ap())
    args.append(nc.dram_tensor("result", (B, S, D), mybir.dt.float32, kind="ExternalOutput").ap())
    build(nc, *args)
    got = run_bass_kernel_spmd(nc, [arrays], core_ids=[0])
    return got.results[0]["result"]
```
